# Optimizing a Trainium2 kernel written in Bass

```python
import numpy as np
import jax
import jax.numpy as jnp

def _softmax(x, axis=-1):
    return jax.nn.softmax(x, axis=axis)

def _gelu(x):
    return jax.nn.gelu(x, approximate=True)

def _silu(x):
    return jax.nn.silu(x)

def _sigmoid(x):
    return jax.nn.sigmoid(x)

def _layernorm(x, axis=-1, eps=1e-05):
    m = jnp.mean(x, axis=axis, keepdims=True)
    v = jnp.var(x, axis=axis, keepdims=True)
    return (x - m) / jnp.sqrt(v + eps)

def _scatter_add(tgt, idx, src, axis=0):
    return tgt.at[idx].add(src)

def _segment_sum(src, seg, n):
    return jax.ops.segment_sum(src, seg, n)
kernel_name = 'mk_xattn_seq_d2_seqx_r8_76b195'

def setup_inputs(seed: int=0):
    np.random.seed(seed)
    _w = jnp.asarray

    def _rec_inputs():
        import jax
        import jax.numpy as jnp
        _rk = jax.random.key(seed)
        x = -0.0005146 + 1 * jax.random.normal(jax.random.fold_in(_rk, 1), (4, 256, 256), jnp.float32)
        _lenS = 256 - jax.random.randint(jax.random.fold_in(_rk, 7), (4,), 0, max(1, 256 // 4) + 1, jnp.int32)
        _lenS2 = 512 - jax.random.randint(jax.random.fold_in(_rk, 8), (4,), 0, max(1, 512 // 4) + 1, jnp.int32)
        _ctx_2048P = jax.random.normal(jax.random.fold_in(_rk, 11), (4, 16, 256), jnp.float32)
        _ctx_2048c = jax.random.dirichlet(jax.random.fold_in(_rk, 511), 0.3 * jnp.ones((16,), jnp.float32), (4, 512))
        _ctx_2048t = jnp.einsum('bsk,bkd->bsd', _ctx_2048c, _ctx_2048P)
        _ctx_2048t = _ctx_2048t * jax.lax.rsqrt(jnp.mean(jnp.square(_ctx_2048t)) + 1e-12) * 0.953939
        ctx_2048 = -0.000392918 + 0.999932 * (_ctx_2048t + 0.3 * jax.random.normal(jax.random.fold_in(_rk, 611), (4, 512, 256), jnp.float32))
        _validS = jnp.arange(256)[None, :] < _lenS[:, None]
        _validS2 = jnp.arange(512)[None, :] < _lenS2[:, None]
        _causal = jnp.tril(jnp.ones((256, 256), dtype=bool))
        mask_BxS2_ik0 = jnp.where(jnp.broadcast_to(_validS2[:, :], (4, 512)), 0, 1).astype(jnp.int32)
        return (x, ctx_2048, mask_BxS2_ik0)
    x, ctx_2048, mask_BxS2_ik0 = _rec_inputs()

    def _L0_xattn_setup():
        import jax, jax.numpy as jnp
        import numpy as np
        B, P, K, H, NH = (4, 256, 32, 256, 16)
        DH = H // NH
        EPS = 1e-06

        def rmsnorm(x, w):
            var = jnp.mean(jnp.square(x), axis=-1, keepdims=True)
            return x * jax.lax.rsqrt(var + EPS) * w
        key = jax.random.key(seed)
        ks = jax.random.split(key, 12)
        s = 0.02
        return {'x': jax.random.normal(ks[0], (B, P, H), jnp.float32), 'latents': jax.random.normal(ks[1], (B, K, H), jnp.float32), 'attention_mask': jax.random.randint(ks[2], (B, P), 0, 2, jnp.int32), 'q_w': s * jax.random.normal(ks[3], (H, H), jnp.float32), 'q_b': jnp.zeros((H,), jnp.float32), 'kv_w': s * jax.random.normal(ks[4], (H, 2 * H), jnp.float32), 'kv_b': jnp.zeros((2 * H,), jnp.float32), 'out_w': s * jax.random.normal(ks[5], (H, H), jnp.float32), 'out_b': jnp.zeros((H,), jnp.float32), 'postnorm_w': jnp.ones((H,), jnp.float32), 'mlp_w1': s * jax.random.normal(ks[6], (H, 4 * H), jnp.float32), 'mlp_b1': jnp.zeros((4 * H,), jnp.float32), 'mlp_w2': s * jax.random.normal(ks[7], (4 * H, H), jnp.float32), 'mlp_b2': jnp.zeros((H,), jnp.float32)}
    _L0_xattn_all = _L0_xattn_setup()
    _L0_xattn_in = {k: v for k, v in _L0_xattn_all.items() if k in ('q_w', 'q_b', 'kv_w', 'kv_b', 'out_w', 'out_b', 'postnorm_w', 'mlp_w1', 'mlp_b1', 'mlp_w2', 'mlp_b2')}
    del _L0_xattn_all

    def _L1_xattn_setup():
        import jax, jax.numpy as jnp
        import numpy as np
        E, H, L, B = (256, 32, 128, 4)
        S = E // H
        DM, DD = (32, 64)

        def _ln(x, w, b, eps=1e-05):
            m = x.mean(-1, keepdims=True)
            v = ((x - m) ** 2).mean(-1, keepdims=True)
            return (x - m) / jnp.sqrt(v + eps) * w + b

        def _block(x, state, ln1_w, ln1_b, ln2_w, ln2_b, maa_x, maa_w1, maa_w2, maa_stack, time_decay, td_w1, td_w2, u, Wr, Wk, Wv, Wg, Wo, gn_w, gn_b, ffn_maa_k, ffn_maa_r, Wfk, Wfr, Wfv):
            b, l, e = x.shape
            h = u.shape[0]
            s_ = e // h
            xa = _ln(x, ln1_w, ln1_b)
            sx = jnp.concatenate([state[:, 1:2] - xa[:, :1], xa[:, :-1] - xa[:, 1:]], axis=1)
            xxx = jnp.tanh((xa + sx * maa_x) @ maa_w1).reshape(b, l, 5, DM)
            xxx = jnp.einsum('blfd,fde->blfe', xxx, maa_w2)
            xm = xa[:, :, None] + sx[:, :, None] * (maa_stack + xxx)
            xk, xw, xv, xr, xg = (xm[:, :, j] for j in range(5))
            w = jnp.exp(-jnp.exp(time_decay + jnp.tanh(xw @ td_w1) @ td_w2)).reshape(b, l, h, s_)
            r = (xr @ Wr.T).reshape(b, l, h, s_)
            k = (xk @ Wk.T).reshape(b, l, h, s_)
            v = (xv @ Wv.T).reshape(b, l, h, s_)
            g = jax.nn.silu(xg @ Wg.T)
            s0 = state[:, 2:2 + s_].reshape(b, h, s_, s_)

            def step(s, rkvw):
                r_t, k_t, v_t, w_t = rkvw
                a = k_t[..., :, None] * v_t[..., None, :]
                out = jnp.einsum('bhi,bhij->bhj', r_t, u * a + s)
                s = a + w_t[..., :, None] * s
                return (s, out)
            rkvw = tuple((jnp.moveaxis(t, 1, 0) for t in (r, k, v, w)))
            _, out = jax.lax.scan(step, s0, rkvw)
            out = jnp.moveaxis(out, 0, 1).reshape(b, l, e)
            og = out.reshape(b, l, h, s_)
            m = og.mean(-1, keepdims=True)
            va = ((og - m) ** 2).mean(-1, keepdims=True)
            og = ((og - m) / jnp.sqrt(va + 1e-05)).reshape(b, l, e) * gn_w + gn_b
            x1 = x + og * g @ Wo.T
            xc = _ln(x1, ln2_w, ln2_b)
            sx2 = jnp.concatenate([state[:, 0:1] - xc[:, :1], xc[:, :-1] - xc[:, 1:]], axis=1)
            xk2 = xc + sx2 * ffn_maa_k
            xr2 = xc + sx2 * ffn_maa_r
            rr = jax.nn.sigmoid(xr2 @ Wfr.T)
            kk = jnp.square(jax.nn.relu(xk2 @ Wfk.T))
            return x1 + rr * (kk @ Wfv.T)
        key = jax.random.key(seed)
        ks = jax.random.split(key, 24)
        sc = 0.02
        d = {'x': jax.random.normal(ks[0], (B, L, E), jnp.float32), 'state': jax.random.normal(ks[1], (B, 2 + S, E), jnp.float32) * 0.1, 'ln1_w': jnp.ones((E,), jnp.float32), 'ln1_b': jnp.zeros((E,), jnp.float32), 'ln2_w': jnp.ones((E,), jnp.float32), 'ln2_b': jnp.zeros((E,), jnp.float32), 'maa_x': jax.random.normal(ks[2], (E,), jnp.float32) * 0.1, 'maa_w1': jax.random.normal(ks[3], (E, 5 * DM), jnp.float32) * sc, 'maa_w2': jax.random.normal(ks[4], (5, DM, E), jnp.float32) * sc, 'maa_stack': jax.random.normal(ks[5], (1, 5, E), jnp.float32) * 0.1, 'time_decay': jax.random.normal(ks[6], (E,), jnp.float32) * 0.5, 'td_w1': jax.random.normal(ks[7], (E, DD), jnp.float32) * sc, 'td_w2': jax.random.normal(ks[8], (DD, E), jnp.float32) * sc, 'u': jax.random.normal(ks[9], (H, S, 1), jnp.float32) * 0.1, 'Wr': jax.random.normal(ks[10], (E, E), jnp.float32) * sc, 'Wk': jax.random.normal(ks[11], (E, E), jnp.float32) * sc, 'Wv': jax.random.normal(ks[12], (E, E), jnp.float32) * sc, 'Wg': jax.random.normal(ks[13], (E, E), jnp.float32) * sc, 'Wo': jax.random.normal(ks[14], (E, E), jnp.float32) * sc, 'gn_w': jnp.ones((E,), jnp.float32), 'gn_b': jnp.zeros((E,), jnp.float32), 'ffn_maa_k': jax.random.normal(ks[15], (E,), jnp.float32) * 0.1, 'ffn_maa_r': jax.random.normal(ks[16], (E,), jnp.float32) * 0.1, 'Wfk': jax.random.normal(ks[17], (E, E), jnp.float32) * sc, 'Wfr': jax.random.normal(ks[18], (E, E), jnp.float32) * sc, 'Wfv': jax.random.normal(ks[19], (E, E), jnp.float32) * sc}
        return d
    _L1_xattn_all = _L1_xattn_setup()
    _L1_xattn_in = {k: v for k, v in _L1_xattn_all.items() if k in ('ln1_w', 'ln1_b', 'ln2_w', 'ln2_b', 'maa_x', 'maa_w1', 'maa_w2', 'maa_stack', 'time_decay', 'td_w1', 'td_w2', 'u', 'Wr', 'Wk', 'Wv', 'Wg', 'Wo', 'gn_w', 'gn_b', 'ffn_maa_k', 'ffn_maa_r', 'Wfk', 'Wfr', 'Wfv')}
    del _L1_xattn_all
    return {'x': x, 'ctx_2048': ctx_2048, 'mask_BxS2_ik0': mask_BxS2_ik0, 'L0_xattn_q_w': _L0_xattn_in['q_w'], 'L0_xattn_q_b': _L0_xattn_in['q_b'], 'L0_xattn_kv_w': _L0_xattn_in['kv_w'], 'L0_xattn_kv_b': _L0_xattn_in['kv_b'], 'L0_xattn_out_w': _L0_xattn_in['out_w'], 'L0_xattn_out_b': _L0_xattn_in['out_b'], 'L0_xattn_postnorm_w': _L0_xattn_in['postnorm_w'], 'L0_xattn_mlp_w1': _L0_xattn_in['mlp_w1'], 'L0_xattn_mlp_b1': _L0_xattn_in['mlp_b1'], 'L0_xattn_mlp_w2': _L0_xattn_in['mlp_w2'], 'L0_xattn_mlp_b2': _L0_xattn_in['mlp_b2'], 'L1_xattn_ln1_w': _L1_xattn_in['ln1_w'], 'L1_xattn_ln1_b': _L1_xattn_in['ln1_b'], 'L1_xattn_ln2_w': _L1_xattn_in['ln2_w'], 'L1_xattn_ln2_b': _L1_xattn_in['ln2_b'], 'L1_xattn_maa_x': _L1_xattn_in['maa_x'], 'L1_xattn_maa_w1': _L1_xattn_in['maa_w1'], 'L1_xattn_maa_w2': _L1_xattn_in['maa_w2'], 'L1_xattn_maa_stack': _L1_xattn_in['maa_stack'], 'L1_xattn_time_decay': _L1_xattn_in['time_decay'], 'L1_xattn_td_w1': _L1_xattn_in['td_w1'], 'L1_xattn_td_w2': _L1_xattn_in['td_w2'], 'L1_xattn_u': _L1_xattn_in['u'], 'L1_xattn_Wr': _L1_xattn_in['Wr'], 'L1_xattn_Wk': _L1_xattn_in['Wk'], 'L1_xattn_Wv': _L1_xattn_in['Wv'], 'L1_xattn_Wg': _L1_xattn_in['Wg'], 'L1_xattn_Wo': _L1_xattn_in['Wo'], 'L1_xattn_gn_w': _L1_xattn_in['gn_w'], 'L1_xattn_gn_b': _L1_xattn_in['gn_b'], 'L1_xattn_ffn_maa_k': _L1_xattn_in['ffn_maa_k'], 'L1_xattn_ffn_maa_r': _L1_xattn_in['ffn_maa_r'], 'L1_xattn_Wfk': _L1_xattn_in['Wfk'], 'L1_xattn_Wfr': _L1_xattn_in['Wfr'], 'L1_xattn_Wfv': _L1_xattn_in['Wfv']}

def reference(x, ctx_2048, mask_BxS2_ik0, L0_xattn_q_w, L0_xattn_q_b, L0_xattn_kv_w, L0_xattn_kv_b, L0_xattn_out_w, L0_xattn_out_b, L0_xattn_postnorm_w, L0_xattn_mlp_w1, L0_xattn_mlp_b1, L0_xattn_mlp_w2, L0_xattn_mlp_b2, L1_xattn_ln1_w, L1_xattn_ln1_b, L1_xattn_ln2_w, L1_xattn_ln2_b, L1_xattn_maa_x, L1_xattn_maa_w1, L1_xattn_maa_w2, L1_xattn_maa_stack, L1_xattn_time_decay, L1_xattn_td_w1, L1_xattn_td_w2, L1_xattn_u, L1_xattn_Wr, L1_xattn_Wk, L1_xattn_Wv, L1_xattn_Wg, L1_xattn_Wo, L1_xattn_gn_w, L1_xattn_gn_b, L1_xattn_ffn_maa_k, L1_xattn_ffn_maa_r, L1_xattn_Wfk, L1_xattn_Wfr, L1_xattn_Wfv):
    import jax
    import jax.numpy as jnp

    def _L0_xattn_ref(x, latents, attention_mask, q_w, q_b, kv_w, kv_b, out_w, out_b, postnorm_w, mlp_w1, mlp_b1, mlp_w2, mlp_b2):
        import jax, jax.numpy as jnp
        import numpy as np
        B, P, K, H, NH = (4, 256, 32, 256, 16)
        DH = H // NH
        EPS = 1e-06

        def rmsnorm(x, w):
            var = jnp.mean(jnp.square(x), axis=-1, keepdims=True)
            return x * jax.lax.rsqrt(var + EPS) * w
        b, p, _ = x.shape
        k_len = latents.shape[1]
        residual = latents
        h = jnp.concatenate([x, latents], axis=1)
        q = (latents @ q_w + q_b).reshape(b, k_len, NH, DH)
        kv = (h @ kv_w + kv_b).reshape(b, p + k_len, NH, DH, 2)
        kmat, v = (kv[..., 0], kv[..., 1])
        attn = jnp.einsum('bkhd,bnhd->bhkn', q, kmat) / DH
        full_mask = jnp.concatenate([attention_mask.astype(bool), jnp.ones((b, k_len), bool)], axis=-1)
        attn = jnp.where(full_mask[:, None, None, :], attn, -jnp.inf)
        attn = jax.nn.softmax(attn.astype(jnp.float32), axis=-1).astype(q.dtype)
        attn_out = jnp.einsum('bhkn,bnhd->bkhd', attn, v).reshape(b, k_len, H)
        attn_out = attn_out @ out_w + out_b + residual
        out = rmsnorm(attn_out, postnorm_w)
        out = jax.nn.gelu(out @ mlp_w1 + mlp_b1) @ mlp_w2 + mlp_b2
        return out + residual

    def _L1_xattn_ref(x, state, ln1_w, ln1_b, ln2_w, ln2_b, maa_x, maa_w1, maa_w2, maa_stack, time_decay, td_w1, td_w2, u, Wr, Wk, Wv, Wg, Wo, gn_w, gn_b, ffn_maa_k, ffn_maa_r, Wfk, Wfr, Wfv):
        import jax, jax.numpy as jnp
        import numpy as np
        E, H, L, B = (256, 32, 128, 4)
        S = E // H
        DM, DD = (32, 64)

        def _ln(x, w, b, eps=1e-05):
            m = x.mean(-1, keepdims=True)
            v = ((x - m) ** 2).mean(-1, keepdims=True)
            return (x - m) / jnp.sqrt(v + eps) * w + b

        def _block(x, state, ln1_w, ln1_b, ln2_w, ln2_b, maa_x, maa_w1, maa_w2, maa_stack, time_decay, td_w1, td_w2, u, Wr, Wk, Wv, Wg, Wo, gn_w, gn_b, ffn_maa_k, ffn_maa_r, Wfk, Wfr, Wfv):
            b, l, e = x.shape
            h = u.shape[0]
            s_ = e // h
            xa = _ln(x, ln1_w, ln1_b)
            sx = jnp.concatenate([state[:, 1:2] - xa[:, :1], xa[:, :-1] - xa[:, 1:]], axis=1)
            xxx = jnp.tanh((xa + sx * maa_x) @ maa_w1).reshape(b, l, 5, DM)
            xxx = jnp.einsum('blfd,fde->blfe', xxx, maa_w2)
            xm = xa[:, :, None] + sx[:, :, None] * (maa_stack + xxx)
            xk, xw, xv, xr, xg = (xm[:, :, j] for j in range(5))
            w = jnp.exp(-jnp.exp(time_decay + jnp.tanh(xw @ td_w1) @ td_w2)).reshape(b, l, h, s_)
            r = (xr @ Wr.T).reshape(b, l, h, s_)
            k = (xk @ Wk.T).reshape(b, l, h, s_)
            v = (xv @ Wv.T).reshape(b, l, h, s_)
            g = jax.nn.silu(xg @ Wg.T)
            s0 = state[:, 2:2 + s_].reshape(b, h, s_, s_)

            def step(s, rkvw):
                r_t, k_t, v_t, w_t = rkvw
                a = k_t[..., :, None] * v_t[..., None, :]
                out = jnp.einsum('bhi,bhij->bhj', r_t, u * a + s)
                s = a + w_t[..., :, None] * s
                return (s, out)
            rkvw = tuple((jnp.moveaxis(t, 1, 0) for t in (r, k, v, w)))
            _, out = jax.lax.scan(step, s0, rkvw)
            out = jnp.moveaxis(out, 0, 1).reshape(b, l, e)
            og = out.reshape(b, l, h, s_)
            m = og.mean(-1, keepdims=True)
            va = ((og - m) ** 2).mean(-1, keepdims=True)
            og = ((og - m) / jnp.sqrt(va + 1e-05)).reshape(b, l, e) * gn_w + gn_b
            x1 = x + og * g @ Wo.T
            xc = _ln(x1, ln2_w, ln2_b)
            sx2 = jnp.concatenate([state[:, 0:1] - xc[:, :1], xc[:, :-1] - xc[:, 1:]], axis=1)
            xk2 = xc + sx2 * ffn_maa_k
            xr2 = xc + sx2 * ffn_maa_r
            rr = jax.nn.sigmoid(xr2 @ Wfr.T)
            kk = jnp.square(jax.nn.relu(xk2 @ Wfk.T))
            return x1 + rr * (kk @ Wfv.T)
        return _block(x, state, ln1_w, ln1_b, ln2_w, ln2_b, maa_x, maa_w1, maa_w2, maa_stack, time_decay, td_w1, td_w2, u, Wr, Wk, Wv, Wg, Wo, gn_w, gn_b, ffn_maa_k, ffn_maa_r, Wfk, Wfr, Wfv)
    x = _L0_xattn_ref(ctx_2048, x, mask_BxS2_ik0, L0_xattn_q_w, L0_xattn_q_b, L0_xattn_kv_w, L0_xattn_kv_b, L0_xattn_out_w, L0_xattn_out_b, L0_xattn_postnorm_w, L0_xattn_mlp_w1, L0_xattn_mlp_b1, L0_xattn_mlp_w2, L0_xattn_mlp_b2)
    x = _L1_xattn_ref(x, ctx_2048, L1_xattn_ln1_w, L1_xattn_ln1_b, L1_xattn_ln2_w, L1_xattn_ln2_b, L1_xattn_maa_x, L1_xattn_maa_w1, L1_xattn_maa_w2, L1_xattn_maa_stack, L1_xattn_time_decay, L1_xattn_td_w1, L1_xattn_td_w2, L1_xattn_u, L1_xattn_Wr, L1_xattn_Wk, L1_xattn_Wv, L1_xattn_Wg, L1_xattn_Wo, L1_xattn_gn_w, L1_xattn_gn_b, L1_xattn_ffn_maa_k, L1_xattn_ffn_maa_r, L1_xattn_Wfk, L1_xattn_Wfr, L1_xattn_Wfv)
    return x

_drawn_inputs = setup_inputs


def setup_inputs(seed=0):
    import zlib

    import numpy as np

    out = dict(_drawn_inputs(seed))
    spreads = {'L0_xattn_q_b': (0.0, 0.8),
     'L0_xattn_kv_b': (0.0, 0.8),
     'L0_xattn_out_b': (0.0, 0.65),
     'L0_xattn_postnorm_w': (1.0, 0.6),
     'L0_xattn_mlp_b1': (0.0, 0.1),
     'L0_xattn_mlp_b2': (0.0, 0.1),
     'L1_xattn_ln1_w': (1.0, 0.582),
     'L1_xattn_ln1_b': (0.0, 0.565),
     'L1_xattn_ln2_w': (1.0, 0.6),
     'L1_xattn_ln2_b': (0.0, 0.8),
     'L1_xattn_gn_w': (1.0, 0.6),
     'L1_xattn_gn_b': (0.0, 0.8)}
    factors = {'ctx_2048': 8.0,
     'L0_xattn_q_w': 8.0,
     'L0_xattn_kv_w': 8.0,
     'L0_xattn_out_w': 8.0,
     'L1_xattn_maa_x': 8.0,
     'L1_xattn_maa_w1': 7.802,
     'L1_xattn_maa_w2': 7.817,
     'L1_xattn_maa_stack': 2.832,
     'L1_xattn_time_decay': 2.886,
     'L1_xattn_td_w1': 8.0,
     'L1_xattn_td_w2': 8.0,
     'L1_xattn_u': 5.772,
     'L1_xattn_ffn_maa_k': 8.0,
     'L1_xattn_ffn_maa_r': 8.0,
     'L1_xattn_Wfk': 2.809,
     'L1_xattn_Wfr': 8.0}
    for name, (base, spread) in spreads.items():
        noise = np.random.default_rng([zlib.crc32(name.encode()), seed]).standard_normal(out[name].shape)
        drawn = base * np.exp(spread * noise) if base else spread * noise
        out[name] = jnp.asarray(drawn.astype(out[name].dtype))
    for name, factor in factors.items():
        out[name] = (out[name] * factor).astype(out[name].dtype)
    return out
```

```python
from contextlib import ExitStack

import numpy as np

import concourse.bass as bass
from concourse import mybir

P = 128
F32 = mybir.dt.float32
BF16 = mybir.dt.bfloat16
I32 = mybir.dt.int32
ALU = mybir.AluOpType
ACT = mybir.ActivationFunctionType
AX = mybir.AxisListType

B, TQ, TC, E = 4, 256, 512, 256
NK = TC + TQ
NH, DH = 16, 16
C = E // P
NT = NK // P
QT = TQ // P
FF = 4 * E
FC = FF // P
H, S = 32, E // 32
DM, DD = 32, 64
NF = 5
HH = NH // 2
KPART = (0, 0, 1, 1, 0, 2)
QPART = (0, 1, 0, 1, 2, 0)
NB = len(KPART)
R_MASK, R_HI, R_LO = NB * DH, NB * DH + 1, NB * DH + 2
MASKED = -1.0e30
LEAD = 10
VW = DH + 1

COLS = {}
_at = 0
for _n, _k in (("q_b", C), ("k_b", C), ("post_w", C), ("b1", FC), ("ln1_w", C), ("ln1_b", C), ("ln2_w", C),
               ("ln2_b", C), ("maa_x", C), ("stack", NF * C), ("decay", C), ("u", C), ("ffn_k", C), ("ffn_r", C),
               ("shift0", B * C * 2), ("state0", B * C * S)):
    COLS[_n] = (_at, _k)
    _at += _k
NCOLS = _at
ROWS = {n: i for i, n in enumerate(("out_b", "v_b", "b2", "gn_w", "gn_b"))}
SQUARE = ("Wr", "Wk", "Wv", "Wg", "Wo", "Wfk", "Wfr", "Wfv")
MIX = {"k": 0, "w": 1, "v": 2, "r": 3, "g": 4}

TAIL = (("oT", "A"), ("proj", "D"), ("zT", "A"), ("up0", "D"), ("up1", "D"), ("up2", "D"), ("up3", "D"),
        ("down", "D"), ("xaT", "A"), ("maa1", "A"), ("mix_v", "D"), ("mix_k", "D"), ("v", "A"), ("mix_w", "D"),
        ("k", "A"), ("td1", "A"), ("mix_r", "D"), ("td2", "A"), ("r", "A"), ("mix_g", "D"), ("vN", "A"),
        ("g", "D"), ("diag", "D"), ("wkv", "D"), ("ogT", "A"), ("wo", "D"), ("xcT", "A"), ("rr", "A"),
        ("kk", "A"), ("fv", "D"))
KQ = ("kq00", "kq01", "kq10", "kq11")
VP = ("vp0", "vp1", "vp2")
READS_LAST = dict(TAIL + tuple((n, "D") for n in KQ) + tuple((n, "A") for n in VP) + (("m", "A"),))
TAIL_NAMES = [n for n, _ in TAIL]


def schedule():
    for b in (0, 1):
        for n in KQ:
            yield ("unit", n, b)
        yield ("spill", b)
        for hf in ((0, 1) if b == 0 else (2,)):
            yield ("stack", hf)
        for n in VP:
            yield ("unit", n, b)
    for t in range(LEAD):
        for qt in range(QT):
            yield ("max", t, qt)
        if t % HH == HH - 1:
            yield ("unit", "m", t // HH)
    total = B * NH
    for t in range(total):
        b, h = divmod(t, NH)
        extra = []
        if b >= 1 and h >= 1:
            extra += [("unit", n, b - 1) for n in TAIL_NAMES[2 * (h - 1):2 * h]]
        if b == 0 and (1 <= h < 5 or 7 <= h < 11):
            b2, i = (2, h - 1) if h < 5 else (3, h - 7)
            extra.append(("unit", KQ[i], b2))
            if i == 3:
                extra.append(("spill", b2))
        if 1 <= b and b + 1 < B and 1 <= h < 4:
            extra.append(("unit", VP[h - 1], b + 1))
        half = (len(extra) + 1) // 2
        if t + LEAD < total:
            yield ("max", t + LEAD, 0)
        yield ("exp", t, 0)
        yield from extra[:half]
        yield ("exp", t, 1)
        if t + LEAD < total:
            yield ("max", t + LEAD, 1)
            if (t + LEAD) % HH == HH - 1:
                yield ("unit", "m", (t + LEAD) // HH)
        yield ("exp", t, 2)
        yield from extra[half:]
        if t >= 1:
            yield ("pv", t - 1)
            if t % HH == 0:
                yield ("onorm", t // HH - 1)
                if t // HH + 2 < 2 * B:
                    yield ("stack", t // HH + 2)
    yield ("pv", total - 1)
    yield ("onorm", 2 * B - 1)
    for n in TAIL_NAMES:
        yield ("unit", n, B - 1)


STEPS = list(schedule())
UNIT = {s[1:]: i for i, s in enumerate([s for s in STEPS if s[0] == "unit"])}
ORDER = sorted(UNIT, key=UNIT.get)


def last_read(i):
    who = READS_LAST[ORDER[i][0]]
    return who, sum(READS_LAST[n] == who for n, _ in ORDER[:i + 1])


def build(nc, hT, x, mask, cols, rows, ident_in, block_in, w_kq, w_vo, w_up, w_down, w_maa1, w_maa2, w_td1, w_td2,
          w_sq, out):
    ctx = ExitStack()
    with ctx:
        def sb(name, shape, dt=F32):
            return ctx.enter_context(nc.sbuf_tensor(name, shape, dt))

        def sem(name):
            return ctx.enter_context(nc.semaphore(name))

        COL = sb("COL", [P, NCOLS])
        ROW = sb("ROW", [P, len(ROWS), E])
        ident = sb("ident", [P, P])
        identb = sb("identb", [P, P], BF16)
        block = sb("block", [P, P // S])
        Wkq = sb("Wkq", [P, 2, C, E])
        Wvo = sb("Wvo", [P, 2, C, E])
        Wup = sb("Wup", [P, C, FF])
        Wdown = sb("Wdown", [P, FC, E])
        Wmaa1 = sb("Wmaa1", [P, C, NF * DM])
        Wmaa2 = sb("Wmaa2", [P, E])
        Wmaa2g = sb("Wmaa2g", [DM, E])
        Wtd1 = sb("Wtd1", [P, C, DD])
        Wtd2 = sb("Wtd2", [DD, E])
        Wsq = sb("Wsq", [P, len(SQUARE), C, E])
        half = sb("half", [P, 2 * H])
        masks = sb("masks", [1, B, TC], I32)
        maskrow = sb("maskrow", [1, B, NK], BF16)

        hTs = [sb(f"hT{i}", [P, C, NK]) for i in range(2)]
        A = sb("A", [P, 2 * S * TQ + S * (TQ + 1)])
        kq = [A[:, c * (NK + TQ):(c + 1) * (NK + TQ)] for c in range(C)]
        at = C * (NK + TQ)
        parts = A[:, at:at + 3 * (NK + TQ)].bitcast(BF16).rearrange("p (k c n) -> p k c n", k=3, c=C)
        Kst = [sb(f"Kst{i}", [P, HH, NK], BF16) for i in range(3)]
        Qst = [sb(f"Qst{i}", [P, HH, TQ], BF16) for i in range(3)]
        Vn = [sb(f"Vn{i}", [P, NT, NH, VW]) for i in range(2)]
        probs = [sb(f"probs{i}", [P, NT, TQ]) for i in range(2)]
        mx = [sb(f"mx{i}", [P, QT, HH]) for i in range(2)]
        mhl = sb("mhl", [P, QT, 2, HH], BF16)
        mT = sb("mT", [2 * HH, TQ], BF16)
        rsum = sb("rsum", [P, QT, HH])
        osb = sb("osb", [P, QT, E])

        xob = sb("xob", [P, QT, E])
        xb2 = sb("xb2", [P, QT, E])
        Z = sb("Z", [P, QT, E])
        T = sb("T", [P, C, TQ])
        XA = sb("XA", [P, C, 1 + TQ])
        SX = sb("SX", [P, C, TQ])
        KT = sb("KT", [P, C, TQ])
        RT = sb("RT", [P, C, TQ])
        WD = sb("WD", [P, C, TQ])
        VT = sb("VT", [P, C, TQ])
        G2 = sb("G2", [P, QT, E])
        TH = sb("TH", [P, QT, E])
        VN = XA[:, :, 0:TQ]
        RUK = T[:, :, :]
        KV = [A[:, c * S * TQ:(c + 1) * S * TQ].rearrange("p (j t) -> p j t", j=S)
              for c in range(C)]
        ST8 = A[:, C * S * TQ:]
        states = ST8.rearrange("p (j t) -> p j t", j=S)
        U = KV[0]
        stat = sb("stat", [P, QT, 6])
        mv = sb("mv", [P, QT, 2])
        ss = sb("ss", [P, QT])
        rstd = sb("rstd", [P, QT])
        gsum = sb("gsum", [P, QT * H])
        gsq = sb("gsq", [P, QT * H])
        grstd = sb("grstd", [P, QT * H])

        def mixbuf(n):
            return ST8[:, n * C * TQ:(n + 1) * C * TQ].rearrange("p (c t) -> p c t", c=C)

        MIXBUF = {"v": 0, "k": 1, "w": 2, "r": 3, "g": 0}

        pMX = ctx.enter_context(nc.psum_tensor("pMX", [P, 1024], F32))
        pST = [ctx.enter_context(nc.psum_tensor(f"pST{i}", [P, 2, TQ], F32)) for i in range(3)]
        pO = ctx.enter_context(nc.psum_tensor("pO", [P, 512], F32))
        pW = [ctx.enter_context(nc.psum_tensor(f"pW{i}", [P, 512], F32)) for i in range(2)]
        o_ps = pO[:, 0:QT * HH * VW].rearrange("p (t h d) -> p t h d", t=QT, h=HH)

        skd = nc.dram_tensor("k_stack", (B, NB, DH, NH, NK), BF16, kind="Internal").ap()
        sqd = nc.dram_tensor("q_stack", (B, NB, DH, NH, TQ), BF16, kind="Internal").ap()
        svd = nc.dram_tensor("v_rows", (B, E, TQ), F32, kind="Internal").ap()

        unit_ready = sem("unit_ready")
        taken_by = {"A": sem("taken_by_act"), "D": sem("taken_by_dve")}
        hT_in = [sem(f"hT_in{i}") for i in range(2)]
        w_in = {n: sem(f"in_{n}") for n in ("kq", "vo", "const", "mask", "mlp", "maa", "sq")}
        const_ok = sem("const_ok")
        identb_ok = sem("identb_ok")
        rows_set = sem("rows_set")
        mask_ok = sem("mask_ok")
        kq_hi = sem("kq_hi")
        kq_rem = sem("kq_rem")
        kq_mid = sem("kq_mid")
        kq_lo = sem("kq_lo")
        kq_out = sem("kq_out")
        stack_in = [sem(f"stack_in{i}") for i in range(3)]
        max_ready, max_done = sem("max_ready"), sem("max_done")
        m_split = sem("m_split")
        m_hi = sem("m_hi")
        m_in = [sem(f"m_in{i}") for i in range(2)]
        st_ready, exp_done = sem("st_ready"), sem("exp_done")
        pv_done = sem("pv_done")
        rs_done = sem("rs_done")
        o_freed = sem("o_freed")
        x_in = sem("x_in")
        v_out, v_in = sem("v_out"), [sem(f"v_in{c}") for c in range(C)]
        out_done = sem("out_done")
        names = ("xob xb ob sq rr1 rs1 z gelu st1 mv1 rr2 rs2 z2 c0 sx xin mix_v mix_k mix_w mix_r mix_g wd rk ruk th "
                 "kv0 kv1 sc0 sc1 p0 p1 gs gc gq gv ge gp gr gw gb gg st2 mv2 rr3 rs3 z3 c1 sx2 xk xr kk fo").split()
        did = {n: sem(f"did_{n}") for n in names}

        def col(name, i=0, n=1, p=P):
            return COL[0:p, COLS[name][0] + i:COLS[name][0] + i + n]

        def row(name, n=QT):
            return ROW[:, ROWS[name], :][:, None, :].to_broadcast([P, n, E])

        def tiles(ap):
            return ap.rearrange("p (a n) -> p a n", a=2)

        def taken(eng, name, b):
            who, n = last_read(UNIT[name, b])
            eng.wait_ge(taken_by[who], n)

        def ready(eng, name, b):
            eng.wait_ge(unit_ready, UNIT[name, b] + 1)
            return pW[UNIT[name, b] % 2]

        blk = ctx.enter_context(nc.Block())

        @blk.sync
        def _(sp):
            sp.dma_start(hTs[0][:], hT[0].rearrange("(c p) n -> p c n", p=P)).then_inc(hT_in[0], 16)
            sp.dma_start(Wkq[:], w_kq).then_inc(w_in["kq"], 16)
            sp.dma_start(masks[:], mask).then_inc(w_in["mask"], 16)
            sp.dma_start(hTs[1][:], hT[1].rearrange("(c p) n -> p c n", p=P)).then_inc(hT_in[1], 16)
            sp.dma_start(Wvo[:], w_vo).then_inc(w_in["vo"], 16)
            sp.dma_start(Wup[:], w_up).then_inc(w_in["mlp"], 16)
            sp.dma_start(Wdown[:], w_down).then_inc(w_in["mlp"], 16)
            sp.dma_start(Wmaa1[:], w_maa1).then_inc(w_in["maa"], 16)
            sp.dma_start(Wmaa2[:], w_maa2[0:P, :]).then_inc(w_in["maa"], 16)
            sp.dma_start(Wmaa2g[:], w_maa2[P:P + DM, :]).then_inc(w_in["maa"], 16)
            sp.dma_start(Wtd1[:], w_td1).then_inc(w_in["maa"], 16)
            sp.dma_start(Wtd2[:], w_td2).then_inc(w_in["maa"], 16)
            sp.dma_start(Wsq[:], w_sq).then_inc(w_in["sq"], 16)
            for step in STEPS:
                kind = step[0]
                if kind == "spill":
                    b = step[1]
                    sp.wait_ge(kq_lo, C * (b + 1))
                    for k in range(NB):
                        sp.dma_start(skd[b, k].rearrange("d (h c) n -> (d h) c n", c=C),
                                     parts[:, KPART[k], :, 0:NK]).then_inc(kq_out, 16)
                        sp.dma_start(sqd[b, k].rearrange("d (h c) n -> (d h) c n", c=C),
                                     parts[:, QPART[k], :, NK:NK + TQ]).then_inc(kq_out, 16)
                elif kind == "stack":
                    hf = step[1]
                    b, part = divmod(hf, 2)
                    s = hf % 3
                    sp.wait_ge(kq_out, 2 * NB * 16 * (b + 1))
                    if hf >= 3:
                        sp.wait_ge(pv_done, HH * (hf - 2))
                    else:
                        sp.wait_ge(const_ok, 1)
                    sp.wait_ge(mask_ok, 1)
                    sp.dma_start(Kst[s][0:NB * DH], skd[b].rearrange("k d h n -> (k d) h n")[:, part * HH:(part + 1) * HH])\
                        .then_inc(stack_in[s], 16)
                    sp.dma_start(Qst[s][0:NB * DH], sqd[b].rearrange("k d h n -> (k d) h n")[:, part * HH:(part + 1) * HH])\
                        .then_inc(stack_in[s], 16)
                    sp.dma_start(Kst[s][R_MASK:R_MASK + 1],
                                 maskrow[0:1, b, :][:, None, :].to_broadcast([1, HH, NK])).then_inc(stack_in[s], 16)
                elif kind == "unit" and step[1] == "vp2" and step[2] + 2 < B:
                    b = step[2]
                    ready(sp, "vp2", b)
                    sp.dma_start(hTs[b % 2][:], hT[b + 2].rearrange("(c p) n -> p c n", p=P)).then_inc(hT_in[b % 2], 16)
                elif kind == "unit" and step[1] == "m":
                    hf = step[2]
                    s = hf % 3
                    taken(sp, "m", hf)
                    for part, r in ((0, R_HI), (1, R_LO)):
                        sp.dma_start(Qst[s][r:r + 1, :, :], mT[part * HH:(part + 1) * HH, :]).then_inc(m_in[hf % 2], 16)
                elif kind == "onorm" and step[1] % 2 == 1:
                    b = step[1] // 2
                    if b >= 1:
                        sp.wait_ge(did["fo"], b)
                    sp.dma_start(xb2[:], x[b].rearrange("(a p) n -> p a n", p=P)).then_inc(x_in, 16)
                elif kind == "unit" and step[1] == "v":
                    b = step[2]
                    taken(sp, "v", b)
                    sp.dma_start(svd[b].rearrange("(c p) t -> p c t", p=P), VT[:]).then_inc(v_out, 16)
                    sp.wait_ge(v_out, 16 * (b + 1))
                    if b == 0:
                        sp.wait_ge(kq_out, 2 * NB * 16 * B)
                    taken(sp, "down", b)
                    for c in range(C):
                        src = svd[b].rearrange("(c h j) t -> c h (j t)", c=C, j=S)[c]
                        sp.dma_start(KV[c].rearrange("p j t -> p (j t)"),
                                     src[:, None, :].to_broadcast([P // S, S, S * TQ])).then_inc(v_in[c], 16)
                elif kind == "unit" and step[1] == "fv":
                    b = step[2]
                    sp.wait_ge(did["fo"], b + 1)
                    sp.dma_start(out[b].rearrange("(a p) n -> p a n", p=P), Z[:]).then_inc(out_done, 16)
            sp.wait_ge(out_done, 16 * B)
            sp.wait_ge(kq_out, 2 * NB * 16 * B)
            sp.wait_ge(v_out, 16 * B)

        @blk.tensor
        def _(pe):
            mm = nc.tensor.matmul

            def claim(name, b):
                i = UNIT[name, b]
                if i >= 2:
                    who, n = last_read(i - 2)
                    pe.wait_ge(taken_by[who], n)
                return pW[i % 2]

            def square(name, b, w, rhs_t, token_major):
                bk = claim(name, b)
                for m in range(2):
                    for c in range(C):
                        if token_major:
                            lhs, rhs = rhs_t[:, c, m * P:(m + 1) * P], w[:, c, :]
                        else:
                            lhs, rhs = w[:, c, m * P:(m + 1) * P], rhs_t[:, c, :]
                        last = mm(bk[:, m * 256:(m + 1) * 256], lhs, rhs, start=c == 0, stop=c == C - 1)
                last.then_inc(unit_ready, 1)

            def transposes(name, b, src):
                bk = claim(name, b)
                for c in range(C):
                    for a in range(QT):
                        last = nc.tensor.transpose(bk[:, c * TQ + a * P:c * TQ + (a + 1) * P],
                                                   src[:, a, c * P:(c + 1) * P], ident[:])
                last.then_inc(unit_ready, 1)

            pe.wait_ge(w_in["kq"], 16)
            pe.wait_ge(const_ok, 1)
            for step in STEPS:
                kind = step[0]
                if kind == "max":
                    _, t, qt = step
                    n = t * QT + qt
                    hf, h = divmod(t, HH)
                    s = hf % 3
                    if h == 0 and qt == 0:
                        pe.wait_ge(stack_in[s], 48 * (hf // 3 + 1))
                    if n >= 1:
                        pe.wait_ge(max_done, n)
                    lhs = Qst[s][0:R_MASK + 1, h, qt * P:(qt + 1) * P]
                    mm(pMX[:, 0:512], lhs, Kst[s][0:R_MASK + 1, h, 0:512], start=True, stop=True)
                    mm(pMX[:, 512:NK], lhs, Kst[s][0:R_MASK + 1, h, 512:NK], start=True, stop=True)\
                        .then_inc(max_ready, 1)
                elif kind == "exp":
                    _, t, pair = step
                    n = 3 * t + pair
                    hf, h = divmod(t, HH)
                    s = hf % 3
                    if h == 0 and pair == 0:
                        pe.wait_ge(m_in[hf % 2], 32 * (hf // 2 + 1))
                    if n >= 3:
                        pe.wait_ge(exp_done, n - 2)
                    for i in range(2):
                        nt = 2 * pair + i
                        last = mm(pST[n % 3][:, i, :], Kst[s][0:R_LO + 1, h, nt * P:(nt + 1) * P],
                                  Qst[s][0:R_LO + 1, h, :], start=True, stop=True)
                    last.then_inc(st_ready, 1)
                elif kind == "pv":
                    t = step[1]
                    b, h = divmod(t, NH)
                    if t % HH == 0:
                        if t:
                            pe.wait_ge(o_freed, t // HH)
                    if h == 0:
                        taken(pe, "vp2", b)
                    pe.wait_ge(exp_done, 3 * (t + 1))
                    for qt in range(QT):
                        for nt in range(NT):
                            last = mm(o_ps[:, qt, h % HH, :], probs[t % 2][:, nt, qt * P:(qt + 1) * P],
                                      Vn[b % 2][:, nt, h, :], start=nt == 0, stop=nt == NT - 1)
                    last.then_inc(pv_done, 1)
                elif kind == "unit":
                    _, name, b = step
                    if name[:2] == "kq":
                        c, piece = int(name[2]), int(name[3])
                        hb = hTs[b % 2]
                        if c == 0 and piece == 0:
                            pe.wait_ge(hT_in[b % 2], 16 * (b // 2 + 1))
                        bk = claim(name, b)
                        jobs = ((0, 0, 512, 0),) if piece == 0 else ((0, 512, NK, 0), (1, TC, NK, 256))
                        for w, lo, hi, at in jobs:
                            for kc in range(C):
                                last = mm(bk[:, at:at + hi - lo], Wkq[:, w, kc, c * P:(c + 1) * P], hb[:, kc, lo:hi],
                                          start=kc == 0, stop=kc == C - 1)
                        last.then_inc(unit_ready, 1)
                    elif name[:2] == "vp":
                        hb = hTs[b % 2]
                        if b == 0 and name == "vp0":
                            pe.wait_ge(w_in["vo"], 16)
                        bk = claim(name, b)
                        for i in range(2):
                            nt = 2 * int(name[2]) + i
                            for kc in range(C):
                                last = mm(bk[:, i * E:(i + 1) * E], hb[:, kc, nt * P:(nt + 1) * P], Wvo[:, 0, kc, :],
                                          start=kc == 0, stop=kc == C - 1)
                        last.then_inc(unit_ready, 1)
                    elif name == "m":
                        pe.wait_ge(m_split, b + 1)
                        if b == 0:
                            pe.wait_ge(identb_ok, 1)
                        bk = claim(name, b)[:, :].bitcast(BF16)
                        for qt in range(QT):
                            last = nc.tensor.transpose(bk[0:2 * HH, qt * P:(qt + 1) * P],
                                                       mhl[:, qt, :, :].rearrange("p l h -> p (l h)"), identb[:])
                        last.then_inc(unit_ready, 1)
                    elif name == "oT":
                        pe.wait_ge(did["ob"], b + 1)
                        if b == 0:
                            pe.wait_ge(w_in["const"], 64)
                        transposes(name, b, osb)
                    elif name == "proj":
                        taken(pe, "oT", b)
                        square(name, b, Wvo[:, 1], T, True)
                    elif name == "zT":
                        pe.wait_ge(did["z"], b + 1)
                        transposes(name, b, Z)
                    elif name[:2] == "up":
                        if name == "up0":
                            taken(pe, "zT", b)
                            if b == 0:
                                pe.wait_ge(w_in["mlp"], 32)
                        bk = claim(name, b)
                        for i in range(2):
                            f = 2 * int(name[2]) + i
                            for c in range(C):
                                last = mm(bk[:, i * TQ:(i + 1) * TQ], Wup[:, c, f * P:(f + 1) * P], T[:, c, :],
                                          start=c == 0, stop=c == C - 1)
                        last.then_inc(unit_ready, 1)
                    elif name == "down":
                        pe.wait_ge(did["gelu"], b + 1)
                        bk = claim(name, b)
                        for a in range(QT):
                            for f in range(FC):
                                last = mm(bk[:, a * E:(a + 1) * E], U[:, f, a * P:(a + 1) * P], Wdown[:, f, :],
                                          start=f == 0, stop=f == FC - 1)
                        last.then_inc(unit_ready, 1)
                    elif name == "xaT":
                        pe.wait_ge(did["z2"], b + 1)
                        transposes(name, b, Z)
                    elif name == "maa1":
                        pe.wait_ge(did["xin"], b + 1)
                        if b == 0:
                            pe.wait_ge(w_in["maa"], 80)
                        bk = claim(name, b)
                        for c in range(C):
                            mm(bk[:, 0:TQ], Wmaa1[:, c, 0:P], T[:, c, :], start=c == 0, stop=c == C - 1)
                        for c in range(C):
                            last = mm(bk[0:DM, TQ:2 * TQ], Wmaa1[:, c, P:NF * DM], T[:, c, :],
                                      start=c == 0, stop=c == C - 1)
                        last.then_inc(unit_ready, 1)
                    elif name[:4] == "mix_":
                        f = MIX[name[4]]
                        taken(pe, "maa1", b)
                        bk = claim(name, b)
                        for c in range(C):
                            if f < 4:
                                lhs, rhs = Wmaa2[f * DM:(f + 1) * DM, c * P:(c + 1) * P], xob[f * DM:(f + 1) * DM, 0, :]
                            else:
                                lhs, rhs = Wmaa2g[:, c * P:(c + 1) * P], xob[0:DM, 1, :]
                            last = mm(bk[:, c * TQ:(c + 1) * TQ], lhs, rhs, start=True, stop=True)
                        last.then_inc(unit_ready, 1)
                    elif name in ("v", "k", "r", "g"):
                        if b == 0 and name == "v":
                            pe.wait_ge(w_in["sq"], 16)
                        pe.wait_ge(did["mix_" + name], b + 1)
                        square(name, b, Wsq[:, SQUARE.index("W" + name)], mixbuf(MIXBUF[name]), name == "g")
                    elif name == "td1":
                        pe.wait_ge(did["mix_w"], b + 1)
                        bk = claim(name, b)
                        for c in range(C):
                            last = mm(bk[0:DD, 0:TQ], Wtd1[:, c, :], mixbuf(MIXBUF["w"])[:, c, :],
                                      start=c == 0, stop=c == C - 1)
                        last.then_inc(unit_ready, 1)
                    elif name == "td2":
                        taken(pe, "td1", b)
                        bk = claim(name, b)
                        for c in range(C):
                            last = mm(bk[:, c * TQ:(c + 1) * TQ], Wtd2[:, c * P:(c + 1) * P], TH[0:DD, 0, :],
                                      start=True, stop=True)
                        last.then_inc(unit_ready, 1)
                    elif name == "vN":
                        taken(pe, "v", b)
                        bk = claim(name, b)
                        for a in range(QT):
                            for c in range(C):
                                last = nc.tensor.transpose(bk[:, a * E + c * P:a * E + (c + 1) * P],
                                                           VT[:, c, a * P:(a + 1) * P], ident[:])
                        last.then_inc(unit_ready, 1)
                    elif name == "diag":
                        pe.wait_ge(did["ruk"], b + 1)
                        bk = claim(name, b)
                        for a in range(QT):
                            for c in range(C):
                                at = a * H + c * (P // S)
                                last = mm(bk[:, at:at + P // S], RUK[:, c, a * P:(a + 1) * P], block[:],
                                          start=True, stop=True)
                        last.then_inc(unit_ready, 1)
                    elif name == "wkv":
                        bk = claim(name, b)
                        for c in range(C):
                            pe.wait_ge(did["p0" if c == 0 else "p1"], b + 1)
                            for a in range(QT):
                                for j in range(S):
                                    at = a * E + j * H + c * (P // S)
                                    last = mm(bk[:, at:at + P // S], KV[c][:, j, a * P:(a + 1) * P], block[:],
                                              start=True, stop=True)
                        last.then_inc(unit_ready, 1)
                    elif name == "ogT":
                        pe.wait_ge(did["gg"], b + 1)
                        transposes(name, b, SX)
                    elif name == "wo":
                        taken(pe, "ogT", b)
                        square(name, b, Wsq[:, SQUARE.index("Wo")], T, True)
                    elif name == "xcT":
                        pe.wait_ge(did["z3"], b + 1)
                        transposes(name, b, Z)
                    elif name == "rr":
                        pe.wait_ge(did["xr"], b + 1)
                        square(name, b, Wsq[:, SQUARE.index("Wfr")], RT, True)
                    elif name == "kk":
                        square(name, b, Wsq[:, SQUARE.index("Wfk")], KT, False)
                    elif name == "fv":
                        pe.wait_ge(did["kk"], b + 1)
                        square(name, b, Wsq[:, SQUARE.index("Wfv")], VT, True)

        @blk.scalar
        def _(act):
            act_fn = nc.scalar.activation
            act.dma_start(COL[:], cols).then_inc(w_in["const"], 16)
            act.dma_start(ident[:], ident_in).then_inc(w_in["const"], 16)
            act.dma_start(block[:], block_in).then_inc(w_in["const"], 16)
            act.dma_start(ROW[:, :, :].rearrange("p r n -> p (r n)"), rows.to_broadcast([P, len(ROWS) * E]))\
                .then_inc(w_in["const"], 16)
            act.wait_ge(w_in["const"], 64)
            for step in STEPS:
                kind = step[0]
                if kind == "exp":
                    _, t, pair = step
                    n = 3 * t + pair
                    act.wait_ge(st_ready, n + 1)
                    if pair == 0 and t >= 2:
                        act.wait_ge(pv_done, t - 1)
                    act_fn(probs[t % 2][:, 2 * pair:2 * pair + 2, :], pST[n % 3][:], ACT.Exp).then_inc(exp_done, 1)
                    continue
                if kind != "unit":
                    continue
                _, name, b = step
                if name in ("kq01", "kq11"):
                    c = int(name[2])
                    n = C * b + c
                    taken(act, name, b)
                    if b >= 1:
                        act.wait_ge(kq_out, 2 * NB * 16 * b)
                    act_fn(parts[:, 0, c, :], kq[c], ACT.Copy).then_inc(kq_hi, 1)
                    act.wait_ge(kq_rem, n + 1)
                    act_fn(parts[:, 1, c, :], kq[c], ACT.Copy).then_inc(kq_mid, 1)
                elif name == "proj":
                    taken(act, name, b)
                    if b >= 1:
                        act.wait_ge(out_done, 16 * b)
                    for a in range(QT):
                        last = act_fn(Z[:, a, :], xob[:, a, :], ACT.Square, accum_out=ss[:, a:a + 1])
                    last.then_inc(did["sq"], 1)
                elif name == "up3":
                    taken(act, name, b)
                    act_fn(U, U, ACT.Gelu_apprx_tanh).then_inc(did["gelu"], 1)
                elif name == "g":
                    bk = ready(act, name, b)
                    act_fn(TH[:], tiles(bk[:]), ACT.Tanh, scale=0.5).then_inc(did["th"], 1)
                elif READS_LAST[name] == "A":
                    bk = ready(act, name, b)
                    view = tiles(bk[:])
                    if name[:2] == "vp":
                        i = int(name[2])
                        if b == 0 and i == 0:
                            act.wait_ge(const_ok, 1)
                        if b >= 2 and i == 0:
                            act.wait_ge(pv_done, NH * (b - 1))
                        last = act_fn(Vn[b % 2][:, 2 * i:2 * i + 2, :, 0:DH],
                                 bk[:, :].rearrange("p (a h d) -> p a h d", a=2, h=NH), ACT.Copy)
                    elif name == "m":
                        if b >= 1:
                            act.wait_ge(m_in[(b - 1) % 2], 32 * ((b - 1) // 2 + 1))
                        last = act_fn(mT[:], bk[:, :].bitcast(BF16)[0:2 * HH, 0:TQ], ACT.Copy)
                    elif name == "ogT":
                        last = act_fn(T[:], view, ACT.Copy, scale=0.5)
                    elif name == "zT":
                        for c in range(C):
                            last = act_fn(T[:, c, :], view[:, c, :], ACT.Copy, scale=col("post_w", c))
                    elif name in ("xaT", "xcT"):
                        ln = "ln1" if name == "xaT" else "ln2"
                        for c in range(C):
                            last = act_fn(XA[:, c, 1:1 + TQ], view[:, c, :], ACT.Identity,
                                     bias=col(ln + "_b", c), scale=col(ln + "_w", c))
                    elif name == "maa1":
                        act_fn(xob[:, 0, :], bk[:, 0:TQ], ACT.Tanh)
                        last = act_fn(xob[0:DM, 1, :], bk[0:DM, TQ:2 * TQ], ACT.Tanh)
                    elif name == "td1":
                        last = act_fn(TH[0:DD, 0, :], bk[0:DD, 0:TQ], ACT.Tanh)
                    elif name == "td2":
                        for c in range(C):
                            last = act_fn(WD[:, c, :], view[:, c, :], ACT.Exp, bias=col("decay", c))
                    elif name == "rr":
                        last = act_fn(TH[:], view, ACT.Tanh, scale=0.5)
                    elif name == "kk":
                        last = act_fn(WD[:], view, ACT.Relu)
                    else:
                        if name == "vN":
                            act.wait_ge(did["mix_g"], b + 1)
                        dst = {"oT": T, "v": VT, "k": KT, "r": RT, "vN": VN}[name]
                        last = act_fn(dst[:, :, :], view, ACT.Copy)
                    last.then_inc(taken_by["A"], 1)
                    if name == "td2":
                        taken(act, name, b)
                        act_fn(WD[:], WD[:], ACT.Exp, scale=-1.0).then_inc(did["wd"], 1)

        @blk.gpsimd
        def _(pool):
            g = nc.gpsimd
            for s in range(3):
                g.memset(Kst[s][R_MASK:R_LO + 1], 1.0)
                last = g.memset(Qst[s][R_MASK:R_LO + 1], 1.0)
            last.then_inc(rows_set, 1)
            pool.wait_ge(rows_set, 1)
            for i in range(2):
                g.memset(Vn[i][:], 1.0)
            g.memset(half[:], -0.5).then_inc(const_ok, 1)
            pool.wait_ge(const_ok, 1)

            def root(src, dst, scale, eps, n, first, second, b):
                g.tensor_scalar(dst, src, scale, eps, ALU.mult, ALU.add).then_inc(did[first], 1)
                pool.wait_ge(did[first], b + 1)
                g.tensor_tensor(dst, dst, half[:, 0:n], ALU.pow).then_inc(did[second], 1)

            for step in STEPS:
                kind = step[0]
                if kind == "onorm" and step[1] % 2 == 1:
                    b = step[1] // 2
                    if b == 0:
                        pool.wait_ge(w_in["const"], 64)
                    pool.wait_ge(x_in, 16 * (b + 1))
                    g.tensor_tensor(xob[:], xb2[:], row("out_b"), ALU.add).then_inc(did["xob"], 1)
                    pool.wait_ge(did["xob"], b + 1)
                    g.tensor_tensor(xb2[:], xb2[:], row("b2"), ALU.add).then_inc(did["xb"], 1)
                    pool.wait_ge(o_freed, 2 * (b + 1))
                    g.tensor_tensor(osb[:], osb[:], row("v_b"), ALU.add).then_inc(did["ob"], 1)
                if kind != "unit":
                    continue
                _, name, b = step
                if name in ("kq01", "kq11"):
                    c = int(name[2])
                    n = C * b + c
                    pool.wait_ge(kq_hi, n + 1)
                    g.tensor_tensor(kq[c], kq[c], parts[:, 0, c, :], ALU.subtract).then_inc(kq_rem, 1)
                    pool.wait_ge(kq_mid, n + 1)
                    g.tensor_tensor(parts[:, 2, c, :], kq[c], parts[:, 1, c, :], ALU.subtract).then_inc(kq_lo, 1)
                elif name == "proj":
                    pool.wait_ge(did["sq"], b + 1)
                    root(ss[:], rstd[:], 1.0 / E, 1e-6, QT, "rr1", "rs1", b)
                elif name == "down":
                    pool.wait_ge(did["mv1"], b + 1)
                    root(mv[:, :, 1], rstd[:], 1.0, 1e-5, QT, "rr2", "rs2", b)
                elif name in ("xaT", "xcT"):
                    first = name == "xaT"
                    at = COLS["shift0"][0] + b * C * 2
                    prev = COL[:, at:at + 2 * C].rearrange("p (c k) -> p c k", c=C)[:, :, 1 if first else 0]
                    taken(pool, name, b)
                    g.tensor_copy(XA[:, :, 0], prev).then_inc(did["c0" if first else "c1"], 1)
                    pool.wait_ge(did["c0" if first else "c1"], b + 1)
                    g.tensor_tensor(SX[:], XA[:, :, 0:TQ], XA[:, :, 1:1 + TQ], ALU.subtract)\
                     .then_inc(did["sx" if first else "sx2"], 1)
                elif name[:4] == "mix_":
                    taken(pool, name, b)
                    mb = mixbuf(MIXBUF[name[4]])
                    g.tensor_tensor(mb, mb, XA[:, :, 1:1 + TQ], ALU.add).then_inc(did[name], 1)
                elif name == "r":
                    taken(pool, "r", b)
                    g.tensor_tensor(RUK, RT[:], KT[:], ALU.mult).then_inc(did["rk"], 1)
                    pool.wait_ge(did["rk"], b + 1)
                    for c in range(C):
                        last = g.tensor_scalar(RUK[:, c, :], RUK[:, c, :], col("u", c), None, ALU.mult)
                    last.then_inc(did["ruk"], 1)
                elif name == "g":
                    pool.wait_ge(v_in[0], 16 * (b + 1))
                    g.tensor_tensor(KV[0], KV[0], KT[:, 0, :][:, None, :].to_broadcast([P, S, TQ]), ALU.mult)\
                     .then_inc(did["kv0"], 1)
                    pool.wait_ge(did["sc0"], b + 1)
                    g.tensor_tensor(KV[0], states[:, :, 0:TQ], RT[:, 0, :][:, None, :].to_broadcast([P, S, TQ]),
                                    ALU.mult).then_inc(did["p0"], 1)
                elif name == "wkv":
                    pool.wait_ge(did["gc"], b + 1)
                    g.tensor_tensor(T[:], SX[:], SX[:], ALU.mult).then_inc(did["gq"], 1)
                    pool.wait_ge(did["gv"], b + 1)
                    root(gsq[:], grstd[:], 1.0 / S, 1e-5, QT * H, "ge", "gp", b)
                    pool.wait_ge(did["gr"], b + 1)
                    g.tensor_tensor(SX[:], SX[:], row("gn_w"), ALU.mult).then_inc(did["gw"], 1)
                    pool.wait_ge(did["gw"], b + 1)
                    g.tensor_tensor(SX[:], SX[:], row("gn_b"), ALU.add).then_inc(did["gb"], 1)
                elif name == "wo":
                    pool.wait_ge(did["mv2"], b + 1)
                    root(mv[:, :, 1], rstd[:], 1.0, 1e-5, QT, "rr3", "rs3", b)
                elif name == "kk":
                    taken(pool, "kk", b)
                    g.tensor_tensor(VT[:], WD[:], WD[:], ALU.mult).then_inc(did["kk"], 1)

        @blk.vector
        def _(dve):
            v = nc.vector
            dve.wait_ge(w_in["mask"], 16)
            v.tensor_scalar(maskrow[:, :, 0:TC], masks[:], 0, MASKED, ALU.is_equal, ALU.mult)
            v.memset(maskrow[:, :, TC:NK], 0.0).then_inc(mask_ok, 1)
            dve.wait_ge(w_in["const"], 64)
            v.tensor_copy(identb[:], ident[:]).then_inc(identb_ok, 1)

            def layernorm(x_, b, st, m, root_name, z):
                for a in range(QT):
                    last = v.bn_stats(stat[:, a, :], x_[:, a, :])
                last.then_inc(did[st], 1)
                dve.wait_ge(did[st], b + 1)
                for a in range(QT):
                    last = v.bn_aggr(mv[:, a, :], stat[:, a, :])
                last.then_inc(did[m], 1)
                dve.wait_ge(did[root_name], b + 1)
                for a in range(QT):
                    last = v.tensor_scalar(Z[:, a, :], x_[:, a, :], mv[:, a, 0:1], rstd[:, a:a + 1],
                                           ALU.subtract, ALU.mult)
                last.then_inc(did[z], 1)

            def scan(c, b, done):
                at = COLS["state0"][0] + (b * C + c) * S
                v.tensor_copy(states[:, :, 0], COL[:, at:at + S])
                for j in range(S):
                    last = v.tensor_tensor_scan(states[:, j, 1:1 + TQ], WD[:, c, :], KV[c][:, j, :],
                                                COL[:, at + j:at + j + 1], ALU.mult, ALU.add)
                last.then_inc(did[done], 1)

            for step in STEPS:
                kind = step[0]
                if kind == "max":
                    _, t, qt = step
                    hf, h = divmod(t, HH)
                    dve.wait_ge(max_ready, t * QT + qt + 1)
                    v.tensor_reduce(mx[hf % 2][:, qt, h:h + 1], pMX[:, 0:NK], AX.X, ALU.max).then_inc(max_done, 1)
                elif kind == "onorm":
                    hf = step[1]
                    b, part = divmod(hf, 2)
                    dve.wait_ge(pv_done, HH * (hf + 1))
                    v.reciprocal(rsum[:], o_ps[:, :, :, DH]).then_inc(rs_done, 1)
                    dve.wait_ge(rs_done, hf + 1)
                    if b >= 1 and part == 0:
                        taken(dve, "oT", b - 1)
                    v.tensor_tensor(osb[:, :, part * HH * DH:(part + 1) * HH * DH].rearrange("p a (h d) -> p a h d", h=HH),
                                    o_ps[:, :, :, 0:DH], rsum[:, :, :, None].to_broadcast([P, QT, HH, DH]), ALU.mult)\
                     .then_inc(o_freed, 1)
                elif kind == "unit":
                    _, name, b = step
                    if name == "m":
                        hf = b
                        dve.wait_ge(max_done, HH * QT * (hf + 1))
                        if hf >= 1:
                            ready(dve, "m", hf - 1)
                        v.tensor_scalar(mhl[:, :, 0, :], mx[hf % 2][:], -1.0, None, ALU.mult).then_inc(m_hi, 1)
                        dve.wait_ge(m_hi, hf + 1)
                        v.scalar_tensor_tensor(mhl[:, :, 1, :], mx[hf % 2][:], -1.0, mhl[:, :, 0, :],
                                               ALU.mult, ALU.subtract).then_inc(m_split, 1)
                    elif name == "xaT":
                        dve.wait_ge(did["sx"], b + 1)
                        for c in range(C):
                            last = v.scalar_tensor_tensor(T[:, c, :], SX[:, c, :], col("maa_x", c), XA[:, c, 1:1 + TQ],
                                                          ALU.mult, ALU.add)
                        last.then_inc(did["xin"], 1)
                    elif name == "xcT":
                        dve.wait_ge(did["sx2"], b + 1)
                        for dst, w, done in ((KT, "ffn_k", "xk"), (RT, "ffn_r", "xr")):
                            for c in range(C):
                                last = v.scalar_tensor_tensor(dst[:, c, :], SX[:, c, :], col(w, c),
                                                              XA[:, c, 1:1 + TQ], ALU.mult, ALU.add)
                            last.then_inc(did[done], 1)
                    if READS_LAST[name] != "D":
                        continue
                    bk = ready(dve, name, b)
                    view = tiles(bk[:])
                    if name[:2] == "kq":
                        c, piece = int(name[2]), int(name[3])
                        if b >= 1 and piece == 0:
                            dve.wait_ge(kq_lo, C * (b - 1) + c + 1)
                        if piece == 0:
                            last = v.tensor_scalar(kq[c][:, 0:512], bk[:], col("k_b", c), None, ALU.add)
                        else:
                            v.tensor_scalar(kq[c][:, 512:NK], bk[:, 0:256], col("k_b", c), None, ALU.add)
                            last = v.tensor_scalar(kq[c][:, NK:NK + TQ], bk[:, 256:512], col("q_b", c), 1.0 / DH,
                                                   ALU.add, ALU.mult)
                        last.then_inc(taken_by["D"], 1)
                    elif name == "proj":
                        dve.wait_ge(did["xb"], b + 1)
                        v.tensor_tensor(xob[:], view, xob[:], ALU.add).then_inc(taken_by["D"], 1)
                        dve.wait_ge(did["rs1"], b + 1)
                        for a in range(QT):
                            last = v.tensor_scalar(Z[:, a, :], xob[:, a, :], rstd[:, a:a + 1], None, ALU.mult)
                        last.then_inc(did["z"], 1)
                    elif name[:2] == "up":
                        if b == 0 and name == "up0":
                            dve.wait_ge(kq_lo, C * B)
                        for i in range(2):
                            f = 2 * int(name[2]) + i
                            last = v.tensor_scalar(U[:, f, :], view[:, i, :], col("b1", f), None, ALU.add)
                        last.then_inc(taken_by["D"], 1)
                    elif name == "down":
                        v.tensor_tensor(xb2[:], view, xb2[:], ALU.add).then_inc(taken_by["D"], 1)
                        taken(dve, name, b)
                        layernorm(xb2, b, "st1", "mv1", "rs2", "z2")
                    elif name[:4] == "mix_":
                        f = MIX[name[4]]
                        if b == 0 and name == "mix_v":
                            dve.wait_ge(kq_out, 2 * NB * 16 * B)
                        for c in range(C):
                            last = v.scalar_tensor_tensor(mixbuf(MIXBUF[name[4]])[:, c, :], view[:, c, :],
                                                          col("stack", f * C + c), SX[:, c, :], ALU.add, ALU.mult)
                        last.then_inc(taken_by["D"], 1)
                    elif name == "g":
                        dve.wait_ge(did["th"], b + 1)
                        v.scalar_tensor_tensor(G2[:], TH[:], 1.0, view, ALU.add, ALU.mult)\
                         .then_inc(taken_by["D"], 1)
                        dve.wait_ge(v_in[1], 16 * (b + 1))
                        v.tensor_tensor(KV[1], KV[1], KT[:, 1, :][:, None, :].to_broadcast([P, S, TQ]), ALU.mult)\
                         .then_inc(did["kv1"], 1)
                        dve.wait_ge(did["wd"], b + 1)
                        dve.wait_ge(did["kv0"], b + 1)
                        scan(0, b, "sc0")
                    elif name == "diag":
                        dve.wait_ge(taken_by["A"], last_read(UNIT["vN", b])[1])
                        vn = VN[:, :, :].rearrange("p a (h j) -> p a h j", j=S)
                        v.tensor_tensor(vn, vn, bk[:, 0:QT * H].rearrange("p (a h) -> p a h", a=QT)[:, :, :, None]
                                        .to_broadcast([P, QT, H, S]), ALU.mult)\
                         .then_inc(taken_by["D"], 1)
                        dve.wait_ge(did["p0"], b + 1)
                        dve.wait_ge(did["kv1"], b + 1)
                        scan(1, b, "sc1")
                        dve.wait_ge(did["sc1"], b + 1)
                        v.tensor_tensor(KV[1], states[:, :, 0:TQ], RT[:, 1, :][:, None, :].to_broadcast([P, S, TQ]),
                                        ALU.mult).then_inc(did["p1"], 1)
                    elif name == "wkv":
                        o4 = SX[:, :, :].rearrange("p a (h j) -> p a h j", j=S)
                        o3 = SX[:, :, :].rearrange("p a (h j) -> p (a h) j", j=S)
                        v.tensor_tensor(o4, bk[:, :].rearrange("p (a j h) -> p a h j", a=QT, j=S),
                                        VN[:, :, :].rearrange("p a (h j) -> p a h j", j=S), ALU.add)\
                         .then_inc(taken_by["D"], 1)
                        taken(dve, name, b)
                        v.tensor_reduce(gsum[:], o3, AX.X, ALU.add).then_inc(did["gs"], 1)
                        dve.wait_ge(did["gs"], b + 1)
                        v.scalar_tensor_tensor(o3, gsum[:, :, None].to_broadcast([P, QT * H, S]), -1.0 / S, o3,
                                               ALU.mult, ALU.add).then_inc(did["gc"], 1)
                        dve.wait_ge(did["gq"], b + 1)
                        v.tensor_reduce(gsq[:], T[:, :, :].rearrange("p a (h j) -> p (a h) j", j=S), AX.X, ALU.add)\
                         .then_inc(did["gv"], 1)
                        dve.wait_ge(did["gp"], b + 1)
                        v.tensor_tensor(o3, o3, grstd[:, :, None].to_broadcast([P, QT * H, S]), ALU.mult)\
                         .then_inc(did["gr"], 1)
                        dve.wait_ge(did["gb"], b + 1)
                        v.tensor_tensor(SX[:], SX[:], G2[:], ALU.mult).then_inc(did["gg"], 1)
                    elif name == "wo":
                        v.tensor_tensor(xob[:], view, xb2[:], ALU.add).then_inc(taken_by["D"], 1)
                        taken(dve, name, b)
                        layernorm(xob, b, "st2", "mv2", "rs3", "z3")
                    elif name == "fv":
                        taken(dve, "rr", b)
                        v.scalar_tensor_tensor(G2[:], TH[:], 1.0, view, ALU.add, ALU.mult).then_inc(taken_by["D"], 1)
                        taken(dve, name, b)
                        v.scalar_tensor_tensor(Z[:], G2[:], 0.5, xob[:], ALU.mult, ALU.add).then_inc(did["fo"], 1)


def kernel(**inputs):
    import concourse.bacc as bacc
    from concourse.bass_utils import run_bass_kernel_spmd

    i = {n: np.asarray(a) for n, a in inputs.items()}
    L0 = {n[len("L0_xattn_"):]: a for n, a in i.items() if n.startswith("L0_xattn_")}
    L1 = {n[len("L1_xattn_"):]: a for n, a in i.items() if n.startswith("L1_xattn_")}
    x, ctxs = i["x"], i["ctx_2048"]

    def chunked(w):
        return w.reshape(w.shape[0] // P, P, -1).transpose(1, 0, 2).reshape(P, -1)

    def by_dim(w):
        return w.reshape(-1, NH // C, C, DH).transpose(0, 2, 3, 1).reshape(w.shape[0], E)

    kvw = L0["kv_w"].reshape(E, NH, DH, 2)
    kvb = L0["kv_b"].reshape(NH, DH, 2)
    k_w, v_w = kvw[..., 0].reshape(E, E), kvw[..., 1].reshape(E, E)
    per_partition = {
        "q_b": by_dim(L0["q_b"].reshape(1, E)).reshape(E, 1), "k_b": by_dim(kvb[..., 0].reshape(1, E)).reshape(E, 1),
        "post_w": L0["postnorm_w"].reshape(E, 1), "b1": L0["mlp_b1"].reshape(FF, 1),
        "ln1_w": L1["ln1_w"].reshape(E, 1), "ln1_b": L1["ln1_b"].reshape(E, 1),
        "ln2_w": L1["ln2_w"].reshape(E, 1), "ln2_b": L1["ln2_b"].reshape(E, 1),
        "maa_x": L1["maa_x"].reshape(E, 1), "stack": L1["maa_stack"].reshape(NF * E, 1),
        "decay": L1["time_decay"].reshape(E, 1), "u": L1["u"].reshape(E, 1),
        "ffn_k": L1["ffn_maa_k"].reshape(E, 1), "ffn_r": L1["ffn_maa_r"].reshape(E, 1),
        "shift0": ctxs[:, 0:2].transpose(0, 2, 1).reshape(B * E, 2),
        "state0": ctxs[:, 2:2 + S].reshape(B * E, S),
    }
    arrays = {
        "hT": np.concatenate([ctxs.transpose(0, 2, 1), x.transpose(0, 2, 1)], axis=2),
        "x": x,
        "mask": i["mask_BxS2_ik0"].reshape(1, B, TC),
        "cols": np.concatenate([chunked(per_partition[n]) for n in COLS], axis=1),
        "rows": np.concatenate([L0["out_b"], kvb[..., 1].reshape(E), L0["mlp_b2"], L1["gn_w"], L1["gn_b"]])[None],
        "ident_in": np.eye(P, dtype=np.float32),
        "block_in": np.kron(np.eye(P // S), np.ones((S, 1))).astype(np.float32),
        "w_kq": np.stack([chunked(by_dim(k_w)), chunked(by_dim(L0["q_w"]))], axis=1).reshape(P, 2, C, E),
        "w_vo": np.stack([chunked(v_w), chunked(L0["out_w"])], axis=1).reshape(P, 2, C, E),
        "w_up": chunked(L0["mlp_w1"]).reshape(P, C, FF),
        "w_down": chunked(L0["mlp_w2"]).reshape(P, FC, E),
        "w_maa1": chunked(L1["maa_w1"]).reshape(P, C, NF * DM),
        "w_maa2": L1["maa_w2"].reshape(NF * DM, E),
        "w_td1": chunked(L1["td_w1"]).reshape(P, C, DD),
        "w_td2": L1["td_w2"],
        "w_sq": np.stack([chunked(L1[n].T) for n in SQUARE], axis=1).reshape(P, len(SQUARE), C, E),
    }
    nc = bacc.Bacc("TRN2", target_bir_lowering=False, num_devices=1)
    arrays = {n: np.ascontiguousarray(a) for n, a in arrays.items()}
    args = {n: nc.dram_tensor(n, a.shape, mybir.dt.from_np(a.dtype), kind="ExternalInput").ap()
            for n, a in arrays.items()}
    out = nc.dram_tensor("out", (B, TQ, E), F32, kind="ExternalOutput").ap()
    build(nc, out=out, **args)
    r = run_bass_kernel_spmd(nc, [arrays], core_ids=[0])
    return r.results[0]["out"]
```

```python
from contextlib import ExitStack

import numpy as np

import concourse.bass as bass
from concourse import mybir

P = 128
F32 = mybir.dt.float32
BF16 = mybir.dt.bfloat16
I32 = mybir.dt.int32
ALU = mybir.AluOpType
ACT = mybir.ActivationFunctionType
AX = mybir.AxisListType

B, TQ, TC, E = 4, 256, 512, 256
NK = TC + TQ
NH, DH = 16, 16
C = E // P
NT = NK // P
QT = TQ // P
FF = 4 * E
FC = FF // P
H, S = 32, E // 32
DM, DD = 32, 64
NF = 5
HH = NH // 2
KPART = (0, 0, 1, 1, 0, 2)
QPART = (0, 1, 0, 1, 2, 0)
NB = len(KPART)
R_MASK, R_HI, R_LO = NB * DH, NB * DH + 1, NB * DH + 2
MASKED = -1.0e30
LEAD = 5
PAIRS = NH // 2
ST_BANKS = 3
UNITS_P = 6
VW = DH + 1

COLS = {}
_at = 0
for _n, _k in (("q_b", C), ("k_b", C), ("post_w", C), ("b1", FC), ("ln1_w", C), ("ln1_b", C), ("ln2_w", C),
               ("ln2_b", C), ("maa_x", C), ("stack", NF * C), ("decay", C), ("u", C), ("ffn_k", C), ("ffn_r", C),
               ("shift0", B * C * 2), ("state0", B * C * S), ("v_b", C)):
    COLS[_n] = (_at, _k)
    _at += _k
NCOLS = _at
ROWS = {n: i for i, n in enumerate(("out_b", "b2", "gn_w", "gn_b"))}
SQUARE = ("Wr", "Wk", "Wv", "Wg", "Wo", "Wfk", "Wfr", "Wfv")
MIX = {"k": 0, "w": 1, "v": 2, "r": 3, "g": 4}

TAIL = (("oT", "A"), ("proj", "D"), ("sq", "-"), ("rms", "-"), ("z", "-"), ("zT", "A"),
        ("up0", "D"), ("up1", "D"), ("up2", "D"), ("up3", "D"), ("gelu", "-"), ("down", "D"),
        ("stat1", "-"), ("root1", "-"), ("z2", "-"), ("xaT", "A"), ("sx", "-"), ("xin", "-"), ("maa1", "A"),
        ("mix_v", "D"), ("add_v", "-"), ("mix_k", "D"), ("add_k", "-"), ("v", "A"), ("mix_w", "D"), ("add_w", "-"),
        ("k", "A"), ("mix_r", "D"), ("add_r", "-"), ("td1", "A"), ("r", "A"), ("mix_g", "D"), ("add_g", "-"),
        ("td2", "A"), ("decay", "-"), ("ruk", "-"), ("g", "D"), ("kv0", "-"), ("diag", "D"), ("gate", "-"),
        ("scan00", "-"), ("kv1", "-"), ("scan01", "-"), ("dT", "A"), ("rs0", "-"),
        ("scan10", "-"), ("scan11", "-"), ("rs1", "-"),
        ("wkv", "A"), ("ojT", "D"), ("center", "-"), ("gsq", "-"), ("gvar", "-"), ("groot", "-"), ("gout", "-"),
        ("ogT", "A"), ("wo", "D"), ("stat2", "-"), ("root2", "-"), ("z3", "-"), ("xcT", "A"), ("sx2", "-"),
        ("xk", "-"), ("kk", "A"), ("kk2", "-"), ("xr", "-"), ("rr", "A"), ("fv", "D"), ("out", "-"))
KQ = ("kq00", "kq01", "kq10", "kq11")
VP = ("vp0", "vp1", "vp2")
READS_LAST = {n: who for n, who in TAIL if who != "-"}
READS_LAST.update({n: "D" for n in KQ + ("oq", "vb")}, **{n: "A" for n in VP + ("m",)})


def kq_steps(b):
    for n in KQ:
        yield ("unit", n, b)
        if n[3] == "1":
            yield ("split", int(n[2]), b)
    yield ("spill", b)


def schedule():
    for b in (0, 1):
        yield from kq_steps(b)
        for hf in ((0, 1) if b == 0 else (2,)):
            yield ("stack", hf)
        for n in VP:
            yield ("unit", n, b)
    yield ("unit", "vb", 0)
    pairs = B * PAIRS

    def maxima(tp):
        for i in range(4):
            yield [("max", 2 * tp + i // 2, i % 2)]
            if i == 3 and tp % 4 == 3:
                yield [("unit", "m", tp // 4)]

    for tp in range(LEAD):
        for piece in maxima(tp):
            yield from piece
    for b in range(B):
        attention = []
        for tp in range(b * PAIRS, (b + 1) * PAIRS):
            ms = list(maxima(tp + LEAD)) if tp + LEAD < pairs else [[], [], [], []]
            first = [("stack", tp // 4 + 2)] if tp % 4 == 0 and 1 <= tp // 4 < 2 * B - 2 else []
            for s in range(3):
                attention.append(first + ms[s])
                first = []
                attention.append([("exp", tp, s)])
                if s or tp:
                    attention.append([("pv",) + ((tp, s - 1) if s else (tp - 1, 2))])
                if s == 0 and tp and tp % 4 == 0:
                    attention[-1].append(("unit", "oq", tp // 4 - 1))
            attention.append([x for piece in ms[3:] for x in piece])
        other = []
        if b == 0:
            k2, k3 = list(kq_steps(2)), list(kq_steps(3))
            other = [[x] for x in k2] + [[]] * 6 + [[x] for x in k3]
        else:
            tail = [[("unit" if who != "-" else "post", n, b - 1)] for n, who in TAIL]
            if b + 1 < B:
                tail[2:2] = [[("unit", n, b + 1)] for n in VP]
            other = tail
        lead = 0 if b == 0 else 4
        for i, piece in enumerate(attention):
            yield from piece
            if i >= lead:
                lo, hi = ((i - lead + k) * len(other) // (len(attention) - lead) for k in (0, 1))
                for x in other[lo:hi]:
                    yield from x
    yield ("pv", pairs - 1, 2)
    yield ("unit", "oq", 2 * B - 1)
    for n, who in TAIL:
        yield ("unit" if who != "-" else "post", n, B - 1)


STEPS = list(schedule())
UNIT = {s[1:]: i for i, s in enumerate([s for s in STEPS if s[0] == "unit"])}
ORDER = sorted(UNIT, key=UNIT.get)


def last_read(i):
    who = READS_LAST[ORDER[i][0]]
    return who, sum(READS_LAST[n] == who for n, _ in ORDER[:i + 1])


def build(nc, hT, x, mask, cols, rows, ident_in, bsum_in, bfull_in, pick_in, w_kq, w_vo, w_up, w_down, w_maa1, w_maa2, w_td1, w_td2,
          w_sq, out):
    ctx = ExitStack()
    with ctx:
        def sb(name, shape, dt=F32):
            return ctx.enter_context(nc.sbuf_tensor(name, shape, dt))

        def sem(name):
            return ctx.enter_context(nc.semaphore(name))

        COL = sb("COL", [P, NCOLS])
        ROW = sb("ROW", [P, len(ROWS), E])
        ident = sb("ident", [P, P])
        identb = sb("identb", [P, P], BF16)
        bsum = sb("bsum", [P, C, H])
        bfull = sb("bfull", [P, P])
        pick = sb("pick", [P, 2 * 32])
        Wkq = sb("Wkq", [P, 2, C, E])
        Wvo = sb("Wvo", [P, 2, C, E])
        Wup = sb("Wup", [P, C, FF])
        Wdown = sb("Wdown", [P, FC, E])
        Wmaa1 = sb("Wmaa1", [P, C, NF * DM])
        Wmaa2 = sb("Wmaa2", [P, E])
        Wmaa2g = sb("Wmaa2g", [DM, E])
        Wtd1 = sb("Wtd1", [P, C, DD])
        Wtd2 = sb("Wtd2", [DD, E])
        Wsq = sb("Wsq", [P, len(SQUARE), C, E])
        half = sb("half", [P, QT])
        masks = sb("masks", [1, B, TC], I32)
        maskrow = sb("maskrow", [1, B, NK], BF16)

        hTs = [sb(f"hT{i}", [P, C, NK]) for i in range(2)]
        A = sb("A", [P, 2 * S * TQ + S * (TQ + 1)])
        kq = [A[:, c * (NK + TQ):(c + 1) * (NK + TQ)] for c in range(C)]
        at = C * (NK + TQ)
        parts = A[:, at:at + 3 * (NK + TQ)].bitcast(BF16).rearrange("p (k c n) -> p k c n", k=3, c=C)
        Kst = [sb(f"Kst{i}", [P, HH, NK], BF16) for i in range(3)]
        Qst = [sb(f"Qst{i}", [P, HH, TQ], BF16) for i in range(3)]
        Vn = [sb(f"Vn{i}", [P, NT * NH * VW + 32 - VW]) for i in range(2)]
        probs = [sb(f"probs{i}", [P, 2, TQ]) for i in range(UNITS_P)]
        mx = [sb(f"mx{i}", [P, QT, HH]) for i in range(2)]
        mhl = sb("mhl", [P, QT, 2, HH], BF16)
        mT = sb("mT", [2 * HH, TQ], BF16)
        oTs = sb("oTs", [P, 4, TQ])
        rsum = sb("rsum", [P, QT, HH])
        osb = sb("osb", [P, QT, E])

        xob = sb("xob", [P, QT, E])
        xb2 = sb("xb2", [P, QT, E])
        Z = sb("Z", [P, QT, E])
        T = sb("T", [P, C, TQ])
        XA = sb("XA", [P, C, 1 + TQ])
        SX = sb("SX", [P, C, TQ])
        KT = sb("KT", [P, C, TQ])
        RT = sb("RT", [P, C, TQ])
        WD = sb("WD", [P, C, TQ])
        VT = sb("VT", [P, C, TQ])
        G2 = sb("G2", [P, QT, E])
        TH = sb("TH", [P, QT, E])
        VN = XA[:, :, 0:TQ]
        RUK = T[:, :, :]
        KV = [A[:, c * S * TQ:(c + 1) * S * TQ].rearrange("p (j t) -> p j t", j=S)
              for c in range(C)]
        ST8 = A[:, C * S * TQ:]
        states = ST8.rearrange("p (j t) -> p j t", j=S)
        U = KV[0]
        stat = sb("stat", [P, QT, 6])
        mv = sb("mv", [P, QT, 2])
        ss = sb("ss", [P, QT])
        rstd = sb("rstd", [P, QT])
        gsum = sb("gsum", [P, QT * H])
        gvar = sb("gvar", [P, QT * H])
        gtmp = sb("gtmp", [P, QT * H])
        grstd = sb("grstd", [P, QT * H])

        def mixbuf(n):
            return ST8[:, n * C * TQ:(n + 1) * C * TQ].rearrange("p (c t) -> p c t", c=C)

        MIXBUF = {"v": 0, "k": 1, "w": 2, "r": 3, "g": 0}

        pMX = ctx.enter_context(nc.psum_tensor("pMX", [P, 1024], F32))
        pST = [ctx.enter_context(nc.psum_tensor(f"pST{i}", [P, 2, TQ], F32)) for i in range(ST_BANKS)]
        pO = ctx.enter_context(nc.psum_tensor("pO", [P, 512], F32))
        pW = [ctx.enter_context(nc.psum_tensor(f"pW{i}", [P, 512], F32)) for i in range(2)]

        skd = nc.dram_tensor("k_stack", (B, NB, DH, NH, NK), BF16, kind="Internal").ap()
        sqd = nc.dram_tensor("q_stack", (B, NB, DH, NH, TQ), BF16, kind="Internal").ap()
        svd = nc.dram_tensor("v_rows", (B, E, TQ), F32, kind="Internal").ap()

        unit_ready = sem("unit_ready")
        taken_by = {"A": sem("taken_by_act"), "D": sem("taken_by_dve")}
        hT_in = [sem(f"hT_in{i}") for i in range(2)]
        w_in = {n: sem(f"in_{n}") for n in ("kq", "vo", "const", "mask", "mlp", "maa", "sq")}
        const_ok = sem("const_ok")
        identb_ok = sem("identb_ok")
        rows_set = sem("rows_set")
        v_ones = sem("v_ones")
        mask_ok = sem("mask_ok")
        kq_hi = sem("kq_hi")
        kq_rem = sem("kq_rem")
        kq_mid = sem("kq_mid")
        kq_lo = sem("kq_lo")
        kq_out = sem("kq_out")
        stack_in = [sem(f"stack_in{i}") for i in range(3)]
        max_ready, max_done = sem("max_ready"), sem("max_done")
        m_split = sem("m_split")
        m_hi = sem("m_hi")
        m_in = [sem(f"m_in{i}") for i in range(2)]
        st_ready, exp_done = sem("st_ready"), sem("exp_done")
        pv_done = sem("pv_done")
        oT_taken = sem("oT_taken")
        rs_done = sem("rs_done")
        newton = sem("newton")
        x_in = sem("x_in")
        v_out, v_in = sem("v_out"), [sem(f"v_in{c}") for c in range(C)]
        out_done = sem("out_done")
        names = ("xob xb sq rr1 rs1 z gelu st1 mv1 rr2 rs2 z2 c0 sx xin mix_v mix_k mix_w mix_r mix_g wd rk ruk th wg "
                 "bg kv0 kv1 sc00 sc01 sc10 sc11 p0 p1 gs gc gq gv ge gr gw gg st2 mv2 rr3 rs3 z3 c1 sx2 xk xr kk fa "
                 "fo").split()
        did = {n: sem(f"did_{n}") for n in names}

        def col(name, i=0, n=1, p=P):
            return COL[0:p, COLS[name][0] + i:COLS[name][0] + i + n]

        def row(name, n=QT):
            return ROW[:, ROWS[name], :][:, None, :].to_broadcast([P, n, E])

        def tiles(ap):
            return ap.rearrange("p (a n) -> p a n", a=2)

        def taken(eng, name, b):
            who, n = last_read(UNIT[name, b])
            eng.wait_ge(taken_by[who], n)

        def ready(eng, name, b):
            eng.wait_ge(unit_ready, UNIT[name, b] + 1)
            return pW[UNIT[name, b] % 2]

        blk = ctx.enter_context(nc.Block())

        @blk.sync
        def _(sp):
            sp.dma_start(hTs[0][:], hT[0].rearrange("(c p) n -> p c n", p=P)).then_inc(hT_in[0], 16)
            sp.dma_start(Wkq[:], w_kq).then_inc(w_in["kq"], 16)
            sp.dma_start(masks[:], mask).then_inc(w_in["mask"], 16)
            sp.dma_start(hTs[1][:], hT[1].rearrange("(c p) n -> p c n", p=P)).then_inc(hT_in[1], 16)
            sp.dma_start(Wvo[:], w_vo).then_inc(w_in["vo"], 16)
            sp.dma_start(Wup[:], w_up).then_inc(w_in["mlp"], 16)
            sp.dma_start(Wdown[:], w_down).then_inc(w_in["mlp"], 16)
            sp.dma_start(Wmaa1[:], w_maa1).then_inc(w_in["maa"], 16)
            sp.dma_start(Wmaa2[:], w_maa2[0:P, :]).then_inc(w_in["maa"], 16)
            sp.dma_start(Wmaa2g[:], w_maa2[P:P + DM, :]).then_inc(w_in["maa"], 16)
            sp.dma_start(Wtd1[:], w_td1).then_inc(w_in["maa"], 16)
            sp.dma_start(Wtd2[:], w_td2).then_inc(w_in["maa"], 16)
            sp.dma_start(Wsq[:], w_sq).then_inc(w_in["sq"], 16)
            for step in STEPS:
                kind = step[0]
                if kind == "spill":
                    b = step[1]
                    sp.wait_ge(kq_lo, C * (b + 1))
                    for k in range(NB):
                        sp.dma_start(skd[b, k].rearrange("d (h c) n -> (d h) c n", c=C),
                                     parts[:, KPART[k], :, 0:NK]).then_inc(kq_out, 16)
                        sp.dma_start(sqd[b, k].rearrange("d (h c) n -> (d h) c n", c=C),
                                     parts[:, QPART[k], :, NK:NK + TQ]).then_inc(kq_out, 16)
                elif kind == "stack":
                    hf = step[1]
                    b, part = divmod(hf, 2)
                    s = hf % 3
                    sp.wait_ge(kq_out, 2 * NB * 16 * (b + 1))
                    if hf >= 3:
                        sp.wait_ge(st_ready, 24 * (hf - 2))
                    else:
                        sp.wait_ge(rows_set, hf + 1)
                    sp.wait_ge(mask_ok, 1)
                    sp.dma_start(Kst[s][0:NB * DH], skd[b].rearrange("k d h n -> (k d) h n")[:, part * HH:(part + 1) * HH])\
                        .then_inc(stack_in[s], 16)
                    sp.dma_start(Qst[s][0:NB * DH], sqd[b].rearrange("k d h n -> (k d) h n")[:, part * HH:(part + 1) * HH])\
                        .then_inc(stack_in[s], 16)
                    sp.dma_start(Kst[s][R_MASK:R_MASK + 1],
                                 maskrow[0:1, b, :][:, None, :].to_broadcast([1, HH, NK])).then_inc(stack_in[s], 16)
                elif kind == "unit" and step[1] == "vp2" and step[2] + 2 < B:
                    b = step[2]
                    ready(sp, "vp2", b)
                    sp.dma_start(hTs[b % 2][:], hT[b + 2].rearrange("(c p) n -> p c n", p=P)).then_inc(hT_in[b % 2], 16)
                elif kind == "unit" and step[1] == "m":
                    hf = step[2]
                    s = hf % 3
                    taken(sp, "m", hf)
                    for part, r in ((0, R_HI), (1, R_LO)):
                        sp.dma_start(Qst[s][r:r + 1, :, :], mT[part * HH:(part + 1) * HH, :]).then_inc(m_in[hf % 2], 16)
                elif kind == "unit" and step[1] == "oq" and step[2] % 2 == 1:
                    b = step[2] // 2
                    if b >= 1:
                        sp.wait_ge(did["fo"], b)
                    sp.dma_start(xb2[:], x[b].rearrange("(a p) n -> p a n", p=P)).then_inc(x_in, 16)
                elif kind == "unit" and step[1] == "v":
                    b = step[2]
                    taken(sp, "v", b)
                    sp.dma_start(svd[b].rearrange("(c p) t -> p c t", p=P), VT[:]).then_inc(v_out, 16)
                    sp.wait_ge(v_out, 16 * (b + 1))
                    if b == 0:
                        sp.wait_ge(kq_out, 2 * NB * 16 * B)
                    taken(sp, "down", b)
                    for c in range(C):
                        src = svd[b].rearrange("(c h j) t -> c h (j t)", c=C, j=S)[c]
                        sp.dma_start(KV[c].rearrange("p j t -> p (j t)"),
                                     src[:, None, :].to_broadcast([P // S, S, S * TQ])).then_inc(v_in[c], 16)
                elif kind == "post" and step[1] == "out":
                    b = step[2]
                    sp.wait_ge(did["fo"], b + 1)
                    sp.dma_start(out[b].rearrange("(a p) n -> p a n", p=P), Z[:]).then_inc(out_done, 16)
            sp.wait_ge(out_done, 16 * B)
            sp.wait_ge(kq_out, 2 * NB * 16 * B)
            sp.wait_ge(v_out, 16 * B)

        @blk.tensor
        def _(pe):
            mm = nc.tensor.matmul

            def claim(name, b):
                i = UNIT[name, b]
                if i >= 2:
                    who, n = last_read(i - 2)
                    pe.wait_ge(taken_by[who], n)
                return pW[i % 2]

            def square(name, b, w, rhs_t, token_major):
                bk = claim(name, b)
                for m in range(2):
                    for c in range(C):
                        if token_major:
                            lhs, rhs = rhs_t[:, c, m * P:(m + 1) * P], w[:, c, :]
                        else:
                            lhs, rhs = w[:, c, m * P:(m + 1) * P], rhs_t[:, c, :]
                        last = mm(bk[:, m * 256:(m + 1) * 256], lhs, rhs, start=c == 0, stop=c == C - 1)
                last.then_inc(unit_ready, 1)

            def transposes(name, b, src):
                bk = claim(name, b)
                for c in range(C):
                    for a in range(QT):
                        last = nc.tensor.transpose(bk[:, c * TQ + a * P:c * TQ + (a + 1) * P],
                                                   src[:, a, c * P:(c + 1) * P], ident[:])
                last.then_inc(unit_ready, 1)

            pe.wait_ge(w_in["kq"], 16)
            for step in STEPS:
                kind = step[0]
                if kind == "max":
                    _, t, qt = step
                    n = t * QT + qt
                    hf, h = divmod(t, HH)
                    s = hf % 3
                    if h == 0 and qt == 0:
                        pe.wait_ge(stack_in[s], 48 * (hf // 3 + 1))
                    if n >= 1:
                        pe.wait_ge(max_done, n)
                    lhs = Qst[s][0:R_MASK + 1, h, qt * P:(qt + 1) * P]
                    mm(pMX[:, 0:512], lhs, Kst[s][0:R_MASK + 1, h, 0:512], start=True, stop=True)
                    mm(pMX[:, 512:NK], lhs, Kst[s][0:R_MASK + 1, h, 512:NK], start=True, stop=True)\
                        .then_inc(max_ready, 1)
                elif kind == "exp":
                    _, tp, stage = step
                    hf = tp // 4
                    s = hf % 3
                    if tp % 4 == 0 and stage == 0:
                        pe.wait_ge(m_in[hf % 2], 32 * (hf // 2 + 1))
                    for hh in range(2):
                        n = 2 * (3 * tp + stage) + hh
                        h = (2 * tp + hh) % HH
                        if n >= ST_BANKS:
                            pe.wait_ge(exp_done, n - ST_BANKS + 1)
                        for i in range(2):
                            nt = 2 * stage + i
                            last = mm(pST[n % ST_BANKS][:, i, :], Kst[s][0:R_LO + 1, h, nt * P:(nt + 1) * P],
                                      Qst[s][0:R_LO + 1, h, :], start=True, stop=True)
                        last.then_inc(st_ready, 1)
                elif kind == "pv":
                    _, tp, stage = step
                    b, pair = divmod(tp, PAIRS)
                    if pair == 0 and stage == 0:
                        taken(pe, "vp2", b)
                        if b == 0:
                            pe.wait_ge(v_ones, 1)
                    if stage == 0 and tp:
                        pe.wait_ge(oT_taken, tp)
                    n = 2 * (3 * tp + stage)
                    pe.wait_ge(exp_done, n + 2)
                    for hh in range(2):
                        for i in range(2):
                            at = ((2 * stage + i) * NH + 2 * pair + hh) * VW
                            j = 2 * hh + i
                            last = mm(pO[32 * j:32 * j + 32, 0:TQ], Vn[b % 2][:, at:at + 32],
                                      probs[(n + hh) % UNITS_P][:, i, :], start=stage == 0, stop=stage == 2)
                    last.then_inc(pv_done, 1)
                elif kind == "unit":
                    _, name, b = step
                    if name[:2] == "kq":
                        c, piece = int(name[2]), int(name[3])
                        hb = hTs[b % 2]
                        if c == 0 and piece == 0:
                            pe.wait_ge(hT_in[b % 2], 16 * (b // 2 + 1))
                        bk = claim(name, b)
                        jobs = ((0, 0, 512, 0),) if piece == 0 else ((0, 512, NK, 0), (1, TC, NK, 256))
                        for w, lo, hi, at in jobs:
                            for kc in range(C):
                                last = mm(bk[:, at:at + hi - lo], Wkq[:, w, kc, c * P:(c + 1) * P], hb[:, kc, lo:hi],
                                          start=kc == 0, stop=kc == C - 1)
                        last.then_inc(unit_ready, 1)
                    elif name[:2] == "vp":
                        hb = hTs[b % 2]
                        if b == 0 and name == "vp0":
                            pe.wait_ge(w_in["vo"], 16)
                        bk = claim(name, b)
                        for i in range(2):
                            nt = 2 * int(name[2]) + i
                            for kc in range(C):
                                last = mm(bk[:, i * E:(i + 1) * E], hb[:, kc, nt * P:(nt + 1) * P], Wvo[:, 0, kc, :],
                                          start=kc == 0, stop=kc == C - 1)
                        last.then_inc(unit_ready, 1)
                    elif name == "m":
                        pe.wait_ge(m_split, b + 1)
                        if b == 0:
                            pe.wait_ge(identb_ok, 1)
                        bk = claim(name, b)[:, :].bitcast(BF16)
                        for qt in range(QT):
                            last = nc.tensor.transpose(bk[0:2 * HH, qt * P:(qt + 1) * P],
                                                       mhl[:, qt, :, :].rearrange("p l h -> p (l h)"), identb[:])
                        last.then_inc(unit_ready, 1)
                    elif name == "vb":
                        pe.wait_ge(w_in["vo"], 16)
                        pe.wait_ge(w_in["const"], 96)
                        bk = claim(name, b)
                        for c in range(C):
                            last = mm(bk[:, 0:E], col("v_b", c).to_broadcast([P, P]), Wvo[:, 1, c, :],
                                      start=c == 0, stop=c == C - 1)
                        last.then_inc(unit_ready, 1)
                    elif name == "oq":
                        hf = b
                        pe.wait_ge(oT_taken, 4 * (hf + 1))
                        bk = claim(name, hf)
                        for qt in range(QT):
                            for p in range(4):
                                at = (qt * 4 + p) * 64
                                last = mm(bk[:, at:at + 64], oTs[:, p, qt * P:(qt + 1) * P], pick[:],
                                          start=True, stop=True)
                        last.then_inc(unit_ready, 1)
                    elif name == "oT":
                        taken(pe, "oq", 2 * b + 1)
                        transposes(name, b, osb)
                    elif name == "proj":
                        taken(pe, "oT", b)
                        square(name, b, Wvo[:, 1], T, True)
                    elif name == "zT":
                        pe.wait_ge(did["z"], b + 1)
                        transposes(name, b, Z)
                    elif name[:2] == "up":
                        if name == "up0":
                            taken(pe, "zT", b)
                            if b == 0:
                                pe.wait_ge(w_in["mlp"], 32)
                        bk = claim(name, b)
                        for i in range(2):
                            f = 2 * int(name[2]) + i
                            for c in range(C):
                                last = mm(bk[:, i * TQ:(i + 1) * TQ], Wup[:, c, f * P:(f + 1) * P], T[:, c, :],
                                          start=c == 0, stop=c == C - 1)
                        last.then_inc(unit_ready, 1)
                    elif name == "down":
                        pe.wait_ge(did["gelu"], b + 1)
                        bk = claim(name, b)
                        for a in range(QT):
                            for f in range(FC):
                                last = mm(bk[:, a * E:(a + 1) * E], U[:, f, a * P:(a + 1) * P], Wdown[:, f, :],
                                          start=f == 0, stop=f == FC - 1)
                        last.then_inc(unit_ready, 1)
                    elif name == "xaT":
                        pe.wait_ge(did["z2"], b + 1)
                        transposes(name, b, Z)
                    elif name == "maa1":
                        pe.wait_ge(did["xin"], b + 1)
                        if b == 0:
                            pe.wait_ge(w_in["maa"], 80)
                        bk = claim(name, b)
                        for c in range(C):
                            mm(bk[:, 0:TQ], Wmaa1[:, c, 0:P], T[:, c, :], start=c == 0, stop=c == C - 1)
                        for c in range(C):
                            last = mm(bk[0:DM, TQ:2 * TQ], Wmaa1[:, c, P:NF * DM], T[:, c, :],
                                      start=c == 0, stop=c == C - 1)
                        last.then_inc(unit_ready, 1)
                    elif name[:4] == "mix_":
                        f = MIX[name[4]]
                        taken(pe, "maa1", b)
                        bk = claim(name, b)
                        for c in range(C):
                            if f < 4:
                                lhs, rhs = Wmaa2[f * DM:(f + 1) * DM, c * P:(c + 1) * P], xob[f * DM:(f + 1) * DM, 0, :]
                            else:
                                lhs, rhs = Wmaa2g[:, c * P:(c + 1) * P], xob[0:DM, 1, :]
                            last = mm(bk[:, c * TQ:(c + 1) * TQ], lhs, rhs, start=True, stop=True)
                        last.then_inc(unit_ready, 1)
                    elif name in ("v", "k", "r", "g"):
                        if b == 0 and name == "v":
                            pe.wait_ge(w_in["sq"], 16)
                        pe.wait_ge(did["mix_" + name], b + 1)
                        square(name, b, Wsq[:, SQUARE.index("W" + name)], mixbuf(MIXBUF[name]), name == "g")
                    elif name == "td1":
                        pe.wait_ge(did["mix_w"], b + 1)
                        bk = claim(name, b)
                        for c in range(C):
                            last = mm(bk[0:DD, 0:TQ], Wtd1[:, c, :], mixbuf(MIXBUF["w"])[:, c, :],
                                      start=c == 0, stop=c == C - 1)
                        last.then_inc(unit_ready, 1)
                    elif name == "td2":
                        taken(pe, "td1", b)
                        bk = claim(name, b)
                        for c in range(C):
                            last = mm(bk[:, c * TQ:(c + 1) * TQ], Wtd2[:, c * P:(c + 1) * P], TH[0:DD, 0, :],
                                      start=True, stop=True)
                        last.then_inc(unit_ready, 1)
                    elif name == "dT":
                        taken(pe, "diag", b)
                        bk = claim(name, b)
                        for a in range(QT):
                            for c in range(C):
                                last = nc.tensor.transpose(bk[:, a * E + c * P:a * E + (c + 1) * P],
                                                           VT[:, c, a * P:(a + 1) * P], ident[:])
                        last.then_inc(unit_ready, 1)
                    elif name == "diag":
                        pe.wait_ge(did["ruk"], b + 1)
                        bk = claim(name, b)
                        for c in range(C):
                            last = mm(bk[:, c * TQ:(c + 1) * TQ], bfull[:], RUK[:, c, :], start=True, stop=True)
                        last.then_inc(unit_ready, 1)
                    elif name == "wkv":
                        pe.wait_ge(did["p0"], b + 1)
                        pe.wait_ge(did["p1"], b + 1)
                        bk = claim(name, b)
                        for jj in range(S // 4):
                            for c in range(C):
                                for j4 in range(4):
                                    last = mm(bk[32 * j4:32 * j4 + 32, jj * TQ:(jj + 1) * TQ], bsum[:, c, :],
                                              KV[c][:, 4 * jj + j4, :], start=c == 0, stop=c == C - 1)
                        last.then_inc(unit_ready, 1)
                    elif name == "ojT":
                        taken(pe, "wkv", b)
                        bk = claim(name, b)
                        for a in range(QT):
                            for jj in range(S // 4):
                                at = a * E + jj * P
                                last = nc.tensor.transpose(bk[:, at:at + P], T[:, jj, a * P:(a + 1) * P], ident[:])
                        last.then_inc(unit_ready, 1)
                    elif name == "ogT":
                        pe.wait_ge(did["gg"], b + 1)
                        transposes(name, b, SX)
                    elif name == "wo":
                        taken(pe, "ogT", b)
                        square(name, b, Wsq[:, SQUARE.index("Wo")], T, True)
                    elif name == "xcT":
                        pe.wait_ge(did["z3"], b + 1)
                        transposes(name, b, Z)
                    elif name == "rr":
                        pe.wait_ge(did["xr"], b + 1)
                        square(name, b, Wsq[:, SQUARE.index("Wfr")], RT, True)
                    elif name == "kk":
                        pe.wait_ge(did["xk"], b + 1)
                        square(name, b, Wsq[:, SQUARE.index("Wfk")], KT, False)
                    elif name == "fv":
                        pe.wait_ge(did["kk"], b + 1)
                        square(name, b, Wsq[:, SQUARE.index("Wfv")], VT, True)

        @blk.scalar
        def _(act):
            act_fn = nc.scalar.activation
            act.dma_start(COL[:], cols).then_inc(w_in["const"], 16)
            for dst, src in ((ident, ident_in), (bsum, bsum_in), (bfull, bfull_in), (pick, pick_in)):
                act.dma_start(dst[:], src).then_inc(w_in["const"], 16)
            act.dma_start(ROW[:, :, :].rearrange("p r n -> p (r n)"), rows.to_broadcast([P, len(ROWS) * E]))\
                .then_inc(w_in["const"], 16)
            act.wait_ge(w_in["const"], 96)
            for step in STEPS:
                kind = step[0]
                if kind == "exp":
                    _, tp, stage = step
                    if tp >= 1:
                        act.wait_ge(pv_done, 3 * (tp - 1) + stage + 1)
                    for hh in range(2):
                        n = 2 * (3 * tp + stage) + hh
                        act.wait_ge(st_ready, n + 1)
                        act_fn(probs[n % UNITS_P][:], pST[n % ST_BANKS][:], ACT.Exp).then_inc(exp_done, 1)
                    continue
                if kind == "pv" and step[2] == 2:
                    tp = step[1]
                    act.wait_ge(pv_done, 3 * tp + 3)
                    if tp >= 4 and tp % 4 == 0:
                        ready(act, "oq", tp // 4 - 1)
                    act_fn(oTs[:, tp % 4, :], pO[:, 0:TQ], ACT.Copy).then_inc(oT_taken, 1)
                    continue
                if kind == "split":
                    _, c, b = step
                    n = C * b + c
                    taken(act, f"kq{c}1", b)
                    if b >= 1:
                        act.wait_ge(kq_out, 2 * NB * 16 * b)
                    act_fn(parts[:, 0, c, :], kq[c], ACT.Copy).then_inc(kq_hi, 1)
                    act.wait_ge(kq_rem, n + 1)
                    act_fn(parts[:, 1, c, :], kq[c], ACT.Copy).then_inc(kq_mid, 1)
                    continue
                if kind not in ("unit", "post"):
                    continue
                _, name, b = step
                if name == "sq":
                    taken(act, "proj", b)
                    if b >= 1:
                        act.wait_ge(out_done, 16 * b)
                    for a in range(QT):
                        last = act_fn(Z[:, a, :], xob[:, a, :], ACT.Square, accum_out=ss[:, a:a + 1])
                    last.then_inc(did["sq"], 1)
                elif name == "gelu":
                    taken(act, "up3", b)
                    act_fn(U, U, ACT.Gelu_apprx_tanh).then_inc(did["gelu"], 1)
                elif name == "gsq":
                    act.wait_ge(did["gc"], b + 1)
                    act_fn(T[:, :, :], SX[:, :, :], ACT.Square).then_inc(did["gq"], 1)
                elif name == "decay":
                    taken(act, "td2", b)
                    act_fn(WD[:], WD[:], ACT.Exp, scale=-1.0).then_inc(did["wd"], 1)
                elif name == "g":
                    bk = ready(act, name, b)
                    act_fn(TH[:], tiles(bk[:]), ACT.Tanh, scale=0.5).then_inc(did["th"], 1)
                elif READS_LAST.get(name) == "A":
                    bk = ready(act, name, b)
                    view = tiles(bk[:])
                    if name[:2] == "vp":
                        i = int(name[2])
                        if b == 0 and i == 0:
                            act.wait_ge(v_ones, 1)
                        if b >= 2 and i == 0:
                            act.wait_ge(pv_done, 3 * PAIRS * (b - 1))
                        at = 2 * i * NH * VW
                        vn = Vn[b % 2][:, at:at + 2 * NH * VW].rearrange("p (a h d) -> p a h d", a=2, h=NH)
                        last = act_fn(vn[:, :, :, 0:DH],
                                 bk[:, :].rearrange("p (a h d) -> p a h d", a=2, h=NH), ACT.Copy)
                    elif name == "m":
                        if b >= 1:
                            act.wait_ge(m_in[(b - 1) % 2], 32 * ((b - 1) // 2 + 1))
                        last = act_fn(mT[:], bk[:, :].bitcast(BF16)[0:2 * HH, 0:TQ], ACT.Copy)
                    elif name == "ogT":
                        last = act_fn(T[:], view, ACT.Copy, scale=0.5)
                    elif name == "zT":
                        for c in range(C):
                            last = act_fn(T[:, c, :], view[:, c, :], ACT.Copy, scale=col("post_w", c))
                    elif name in ("xaT", "xcT"):
                        ln = "ln1" if name == "xaT" else "ln2"
                        for c in range(C):
                            last = act_fn(XA[:, c, 1:1 + TQ], view[:, c, :], ACT.Identity,
                                     bias=col(ln + "_b", c), scale=col(ln + "_w", c))
                    elif name == "maa1":
                        act_fn(xob[:, 0, :], bk[:, 0:TQ], ACT.Tanh)
                        last = act_fn(xob[0:DM, 1, :], bk[0:DM, TQ:2 * TQ], ACT.Tanh)
                    elif name == "td1":
                        last = act_fn(TH[0:DD, 0, :], bk[0:DD, 0:TQ], ACT.Tanh)
                    elif name == "td2":
                        for c in range(C):
                            last = act_fn(WD[:, c, :], view[:, c, :], ACT.Exp, bias=col("decay", c))
                    elif name == "rr":
                        last = act_fn(TH[:], view, ACT.Tanh, scale=0.5)
                    elif name == "kk":
                        last = act_fn(WD[:], view, ACT.Relu)
                    else:
                        if name == "dT":
                            act.wait_ge(did["mix_g"], b + 1)
                        dst = {"oT": T, "v": VT, "k": KT, "r": RT, "dT": VN, "wkv": T}[name]
                        last = act_fn(dst[:, :, :], view, ACT.Copy)
                    last.then_inc(taken_by["A"], 1)

        @blk.gpsimd
        def _(pool):
            g = nc.gpsimd
            ones2 = float(np.array([0x3F803F80], np.uint32).view(np.float32)[0])
            for s in range(3):
                g.memset(Kst[s][R_MASK:R_LO + 1].rearrange("p h n -> p (h n)").bitcast(F32), ones2)
                g.memset(Qst[s][R_MASK:R_LO + 1].rearrange("p h n -> p (h n)").bitcast(F32), ones2)\
                 .then_inc(rows_set, 1)
                pool.wait_ge(rows_set, s + 1)
            for i in range(2):
                g.memset(Vn[i][:, NT * NH * VW:], 0.0)
                last = g.memset(Vn[i][:, DH:NT * NH * VW:VW], 1.0)
            last.then_inc(v_ones, 1)
            g.memset(half[:], -0.5).then_inc(const_ok, 1)
            pool.wait_ge(const_ok, 1)

            def root(src, scale, eps, first, second, b):
                g.tensor_scalar(rstd[:], src, scale, eps, ALU.mult, ALU.add).then_inc(did[first], 1)
                pool.wait_ge(did[first], b + 1)
                g.tensor_tensor(rstd[:], rstd[:], half[:], ALU.pow).then_inc(did[second], 1)

            for step in STEPS:
                kind = step[0]
                if kind == "split":
                    _, c, b = step
                    pool.wait_ge(kq_mid, C * b + c + 1)
                    g.tensor_tensor(parts[:, 2, c, :], kq[c], parts[:, 1, c, :], ALU.subtract).then_inc(kq_lo, 1)
                    continue
                if kind not in ("unit", "post"):
                    continue
                _, name, b = step
                if name == "oq" and b % 2 == 1:
                    b = b // 2
                    if b == 0:
                        taken(pool, "vb", 0)
                    pool.wait_ge(x_in, 16 * (b + 1))
                    g.tensor_tensor(xob[:], xb2[:], row("out_b"), ALU.add).then_inc(did["xob"], 1)
                    pool.wait_ge(did["xob"], b + 1)
                    g.tensor_tensor(xb2[:], xb2[:], row("b2"), ALU.add).then_inc(did["xb"], 1)
                elif name == "rms":
                    pool.wait_ge(did["sq"], b + 1)
                    root(ss[:], 1.0 / E, 1e-6, "rr1", "rs1", b)
                elif name == "root1":
                    pool.wait_ge(did["mv1"], b + 1)
                    root(mv[:, :, 1], 1.0, 1e-5, "rr2", "rs2", b)
                elif name == "root2":
                    pool.wait_ge(did["mv2"], b + 1)
                    root(mv[:, :, 1], 1.0, 1e-5, "rr3", "rs3", b)
                elif name in ("xaT", "xcT"):
                    first = name == "xaT"
                    at = COLS["shift0"][0] + b * C * 2
                    prev = COL[:, at:at + 2 * C].rearrange("p (c k) -> p c k", c=C)[:, :, 1 if first else 0]
                    pool.wait_ge(did["z2" if first else "z3"], b + 1)
                    g.tensor_copy(XA[:, :, 0], prev).then_inc(did["c0" if first else "c1"], 1)
                elif name in ("sx", "sx2"):
                    first = name == "sx"
                    taken(pool, "xaT" if first else "xcT", b)
                    pool.wait_ge(did["c0" if first else "c1"], b + 1)
                    g.tensor_tensor(SX[:], XA[:, :, 0:TQ], XA[:, :, 1:1 + TQ], ALU.subtract).then_inc(did[name], 1)
                elif name[:4] == "add_":
                    taken(pool, "mix_" + name[4], b)
                    mb = mixbuf(MIXBUF[name[4]])
                    g.tensor_tensor(mb, mb, XA[:, :, 1:1 + TQ], ALU.add).then_inc(did["mix_" + name[4]], 1)
                elif name == "ruk":
                    taken(pool, "r", b)
                    g.tensor_tensor(RUK, RT[:], KT[:], ALU.mult).then_inc(did["rk"], 1)
                    pool.wait_ge(did["rk"], b + 1)
                    for c in range(C):
                        last = g.tensor_scalar(RUK[:, c, :], RUK[:, c, :], col("u", c), None, ALU.mult)
                    last.then_inc(did["ruk"], 1)
                elif name in ("kv0", "kv1"):
                    c = int(name[2])
                    pool.wait_ge(v_in[c], 16 * (b + 1))
                    taken(pool, "k", b)
                    g.tensor_tensor(KV[c], KV[c], KT[:, c, :][:, None, :].to_broadcast([P, S, TQ]), ALU.mult)\
                     .then_inc(did[name], 1)
                elif name == "gate":
                    taken(pool, "g", b)
                    g.tensor_tensor(TH[:], G2[:], row("gn_w"), ALU.mult).then_inc(did["wg"], 1)
                    pool.wait_ge(did["wg"], b + 1)
                    g.tensor_tensor(G2[:], G2[:], row("gn_b"), ALU.mult).then_inc(did["bg"], 1)
                elif name == "kk2":
                    taken(pool, "kk", b)
                    g.tensor_tensor(VT[:], WD[:], WD[:], ALU.mult).then_inc(did["kk"], 1)

        @blk.vector
        def _(dve):
            v = nc.vector
            dve.wait_ge(w_in["mask"], 16)
            v.tensor_scalar(maskrow[:, :, 0:TC], masks[:], 0, MASKED, ALU.is_equal, ALU.mult)
            v.memset(maskrow[:, :, TC:NK], 0.0).then_inc(mask_ok, 1)
            dve.wait_ge(w_in["const"], 96)
            v.tensor_copy(identb[:], ident[:]).then_inc(identb_ok, 1)

            def moments(x_, b, st, m):
                for a in range(QT):
                    last = v.bn_stats(stat[:, a, :], x_[:, a, :])
                last.then_inc(did[st], 1)
                dve.wait_ge(did[st], b + 1)
                for a in range(QT):
                    last = v.bn_aggr(mv[:, a, :], stat[:, a, :])
                last.then_inc(did[m], 1)

            def scan(c, first, b, done):
                at = COLS["state0"][0] + (b * C + c) * S
                js = range(first, first + S // 2)
                v.tensor_copy(states[:, first:first + S // 2, 0], COL[:, at + first:at + first + S // 2])
                for j in js:
                    last = v.tensor_tensor_scan(states[:, j, 1:1 + TQ], WD[:, c, :], KV[c][:, j, :],
                                                COL[:, at + j:at + j + 1], ALU.mult, ALU.add)
                last.then_inc(did[done], 1)

            def reciprocal_root(b):
                n = 10 * b
                v.tensor_scalar(gtmp[:].bitcast(I32), gvar[:].bitcast(I32), 1, None, ALU.logical_shift_right)\
                 .then_inc(newton, 1)
                dve.wait_ge(newton, n + 1)
                v.tensor_scalar(grstd[:].bitcast(I32), gtmp[:].bitcast(I32), -1.0, float(0x5F3759DF),
                                ALU.mult, ALU.add).then_inc(newton, 1)
                for i in range(3):
                    dve.wait_ge(newton, n + 3 * i + 2)
                    v.tensor_tensor(gtmp[:], grstd[:], grstd[:], ALU.mult).then_inc(newton, 1)
                    dve.wait_ge(newton, n + 3 * i + 3)
                    v.scalar_tensor_tensor(gtmp[:], gtmp[:], -0.5, gvar[:], ALU.mult, ALU.mult).then_inc(newton, 1)
                    dve.wait_ge(newton, n + 3 * i + 4)
                    last = v.scalar_tensor_tensor(grstd[:], gtmp[:], 1.5, grstd[:], ALU.add, ALU.mult)
                    if i < 2:
                        last.then_inc(newton, 1)
                return last

            for step in STEPS:
                kind = step[0]
                if kind == "max":
                    _, t, qt = step
                    hf, h = divmod(t, HH)
                    dve.wait_ge(max_ready, t * QT + qt + 1)
                    v.tensor_reduce(mx[hf % 2][:, qt, h:h + 1], pMX[:, 0:NK], AX.X, ALU.max).then_inc(max_done, 1)
                elif kind == "split":
                    _, c, b = step
                    n = C * b + c
                    dve.wait_ge(kq_hi, n + 1)
                    v.tensor_tensor(kq[c], kq[c], parts[:, 0, c, :], ALU.subtract).then_inc(kq_rem, 1)
                elif kind == "post":
                    _, name, b = step
                    if name == "z":
                        dve.wait_ge(did["rs1"], b + 1)
                        for a in range(QT):
                            last = v.tensor_scalar(Z[:, a, :], xob[:, a, :], rstd[:, a:a + 1], None, ALU.mult)
                        last.then_inc(did["z"], 1)
                    elif name in ("stat1", "stat2"):
                        first = name == "stat1"
                        taken(dve, "down" if first else "wo", b)
                        moments(xb2 if first else xob, b, "st1" if first else "st2", "mv1" if first else "mv2")
                    elif name in ("z2", "z3"):
                        src = xb2 if name == "z2" else xob
                        dve.wait_ge(did["rs2" if name == "z2" else "rs3"], b + 1)
                        for a in range(QT):
                            last = v.tensor_scalar(Z[:, a, :], src[:, a, :], mv[:, a, 0:1], rstd[:, a:a + 1],
                                                   ALU.subtract, ALU.mult)
                        last.then_inc(did[name], 1)
                    elif name == "xin":
                        dve.wait_ge(did["sx"], b + 1)
                        for c in range(C):
                            last = v.scalar_tensor_tensor(T[:, c, :], SX[:, c, :], col("maa_x", c), XA[:, c, 1:1 + TQ],
                                                          ALU.mult, ALU.add)
                        last.then_inc(did["xin"], 1)
                    elif name in ("xk", "xr"):
                        dst = KT if name == "xk" else RT
                        dve.wait_ge(did["sx2"], b + 1)
                        for c in range(C):
                            last = v.scalar_tensor_tensor(dst[:, c, :], SX[:, c, :], col("ffn_" + name[1], c),
                                                          XA[:, c, 1:1 + TQ], ALU.mult, ALU.add)
                        last.then_inc(did[name], 1)
                    elif name[:4] == "scan":
                        c, part = int(name[4]), int(name[5])
                        if part == 0:
                            dve.wait_ge(did["wd"], b + 1)
                            dve.wait_ge(did[f"kv{c}"], b + 1)
                            if c == 1:
                                dve.wait_ge(did["p0"], b + 1)
                        scan(c, part * S // 2, b, "sc" + name[4:])
                    elif name in ("rs0", "rs1"):
                        c = int(name[2])
                        dve.wait_ge(did[f"sc{c}1"], b + 1)
                        v.tensor_tensor(KV[c], states[:, :, 0:TQ], RT[:, c, :][:, None, :].to_broadcast([P, S, TQ]),
                                        ALU.mult).then_inc(did[f"p{c}"], 1)
                    elif name == "center":
                        o3 = SX[:, :, :].rearrange("p a (h j) -> p (a h) j", j=S)
                        taken(dve, "ojT", b)
                        v.tensor_reduce(gsum[:], o3, AX.X, ALU.add).then_inc(did["gs"], 1)
                        dve.wait_ge(did["gs"], b + 1)
                        v.scalar_tensor_tensor(o3, gsum[:, :, None].to_broadcast([P, QT * H, S]), -1.0 / S, o3,
                                               ALU.mult, ALU.add).then_inc(did["gc"], 1)
                    elif name == "gvar":
                        dve.wait_ge(did["gq"], b + 1)
                        v.tensor_reduce(gvar[:], T[:, :, :].rearrange("p a (h j) -> p (a h) j", j=S), AX.X, ALU.add)\
                         .then_inc(did["gv"], 1)
                        dve.wait_ge(did["gv"], b + 1)
                        v.tensor_scalar(gvar[:], gvar[:], 1.0 / S, 1e-5, ALU.mult, ALU.add).then_inc(did["ge"], 1)
                    elif name == "groot":
                        dve.wait_ge(did["ge"], b + 1)
                        reciprocal_root(b).then_inc(did["gr"], 1)
                    elif name == "gout":
                        o3 = SX[:, :, :].rearrange("p a (h j) -> p (a h) j", j=S)
                        dve.wait_ge(did["gr"], b + 1)
                        v.tensor_tensor(o3, o3, grstd[:, :, None].to_broadcast([P, QT * H, S]), ALU.mult)\
                         .then_inc(did["gw"], 1)
                        dve.wait_ge(did["gw"], b + 1)
                        dve.wait_ge(did["bg"], b + 1)
                        v.tensor_tensor(SX[:], SX[:], TH[:], ALU.mult).then_inc(did["fa"], 1)
                        dve.wait_ge(did["fa"], b + 1)
                        v.tensor_tensor(SX[:], SX[:], G2[:], ALU.add).then_inc(did["gg"], 1)
                    elif name == "out":
                        taken(dve, "fv", b)
                        v.scalar_tensor_tensor(Z[:], G2[:], 0.5, xob[:], ALU.mult, ALU.add).then_inc(did["fo"], 1)
                elif kind == "unit":
                    _, name, b = step
                    if name == "m":
                        hf = b
                        dve.wait_ge(max_done, HH * QT * (hf + 1))
                        if hf >= 1:
                            ready(dve, "m", hf - 1)
                        v.tensor_scalar(mhl[:, :, 0, :], mx[hf % 2][:], -1.0, None, ALU.mult).then_inc(m_hi, 1)
                        dve.wait_ge(m_hi, hf + 1)
                        v.scalar_tensor_tensor(mhl[:, :, 1, :], mx[hf % 2][:], -1.0, mhl[:, :, 0, :],
                                               ALU.mult, ALU.subtract).then_inc(m_split, 1)
                    if READS_LAST[name] != "D":
                        continue
                    bk = ready(dve, name, b)
                    view = tiles(bk[:])
                    if name[:2] == "kq":
                        c, piece = int(name[2]), int(name[3])
                        if b >= 1 and piece == 0:
                            dve.wait_ge(kq_lo, C * (b - 1) + c + 1)
                        if piece == 0:
                            last = v.tensor_scalar(kq[c][:, 0:512], bk[:], col("k_b", c), None, ALU.add)
                        else:
                            v.tensor_scalar(kq[c][:, 512:NK], bk[:, 0:256], col("k_b", c), None, ALU.add)
                            last = v.tensor_scalar(kq[c][:, NK:NK + TQ], bk[:, 256:512], col("q_b", c), 1.0 / DH,
                                                   ALU.add, ALU.mult)
                        last.then_inc(taken_by["D"], 1)
                    elif name == "vb":
                        out_b = ROW[:, ROWS["out_b"], :]
                        v.tensor_tensor(out_b, bk[:, 0:E], out_b, ALU.add).then_inc(taken_by["D"], 1)
                    elif name == "oq":
                        hf = b
                        b, part = divmod(hf, 2)
                        o_ps = bk[:, :].rearrange("p (t h d) -> p t h d", t=QT, h=HH)
                        v.reciprocal(rsum[:], o_ps[:, :, :, DH]).then_inc(rs_done, 1)
                        dve.wait_ge(rs_done, hf + 1)
                        if b >= 1 and part == 0:
                            taken(dve, "oT", b - 1)
                        at = part * HH * DH
                        v.tensor_tensor(osb[:, :, at:at + HH * DH].rearrange("p a (h d) -> p a h d", h=HH),
                                        o_ps[:, :, :, 0:DH], rsum[:, :, :, None].to_broadcast([P, QT, HH, DH]),
                                        ALU.mult).then_inc(taken_by["D"], 1)
                    elif name == "proj":
                        dve.wait_ge(did["xb"], b + 1)
                        v.tensor_tensor(xob[:], view, xob[:], ALU.add).then_inc(taken_by["D"], 1)
                    elif name[:2] == "up":
                        if b == 0 and name == "up0":
                            dve.wait_ge(kq_lo, C * B)
                        for i in range(2):
                            f = 2 * int(name[2]) + i
                            last = v.tensor_scalar(U[:, f, :], view[:, i, :], col("b1", f), None, ALU.add)
                        last.then_inc(taken_by["D"], 1)
                    elif name == "down":
                        v.tensor_tensor(xb2[:], view, xb2[:], ALU.add).then_inc(taken_by["D"], 1)
                    elif name[:4] == "mix_":
                        f = MIX[name[4]]
                        if b == 0 and name == "mix_v":
                            dve.wait_ge(kq_out, 2 * NB * 16 * B)
                        for c in range(C):
                            last = v.scalar_tensor_tensor(mixbuf(MIXBUF[name[4]])[:, c, :], view[:, c, :],
                                                          col("stack", f * C + c), SX[:, c, :], ALU.add, ALU.mult)
                        last.then_inc(taken_by["D"], 1)
                    elif name == "g":
                        dve.wait_ge(did["th"], b + 1)
                        v.scalar_tensor_tensor(G2[:], TH[:], 1.0, view, ALU.add, ALU.mult)\
                         .then_inc(taken_by["D"], 1)
                    elif name == "diag":
                        dve.wait_ge(v_out, 16 * (b + 1))
                        v.tensor_tensor(VT[:], view, VT[:], ALU.mult).then_inc(taken_by["D"], 1)
                    elif name == "ojT":
                        taken(dve, "dT", b)
                        v.tensor_tensor(SX[:, :, :].rearrange("p a (h j) -> p a h j", j=S),
                                        bk[:, :].rearrange("p (a j h) -> p a h j", a=QT, j=S),
                                        VN.rearrange("p a (h j) -> p a h j", j=S), ALU.add)\
                         .then_inc(taken_by["D"], 1)
                    elif name == "wo":
                        v.tensor_tensor(xob[:], view, xb2[:], ALU.add).then_inc(taken_by["D"], 1)
                    elif name == "fv":
                        taken(dve, "rr", b)
                        v.scalar_tensor_tensor(G2[:], TH[:], 1.0, view, ALU.add, ALU.mult).then_inc(taken_by["D"], 1)


def kernel(**inputs):
    import concourse.bacc as bacc
    from concourse.bass_utils import run_bass_kernel_spmd

    i = {n: np.asarray(a) for n, a in inputs.items()}
    L0 = {n[len("L0_xattn_"):]: a for n, a in i.items() if n.startswith("L0_xattn_")}
    L1 = {n[len("L1_xattn_"):]: a for n, a in i.items() if n.startswith("L1_xattn_")}
    x, ctxs = i["x"], i["ctx_2048"]

    def chunked(w):
        return w.reshape(w.shape[0] // P, P, -1).transpose(1, 0, 2).reshape(P, -1)

    def by_dim(w):
        return w.reshape(-1, NH // C, C, DH).transpose(0, 2, 3, 1).reshape(w.shape[0], E)

    kvw = L0["kv_w"].reshape(E, NH, DH, 2)
    kvb = L0["kv_b"].reshape(NH, DH, 2)
    k_w, v_w = kvw[..., 0].reshape(E, E), kvw[..., 1].reshape(E, E)
    per_partition = {
        "q_b": by_dim(L0["q_b"].reshape(1, E)).reshape(E, 1), "k_b": by_dim(kvb[..., 0].reshape(1, E)).reshape(E, 1),
        "post_w": L0["postnorm_w"].reshape(E, 1), "b1": L0["mlp_b1"].reshape(FF, 1),
        "ln1_w": L1["ln1_w"].reshape(E, 1), "ln1_b": L1["ln1_b"].reshape(E, 1),
        "ln2_w": L1["ln2_w"].reshape(E, 1), "ln2_b": L1["ln2_b"].reshape(E, 1),
        "maa_x": L1["maa_x"].reshape(E, 1), "stack": L1["maa_stack"].reshape(NF * E, 1),
        "decay": L1["time_decay"].reshape(E, 1), "u": L1["u"].reshape(E, 1),
        "ffn_k": L1["ffn_maa_k"].reshape(E, 1), "ffn_r": L1["ffn_maa_r"].reshape(E, 1),
        "shift0": ctxs[:, 0:2].transpose(0, 2, 1).reshape(B * E, 2),
        "v_b": kvb[..., 1].reshape(E, 1),
        "state0": ctxs[:, 2:2 + S].reshape(B * E, S),
    }
    arrays = {
        "hT": np.concatenate([ctxs.transpose(0, 2, 1), x.transpose(0, 2, 1)], axis=2),
        "x": x,
        "mask": i["mask_BxS2_ik0"].reshape(1, B, TC),
        "cols": np.concatenate([chunked(per_partition[n]) for n in COLS], axis=1),
        "rows": np.concatenate([L0["out_b"], L0["mlp_b2"], L1["gn_w"], L1["gn_b"]])[None],
        "ident_in": np.eye(P, dtype=np.float32),
        "bsum_in": np.kron(np.eye(H), np.ones((S, 1))).astype(np.float32).reshape(C, P, H).transpose(1, 0, 2),
        "bfull_in": np.kron(np.eye(P // S), np.ones((S, S))).astype(np.float32),
        "pick_in": np.kron(np.eye(2), np.kron(np.ones((2, 1)), np.diag([1] * VW + [0] * (32 - VW)))).astype(np.float32),
        "w_kq": np.stack([chunked(by_dim(k_w)), chunked(by_dim(L0["q_w"]))], axis=1).reshape(P, 2, C, E),
        "w_vo": np.stack([chunked(v_w), chunked(L0["out_w"])], axis=1).reshape(P, 2, C, E),
        "w_up": chunked(L0["mlp_w1"]).reshape(P, C, FF),
        "w_down": chunked(L0["mlp_w2"]).reshape(P, FC, E),
        "w_maa1": chunked(L1["maa_w1"]).reshape(P, C, NF * DM),
        "w_maa2": L1["maa_w2"].reshape(NF * DM, E),
        "w_td1": chunked(L1["td_w1"]).reshape(P, C, DD),
        "w_td2": L1["td_w2"],
        "w_sq": np.stack([chunked(L1[n].T) for n in SQUARE], axis=1).reshape(P, len(SQUARE), C, E),
    }
    nc = bacc.Bacc("TRN2", target_bir_lowering=False, num_devices=1)
    arrays = {n: np.ascontiguousarray(a) for n, a in arrays.items()}
    args = {n: nc.dram_tensor(n, a.shape, mybir.dt.from_np(a.dtype), kind="ExternalInput").ap()
            for n, a in arrays.items()}
    out = nc.dram_tensor("out", (B, TQ, E), F32, kind="ExternalOutput").ap()
    build(nc, out=out, **args)
    r = run_bass_kernel_spmd(nc, [arrays], core_ids=[0])
    return r.results[0]["out"]
```

```python
from contextlib import ExitStack

import numpy as np

import concourse.bass as bass
from concourse import mybir

P = 128
F32 = mybir.dt.float32
BF16 = mybir.dt.bfloat16
I32 = mybir.dt.int32
ALU = mybir.AluOpType
ACT = mybir.ActivationFunctionType
AX = mybir.AxisListType

B, TQ, TC, E = 4, 256, 512, 256
NK = TC + TQ
NH, DH = 16, 16
C = E // P
NT = NK // P
QT = TQ // P
FF = 4 * E
FC = FF // P
H, S = 32, E // 32
DM, DD = 32, 64
NF = 5
HH = NH // 2
NB = 6
K_BLOCKS = ((0, 0, 3, 1), (1, 3, 5, 1), (2, 5, 6, 1))
Q_BLOCKS = ((0, 0, 4, 3), (0, 5, 6, 1), (1, 1, 5, 3), (2, 2, 3, 1))
SPILLS = C * (len(K_BLOCKS) + len(Q_BLOCKS))
FILLS = 3
R_MASK, R_HI, R_LO = NB * DH, NB * DH + 1, NB * DH + 2
MASKED = -1.0e30
LEAD = 5
PAIRS = NH // 2
ST_BANKS = 3
UNITS_P = 6
VW = DH + 1

COLS = {}
_at = 0
for _n, _k in (("q_b", C), ("k_b", C), ("post_w", C), ("b1", FC), ("ln1_w", C), ("ln1_b", C), ("ln2_w", C),
               ("ln2_b", C), ("maa_x", C), ("stack", NF * C), ("decay", C), ("u", C), ("ffn_k", C), ("ffn_r", C),
               ("shift0", B * C * 2), ("state0", B * C * S), ("v_b", C)):
    COLS[_n] = (_at, _k)
    _at += _k
NCOLS = _at
ROWS = {n: i for i, n in enumerate(("out_b", "b2", "gn_w", "gn_b"))}
SQUARE = ("Wr", "Wk", "Wv", "Wg", "Wo", "Wfk", "Wfr", "Wfv")
MIX = {"k": 0, "w": 1, "v": 2, "r": 3, "g": 4}

TAIL = (("x", "-"), ("oT", "A"), ("proj", "D"), ("sq", "-"), ("rms", "-"), ("z", "-"), ("zT", "A"),
        ("up0", "D"), ("up1", "D"), ("up2", "D"), ("gelu0", "-"), ("up3", "D"), ("gelu1", "-"), ("down", "D"),
        ("stat1", "-"), ("root1", "-"), ("z2", "-"), ("xaT", "A"), ("sx", "-"), ("xin", "-"), ("maa1", "A"),
        ("mix_v", "D"), ("add_v", "-"), ("mix_w", "D"), ("v", "A"), ("add_w", "-"), ("mix_k", "D"), ("add_k", "-"),
        ("maag", "A"), ("td1", "A"), ("k", "A"), ("mix_r", "D"), ("add_r", "-"), ("td2", "A"), ("decay", "-"),
        ("mix_g", "D"), ("add_g", "-"), ("r", "A"), ("kv1", "-"), ("kv0", "-"), ("ruk", "-"), ("scan00", "-"),
        ("rs00", "-"), ("g", "D"), ("scan01", "-"), ("rs01", "-"), ("scan10", "-"), ("rs10", "-"), ("diag", "D"),
        ("scan11", "-"), ("rs11", "-"), ("gate", "-"), ("dT", "A"), ("wkv", "A"), ("ojT", "D"),
        ("center", "-"), ("gsq", "-"), ("gated", "-"), ("gvar", "-"), ("groot", "-"), ("gout", "-"),
        ("ogT", "A"), ("wo", "D"), ("stat2", "-"), ("root2", "-"), ("z3", "-"), ("xcT", "A"), ("sx2", "-"),
        ("xk", "-"), ("kk", "A"), ("xr", "-"), ("kk2", "-"), ("rr", "A"), ("fv", "D"), ("out", "-"))
TAIL_NAMES = {n for n, _ in TAIL}
KQ = ("kq00", "kq01", "kq10", "kq11")
VP = ("vp0", "vp1", "vp2")
READS_LAST = {n: who for n, who in TAIL if who != "-"}
READS_LAST.update({n: "D" for n in KQ + ("oq", "vb")}, **{n: "A" for n in VP + ("m",)})

GAPS_FIRST = (0, 0, 0, 0, 0, 0, 6, 1, 13, 0)
GAPS_KQ = (0, 1, 5, 7, 20, 10, 1, 11, 27, 3, 9, 0)
GAPS_VP = ((0, 3, 2), (15, 1, 21))
GAPS_TAIL = ((8, 6, 0, 0, 0, 0, 0, 6, 0, 2, 0, 0, 0, 0, 0, 0, 5, 6, 1, 0, 1, 1, 0, 3, 1, 2, 1, 4, 1, 3, 0, 4, 0, 0, 0,
              0, 0, 0, 0, 0, 0, 4, 0, 0, 0, 6, 0, 1, 0, 2, 1, 0, 0, 4, 0, 1, 6, 4, 0, 1, 0, 5, 0, 0, 0, 0, 1, 2, 0, 2,
              0, 1, 0, 0, 0),
             (23, 1, 0, 0, 2, 0, 3, 6, 0, 0, 1, 0, 0, 0, 0, 0, 4, 1, 2, 10, 2, 0, 0, 4, 2, 0, 3, 0, 0, 0, 0, 4, 0, 0,
              0, 0, 0, 0, 0, 0, 0, 0, 0, 0, 2, 0, 1, 2, 0, 6, 1, 0, 3, 0, 3, 0, 2, 3, 0, 1, 0, 4, 2, 0, 2, 1, 0, 0, 2,
              6, 0, 0, 0, 0, 6),
             (8, 0, 0, 0, 0, 0, 0, 2, 0, 2, 0, 0, 0, 1, 0, 0, 0, 2, 0, 1, 7, 0, 0, 0, 1, 0, 7, 0, 0, 0, 1, 0, 0, 0, 0,
              0, 0, 0, 4, 1, 0, 0, 0, 1, 0, 2, 0, 6, 0, 1, 1, 2, 1, 0, 2, 0, 3, 4, 0, 8, 0, 1, 2, 0, 2, 3, 1, 0, 1, 5,
              0, 0, 7, 3, 35))


def kq_steps(b):
    for n in KQ:
        yield ("unit", n, b)
        if n[3] == "1":
            yield ("split", int(n[2]), b)


def schedule():
    pairs = B * PAIRS

    def fill(tp, i):
        yield ("max", tp * 2 * FILLS + i)
        if tp % 4 == 3 and i == 2 * FILLS - 1:
            yield ("unit", "m", tp // 4)

    def merge(attention, others, gaps):
        at = 0
        for other, gap in zip(others, gaps):
            yield from attention[at:at + gap]
            at += gap
            yield other
        yield from attention[at:]

    def tail(b):
        return [("unit" if who != "-" else "post", n, b) for n, who in TAIL]

    yield from kq_steps(0)
    for hf in (0, 1):
        yield ("stack", hf)
    for n in VP:
        yield ("unit", n, 0)
    yield ("unit", "vb", 0)
    first = [x for tp in range(LEAD) for i in range(2 * FILLS) for x in fill(tp, i)]
    yield from merge(first, list(kq_steps(1)) + [("stack", 2)] + [("unit", n, 1) for n in VP], GAPS_FIRST)

    base = []
    for b in range(B):
        attention = []
        for tp in range(b * PAIRS, (b + 1) * PAIRS):
            ahead = [list(fill(tp + LEAD, i)) if tp + LEAD < pairs else [] for i in range(2 * FILLS)]
            if tp % 4 == 0 and 1 <= tp // 4 < 2 * B - 2:
                attention.append(("stack", tp // 4 + 2))
            for s in range(3):
                attention += ahead[2 * s] + [("exp", tp, s)] + ahead[2 * s + 1]
                if s or tp:
                    attention.append(("pv",) + ((tp, s - 1) if s else (tp - 1, 2)))
                if s == 0 and tp and tp % 4 == 0:
                    attention.append(("unit", "oq", tp // 4 - 1))
        if b == 0:
            yield from merge(attention, list(kq_steps(2)) + list(kq_steps(3)), GAPS_KQ)
        elif b + 1 < B:
            base += merge(attention, [("unit", n, b + 1) for n in VP], GAPS_VP[b - 1])
        else:
            base += attention + [("pv", pairs - 1, 2), ("unit", "oq", 2 * B - 1)] + tail(b)
    yield from merge(base, [x for b in range(B - 1) for x in tail(b)], sum(GAPS_TAIL, ()))


STEPS = list(schedule())
UNIT = {s[1:]: i for i, s in enumerate([s for s in STEPS if s[0] == "unit"])}
ORDER = sorted(UNIT, key=UNIT.get)


def last_read(i):
    who = READS_LAST[ORDER[i][0]]
    return who, sum(READS_LAST[n] == who for n, _ in ORDER[:i + 1])


def build(nc, hT, x, mask, cols, rows, ident_in, bsum_in, bfull_in, pick_in, w_kq, w_vo, w_up, w_down,
          w_maa1, w_maa2, w_td1, w_td2, w_sq, out):
    ctx = ExitStack()
    with ctx:
        def sb(name, shape, dt=F32):
            return ctx.enter_context(nc.sbuf_tensor(name, shape, dt))

        def sem(name):
            return ctx.enter_context(nc.semaphore(name))

        COL = sb("COL", [P, NCOLS])
        ROW = sb("ROW", [P, len(ROWS), E])
        ident = sb("ident", [P, P])
        identb = sb("identb", [P, P], BF16)
        bsum = sb("bsum", [P, C, H])
        bfull = sb("bfull", [P, P])
        pick = sb("pick", [P, 2 * 32])
        Wkq = sb("Wkq", [P, 2, C, E])
        Wvo = sb("Wvo", [P, 2, C, E])
        Wup = sb("Wup", [P, C, FF])
        Wdown = sb("Wdown", [P, FC, E])
        Wmaa1 = sb("Wmaa1", [P, C, NF * DM])
        Wmaa2 = sb("Wmaa2", [P, E])
        Wmaa2g = sb("Wmaa2g", [DM, E])
        Wtd1 = sb("Wtd1", [P, C, DD])
        Wtd2 = sb("Wtd2", [DD, E])
        Wsq = sb("Wsq", [P, len(SQUARE), C, E])
        half = sb("half", [P, QT])
        maskrow = sb("maskrow", [1, B, NK], BF16)

        hTs = [sb(f"hT{i}", [P, C, NK]) for i in range(2)]
        A = sb("A", [P, 3 * S * TQ])
        kq = [A[:, c * (NK + TQ):(c + 1) * (NK + TQ)] for c in range(C)]
        at = C * (NK + TQ)
        parts = A[:, at:at + 3 * (NK + TQ)].bitcast(BF16).rearrange("p (k c n) -> p k c n", k=3, c=C)
        KstAll = sb("Kst", [P, 3, HH, NK], BF16)
        Kst = [KstAll[:, i] for i in range(3)]
        masks = Kst[2][0:1].rearrange("p h n -> p (h n)").bitcast(I32)[:, 0:B * TC]\
            .rearrange("p (b n) -> p b n", b=B)
        Qst = [sb(f"Qst{i}", [P, HH, TQ], BF16) for i in range(3)]
        Vn = [sb(f"Vn{i}", [P, NT * NH * VW + 32 - VW]) for i in range(2)]
        probs = [sb(f"probs{i}", [P, 2, TQ]) for i in range(UNITS_P)]
        mx = [sb(f"mx{i}", [P, 2, QT, HH]) for i in range(2)]
        mhl = sb("mhl", [P, QT, 2, HH], BF16)
        mT = sb("mT", [2 * HH, TQ], BF16)
        oTs = sb("oTs", [P, 4, TQ])
        rsum = sb("rsum", [P, QT, HH])
        osb = [sb(f"osb{i}", [P, QT, E]) for i in range(2)]

        def rows_of(name):
            return sb(name, [P, QT, E])[:, :, :]

        def small(name, *shape):
            return [sb(f"{name}{i}", [P, *shape]) for i in range(2)]

        stat_, mv_, ss_, rstd_ = small("stat", QT, 6), small("mv", QT, 2), small("ss", QT), small("rstd", QT)
        gsum_, gvar_, gtmp_, grstd_ = (small(n, QT * H) for n in ("gsum", "gvar", "gtmp", "grstd"))

        class Tail:

            def __init__(self, i):
                if i == 0:
                    wide = A[:, :]
                    rows = [rows_of(n) for n in ("xob", "xb2", "Z", "T", "SX", "KT", "RT", "WD", "VT", "G2", "TH")]
                    xa = sb("XA", [P, C * (1 + TQ)])[:, :]
                else:
                    wide = KstAll[:, 0:2].rearrange("p i h n -> p (i h n)").bitcast(F32)
                    free = [hTs[k][:, :, :].rearrange("p c n -> p (c n)") for k in range(2)] +\
                           [Qst[k][:, :, :].rearrange("p h n -> p (h n)").bitcast(F32) for k in range(3)]
                    rows = [f[:, k * C * TQ:(k + 1) * C * TQ].rearrange("p (c t) -> p c t", c=C)
                            for f, count in zip(free, (3, 3, 2, 2, 2)) for k in range(count)]
                    xa = Kst[2].rearrange("p h n -> p (h n)").bitcast(F32)[:, 0:C * (1 + TQ)]
                self.xob = rows[0]
                self.xb2 = rows[1]
                self.Z = rows[2]
                self.T = rows[3]
                self.SX = rows[4]
                self.KT, self.RT, self.WD, self.VT, self.G2, self.TH = rows[5:11]
                self.XA = xa.rearrange("p (c t) -> p c t", c=C)
                self.VN = self.XA[:, :, 0:TQ]
                self.RUK = self.T
                region = [wide[:, k * S * TQ:(k + 1) * S * TQ].rearrange("p (j t) -> p j t", j=S) for k in range(3)]
                self.KV, self.PR = region[0:C], (region[2], region[0])
                self.U = region[0]
                mixes = wide[:, C * S * TQ:].rearrange("p (m c t) -> p m c t", m=4, c=C)
                self.mixed = {n: mixes[:, k] for k, n in enumerate("vkwr")}
                self.mixed["g"] = self.Z
                self.stat, self.mv, self.ss, self.rstd = stat_[i], mv_[i], ss_[i], rstd_[i]
                self.gsum, self.gvar, self.gtmp, self.grstd = gsum_[i], gvar_[i], gtmp_[i], grstd_[i]

        TAILS = [Tail(0), Tail(1)]

        pMX = [ctx.enter_context(nc.psum_tensor(f"pMX{i}", [P, 512], F32)) for i in range(2)]
        pST = [ctx.enter_context(nc.psum_tensor(f"pST{i}", [P, 2, TQ], F32)) for i in range(ST_BANKS)]
        pO = ctx.enter_context(nc.psum_tensor("pO", [P, 512], F32))
        pW = [ctx.enter_context(nc.psum_tensor(f"pW{i}", [P, 512], F32)) for i in range(2)]

        skd = nc.dram_tensor("k_stack", (B, NB, DH, NH, NK), BF16, kind="Internal").ap()
        sqd = nc.dram_tensor("q_stack", (B, NB, DH, NH, TQ), BF16, kind="Internal").ap()
        svd = nc.dram_tensor("v_rows", (B, E, TQ), F32, kind="Internal").ap()

        unit_ready = sem("unit_ready")
        taken_by = {"A": sem("taken_by_act"), "D": sem("taken_by_dve")}
        hT_in = [sem(f"hT_in{i}") for i in range(2)]
        w_in = {n: sem(f"in_{n}") for n in ("kq", "vo", "cols", "const", "mask", "mlp", "maa", "sq")}
        half_ok = sem("half_ok")
        identb_ok = sem("identb_ok")
        rows_set = sem("rows_set")
        v_ones = sem("v_ones")
        mask_ok = sem("mask_ok")
        kq_hi = sem("kq_hi")
        kq_rem = sem("kq_rem")
        kq_mid = sem("kq_mid")
        kq_lo = sem("kq_lo")
        kq_out = sem("kq_out")
        stack_in = [sem(f"stack_in{i}") for i in range(3)]
        max_ready, max_done = sem("max_ready"), sem("max_done")
        m_all = sem("m_all")
        m_hi = sem("m_hi")
        m_split = sem("m_split")
        m_in = [sem(f"m_in{i}") for i in range(2)]
        st_ready, exp_done = sem("st_ready"), sem("exp_done")
        pv_done = sem("pv_done")
        oT_taken = sem("oT_taken")
        rs_done = sem("rs_done")
        newton = sem("newton")
        x_in = sem("x_in")
        v_out, v_in = sem("v_out"), [sem(f"v_in{c}") for c in range(C)]
        out_done = sem("out_done")
        names = ("xob xb sq rr1 rs1 z gelu0 gelu1 st1 mv1 rr2 rs2 z2 c0 sx xin mix_v mix_k mix_w mix_r mix_g "
                 "wd ruk th wg bg kv0 kv1 sc00 sc01 sc10 sc11 p00 p01 p10 p11 gs gc gq gv ge gr gt gw gg "
                 "st2 mv2 rr3 rs3 z3 c1 sx2 xk xr kk fo").split()
        did = {n: sem(f"did_{n}") for n in names}

        def col(name, i=0, n=1, p=P):
            return COL[0:p, COLS[name][0] + i:COLS[name][0] + i + n]

        def row(name, n=QT):
            return ROW[:, ROWS[name], :][:, None, :].to_broadcast([P, n, E])

        def tail_of(step):
            return TAILS[step[0] in ("unit", "post") and step[1] in TAIL_NAMES and step[2] == B - 1]

        def tiles(ap):
            return ap.rearrange("p (a n) -> p a n", a=2)

        def taken(eng, name, b):
            who, n = last_read(UNIT[name, b])
            eng.wait_ge(taken_by[who], n)

        def ready(eng, name, b):
            eng.wait_ge(unit_ready, UNIT[name, b] + 1)
            return pW[UNIT[name, b] % 2]

        blk = ctx.enter_context(nc.Block())

        @blk.sync
        def _(sp):
            sp.dma_start(hTs[0][:], hT[0].rearrange("(c p) n -> p c n", p=P)).then_inc(hT_in[0], 16)
            sp.dma_start(Wkq[:], w_kq).then_inc(w_in["kq"], 16)
            sp.dma_start(masks, mask).then_inc(w_in["mask"], 16)
            sp.dma_start(Wvo[:], w_vo).then_inc(w_in["vo"], 16)
            for step in STEPS:
                kind = step[0]
                X = tail_of(step)
                if kind == "split":
                    _, c, b = step
                    for part, split in enumerate((kq_hi, kq_mid, kq_lo)):
                        sp.wait_ge(split, C * b + c + 1)
                        for blocks, dst, lo, hi in ((K_BLOCKS, skd, 0, NK), (Q_BLOCKS, sqd, NK, NK + TQ)):
                            for p_, first, end, by in blocks:
                                if p_ == part:
                                    n = len(range(first, end, by))
                                    sp.dma_start(dst[b, first:end:by, :, c::C].rearrange("k d h n -> (d h) k n"),
                                                 parts[:, part, c, lo:hi][:, None].to_broadcast([P, n, hi - lo]))\
                                      .then_inc(kq_out, 16)
                elif kind == "stack":
                    hf = step[1]
                    b, part = divmod(hf, 2)
                    s = hf % 3
                    sp.wait_ge(kq_out, SPILLS * 16 * (b + 1))
                    if hf >= 3:
                        sp.wait_ge(st_ready, 24 * (hf - 2))
                    else:
                        sp.wait_ge(rows_set, hf + 1)
                    sp.wait_ge(mask_ok, 1)
                    sp.dma_start(Kst[s][0:NB * DH], skd[b].rearrange("k d h n -> (k d) h n")[:, part * HH:(part + 1) * HH])\
                        .then_inc(stack_in[s], 16)
                    sp.dma_start(Qst[s][0:NB * DH], sqd[b].rearrange("k d h n -> (k d) h n")[:, part * HH:(part + 1) * HH])\
                        .then_inc(stack_in[s], 16)
                    sp.dma_start(Kst[s][R_MASK:R_MASK + 1],
                                 maskrow[0:1, b, :][:, None, :].to_broadcast([1, HH, NK])).then_inc(stack_in[s], 16)
                    if hf == 1:
                        sp.dma_start(Wup[:], w_up).then_inc(w_in["mlp"], 16)
                        sp.dma_start(Wdown[:], w_down).then_inc(w_in["mlp"], 16)
                        sp.dma_start(Wmaa1[:], w_maa1).then_inc(w_in["maa"], 16)
                        sp.dma_start(Wmaa2[:], w_maa2[0:P, :]).then_inc(w_in["maa"], 16)
                        sp.dma_start(Wmaa2g[:], w_maa2[P:P + DM, :]).then_inc(w_in["maa"], 16)
                        sp.dma_start(Wtd1[:], w_td1).then_inc(w_in["maa"], 16)
                        sp.dma_start(Wtd2[:], w_td2).then_inc(w_in["maa"], 16)
                        sp.dma_start(Wsq[:], w_sq).then_inc(w_in["sq"], 16)
                elif kind == "unit" and step[1] == "vp2" and step[2] + 2 < B:
                    b = step[2]
                    ready(sp, "vp2", b)
                    sp.dma_start(hTs[b % 2][:], hT[b + 2].rearrange("(c p) n -> p c n", p=P)).then_inc(hT_in[b % 2], 16)
                elif kind == "unit" and step[1] == "m":
                    hf = step[2]
                    s = hf % 3
                    taken(sp, "m", hf)
                    for part, r in ((0, R_HI), (1, R_LO)):
                        sp.dma_start(Qst[s][r:r + 1, :, :], mT[part * HH:(part + 1) * HH, :]).then_inc(m_in[hf % 2], 16)
                elif kind == "post" and step[1] == "x":
                    b = step[2]
                    if b == B - 1:
                        ready(sp, "vp2", b)
                    elif b >= 1:
                        sp.wait_ge(did["fo"], b)
                    sp.dma_start(X.xb2, x[b].rearrange("(a p) n -> p a n", p=P)).then_inc(x_in, 16)
                elif kind == "unit" and step[1] == "v":
                    b = step[2]
                    taken(sp, "v", b)
                    sp.dma_start(svd[b].rearrange("(c p) t -> p c t", p=P), X.VT).then_inc(v_out, 16)
                    sp.wait_ge(v_out, 16 * (b + 1))
                    if b == 0:
                        sp.wait_ge(kq_out, SPILLS * 16 * B)
                    taken(sp, "down", b)
                    for c in range(C):
                        src = svd[b].rearrange("(c h j) t -> c h (j t)", c=C, j=S)[c]
                        sp.dma_start(X.KV[c].rearrange("p j t -> p (j t)"),
                                     src[:, None, :].to_broadcast([P // S, S, S * TQ])).then_inc(v_in[c], 16)
                elif kind == "post" and step[1] == "out":
                    b = step[2]
                    sp.wait_ge(did["fo"], b + 1)
                    sp.dma_start(out[b].rearrange("(a p) n -> p a n", p=P), X.Z).then_inc(out_done, 16)
            sp.wait_ge(out_done, 16 * B)
            sp.wait_ge(kq_out, SPILLS * 16 * B)
            sp.wait_ge(v_out, 16 * B)

        @blk.tensor
        def _(pe):
            mm = nc.tensor.matmul

            def claim(name, b):
                i = UNIT[name, b]
                if i >= 2:
                    who, n = last_read(i - 2)
                    pe.wait_ge(taken_by[who], n)
                return pW[i % 2]

            def square(name, b, w, rhs_t, token_major):
                bk = claim(name, b)
                for m in range(2):
                    for c in range(C):
                        if token_major:
                            lhs, rhs = rhs_t[:, c, m * P:(m + 1) * P], w[:, c, :]
                        else:
                            lhs, rhs = w[:, c, m * P:(m + 1) * P], rhs_t[:, c, :]
                        last = mm(bk[:, m * 256:(m + 1) * 256], lhs, rhs, start=c == 0, stop=c == C - 1)
                last.then_inc(unit_ready, 1)

            def transposes(name, b, src):
                bk = claim(name, b)
                for c in range(C):
                    for a in range(QT):
                        last = nc.tensor.transpose(bk[:, c * TQ + a * P:c * TQ + (a + 1) * P],
                                                   src[:, a, c * P:(c + 1) * P], ident[:])
                last.then_inc(unit_ready, 1)

            pe.wait_ge(w_in["kq"], 16)
            for step in STEPS:
                kind = step[0]
                X = tail_of(step)
                if kind == "max":
                    n = step[1]
                    t, i = divmod(n, FILLS)
                    hf, h = divmod(t, HH)
                    s = hf % 3
                    if h == 0 and i == 0:
                        pe.wait_ge(stack_in[s], 48 * (hf // 3 + 1))
                    if n >= 2:
                        pe.wait_ge(max_done, n - 1)
                    jobs = ((i, 0, 512, 0),) if i < QT else ((0, 512, NK, 0), (1, 512, NK, NK - 512))
                    for qt, lo, hi, at in jobs:
                        last = mm(pMX[n % 2][:, at:at + hi - lo], Qst[s][0:R_MASK + 1, h, qt * P:(qt + 1) * P],
                                  Kst[s][0:R_MASK + 1, h, lo:hi], start=True, stop=True)
                    last.then_inc(max_ready, 1)
                elif kind == "exp":
                    _, tp, stage = step
                    hf = tp // 4
                    s = hf % 3
                    if tp % 4 == 0 and stage == 0:
                        pe.wait_ge(m_in[hf % 2], 32 * (hf // 2 + 1))
                    for hh in range(2):
                        n = 2 * (3 * tp + stage) + hh
                        h = (2 * tp + hh) % HH
                        if n >= ST_BANKS:
                            pe.wait_ge(exp_done, n - ST_BANKS + 1)
                        for i in range(2):
                            nt = 2 * stage + i
                            last = mm(pST[n % ST_BANKS][:, i, :], Kst[s][0:R_LO + 1, h, nt * P:(nt + 1) * P],
                                      Qst[s][0:R_LO + 1, h, :], start=True, stop=True)
                        last.then_inc(st_ready, 1)
                elif kind == "pv":
                    _, tp, stage = step
                    b, pair = divmod(tp, PAIRS)
                    if pair == 0 and stage == 0:
                        taken(pe, "vp2", b)
                        if b == 0:
                            pe.wait_ge(v_ones, 1)
                    if stage == 0 and tp:
                        pe.wait_ge(oT_taken, tp)
                    n = 2 * (3 * tp + stage)
                    pe.wait_ge(exp_done, n + 2)
                    for hh in range(2):
                        for i in range(2):
                            at = ((2 * stage + i) * NH + 2 * pair + hh) * VW
                            j = 2 * hh + i
                            last = mm(pO[32 * j:32 * j + 32, 0:TQ], Vn[b % 2][:, at:at + 32],
                                      probs[(n + hh) % UNITS_P][:, i, :], start=stage == 0, stop=stage == 2)
                    last.then_inc(pv_done, 1)
                elif kind == "unit":
                    _, name, b = step
                    if name[:2] == "kq":
                        c, piece = int(name[2]), int(name[3])
                        hb = hTs[b % 2]
                        if c == 0 and piece == 0:
                            pe.wait_ge(hT_in[b % 2], 16 * (b // 2 + 1))
                        bk = claim(name, b)
                        jobs = ((0, 0, 512, 0),) if piece == 0 else ((0, 512, NK, 0), (1, TC, NK, 256))
                        for w, lo, hi, at in jobs:
                            for kc in range(C):
                                last = mm(bk[:, at:at + hi - lo], Wkq[:, w, kc, c * P:(c + 1) * P], hb[:, kc, lo:hi],
                                          start=kc == 0, stop=kc == C - 1)
                        last.then_inc(unit_ready, 1)
                    elif name[:2] == "vp":
                        hb = hTs[b % 2]
                        if b == 0 and name == "vp0":
                            pe.wait_ge(w_in["vo"], 16)
                        bk = claim(name, b)
                        for i in range(2):
                            nt = 2 * int(name[2]) + i
                            for kc in range(C):
                                last = mm(bk[:, i * E:(i + 1) * E], hb[:, kc, nt * P:(nt + 1) * P], Wvo[:, 0, kc, :],
                                          start=kc == 0, stop=kc == C - 1)
                        last.then_inc(unit_ready, 1)
                    elif name == "m":
                        pe.wait_ge(m_split, b + 1)
                        if b == 0:
                            pe.wait_ge(identb_ok, 1)
                        bk = claim(name, b)[:, :].bitcast(BF16)
                        for qt in range(QT):
                            last = nc.tensor.transpose(bk[0:2 * HH, qt * P:(qt + 1) * P],
                                                       mhl[:, qt, :, :].rearrange("p l h -> p (l h)"), identb[:])
                        last.then_inc(unit_ready, 1)
                    elif name == "vb":
                        pe.wait_ge(w_in["vo"], 16)
                        pe.wait_ge(w_in["cols"], 16)
                        pe.wait_ge(w_in["const"], 80)
                        bk = claim(name, b)
                        for c in range(C):
                            last = mm(bk[:, 0:E], col("v_b", c).to_broadcast([P, P]), Wvo[:, 1, c, :],
                                      start=c == 0, stop=c == C - 1)
                        last.then_inc(unit_ready, 1)
                    elif name == "oq":
                        hf = b
                        pe.wait_ge(oT_taken, 4 * (hf + 1))
                        bk = claim(name, hf)
                        for qt in range(QT):
                            for p in range(4):
                                at = (qt * 4 + p) * 64
                                last = mm(bk[:, at:at + 64], oTs[:, p, qt * P:(qt + 1) * P], pick[:],
                                          start=True, stop=True)
                        last.then_inc(unit_ready, 1)
                    elif name == "oT":
                        taken(pe, "oq", 2 * b + 1)
                        transposes(name, b, osb[b % 2])
                    elif name == "proj":
                        taken(pe, "oT", b)
                        square(name, b, Wvo[:, 1], X.T, True)
                    elif name == "zT":
                        pe.wait_ge(did["z"], b + 1)
                        transposes(name, b, X.Z)
                    elif name[:2] == "up":
                        if name == "up0":
                            taken(pe, "zT", b)
                            if b == 0:
                                pe.wait_ge(w_in["mlp"], 32)
                        bk = claim(name, b)
                        for i in range(2):
                            f = 2 * int(name[2]) + i
                            for c in range(C):
                                last = mm(bk[:, i * TQ:(i + 1) * TQ], Wup[:, c, f * P:(f + 1) * P], X.T[:, c, :],
                                          start=c == 0, stop=c == C - 1)
                        last.then_inc(unit_ready, 1)
                    elif name == "down":
                        bk = claim(name, b)
                        for a in range(QT):
                            for f in range(FC):
                                if a == 0 and f in (0, FC // 2):
                                    pe.wait_ge(did["gelu0" if f == 0 else "gelu1"], b + 1)
                                last = mm(bk[:, a * E:(a + 1) * E], X.U[:, f, a * P:(a + 1) * P], Wdown[:, f, :],
                                          start=f == 0, stop=f == FC - 1)
                        last.then_inc(unit_ready, 1)
                    elif name == "xaT":
                        pe.wait_ge(did["z2"], b + 1)
                        transposes(name, b, X.Z)
                    elif name == "maa1":
                        pe.wait_ge(did["xin"], b + 1)
                        if b == 0:
                            pe.wait_ge(w_in["maa"], 80)
                        bk = claim(name, b)
                        for c in range(C):
                            last = mm(bk[:, 0:TQ], Wmaa1[:, c, 0:P], X.T[:, c, :], start=c == 0, stop=c == C - 1)
                        last.then_inc(unit_ready, 1)
                    elif name == "maag":
                        bk = claim(name, b)
                        for c in range(C):
                            last = mm(bk[0:DM, 0:TQ], Wmaa1[:, c, P:NF * DM], X.T[:, c, :], start=c == 0, stop=c == C - 1)
                        last.then_inc(unit_ready, 1)
                    elif name[:4] == "mix_":
                        f = MIX[name[4]]
                        taken(pe, "maag" if f == 4 else "maa1", b)
                        bk = claim(name, b)
                        for c in range(C):
                            if f < 4:
                                lhs, rhs = Wmaa2[f * DM:(f + 1) * DM, c * P:(c + 1) * P], X.xob[f * DM:(f + 1) * DM, 0, :]
                            else:
                                lhs, rhs = Wmaa2g[:, c * P:(c + 1) * P], X.xob[0:DM, 1, :]
                            last = mm(bk[:, c * TQ:(c + 1) * TQ], lhs, rhs, start=True, stop=True)
                        last.then_inc(unit_ready, 1)
                    elif name in ("v", "k", "r", "g"):
                        if b == 0 and name == "v":
                            pe.wait_ge(w_in["sq"], 16)
                        pe.wait_ge(did["mix_" + name], b + 1)
                        square(name, b, Wsq[:, SQUARE.index("W" + name)], X.mixed[name], name == "g")
                    elif name == "td1":
                        pe.wait_ge(did["mix_w"], b + 1)
                        bk = claim(name, b)
                        for c in range(C):
                            last = mm(bk[0:DD, 0:TQ], Wtd1[:, c, :], X.mixed["w"][:, c, :],
                                      start=c == 0, stop=c == C - 1)
                        last.then_inc(unit_ready, 1)
                    elif name == "td2":
                        taken(pe, "td1", b)
                        bk = claim(name, b)
                        for c in range(C):
                            last = mm(bk[:, c * TQ:(c + 1) * TQ], Wtd2[:, c * P:(c + 1) * P], X.TH[0:DD, 0, :],
                                      start=True, stop=True)
                        last.then_inc(unit_ready, 1)
                    elif name == "dT":
                        taken(pe, "diag", b)
                        bk = claim(name, b)
                        for a in range(QT):
                            for c in range(C):
                                last = nc.tensor.transpose(bk[:, a * E + c * P:a * E + (c + 1) * P],
                                                           X.VT[:, c, a * P:(a + 1) * P], ident[:])
                        last.then_inc(unit_ready, 1)
                    elif name == "diag":
                        pe.wait_ge(did["ruk"], b + 1)
                        bk = claim(name, b)
                        for c in range(C):
                            last = mm(bk[:, c * TQ:(c + 1) * TQ], bfull[:], X.RUK[:, c, :], start=True, stop=True)
                        last.then_inc(unit_ready, 1)
                    elif name == "wkv":
                        bk = claim(name, b)
                        for jj in range(S // 4):
                            for c in range(C):
                                pe.wait_ge(did[f"p{c}{jj}"], (b + 1) * (2 if jj == 0 else 1))
                            for c in range(C):
                                for j4 in range(4):
                                    last = mm(bk[32 * j4:32 * j4 + 32, jj * TQ:(jj + 1) * TQ], bsum[:, c, :],
                                              X.PR[c][:, 4 * jj + j4, :], start=c == 0, stop=c == C - 1)
                        last.then_inc(unit_ready, 1)
                    elif name == "ojT":
                        taken(pe, "wkv", b)
                        bk = claim(name, b)
                        for a in range(QT):
                            for jj in range(S // 4):
                                at = a * E + jj * P
                                last = nc.tensor.transpose(bk[:, at:at + P], X.T[:, jj, a * P:(a + 1) * P], ident[:])
                        last.then_inc(unit_ready, 1)
                    elif name == "ogT":
                        pe.wait_ge(did["gg"], b + 1)
                        transposes(name, b, X.SX)
                    elif name == "wo":
                        taken(pe, "ogT", b)
                        square(name, b, Wsq[:, SQUARE.index("Wo")], X.T, True)
                    elif name == "xcT":
                        pe.wait_ge(did["z3"], b + 1)
                        transposes(name, b, X.Z)
                    elif name == "rr":
                        pe.wait_ge(did["xr"], b + 1)
                        square(name, b, Wsq[:, SQUARE.index("Wfr")], X.RT, True)
                    elif name == "kk":
                        pe.wait_ge(did["xk"], b + 1)
                        square(name, b, Wsq[:, SQUARE.index("Wfk")], X.KT, False)
                    elif name == "fv":
                        pe.wait_ge(did["kk"], b + 1)
                        square(name, b, Wsq[:, SQUARE.index("Wfv")], X.VT, True)

        @blk.scalar
        def _(act):
            act_fn = nc.scalar.activation
            act.dma_start(COL[:], cols).then_inc(w_in["cols"], 16)
            for dst, src in ((ident, ident_in), (bsum, bsum_in), (bfull, bfull_in), (pick, pick_in)):
                act.dma_start(dst[:], src).then_inc(w_in["const"], 16)
            act.dma_start(ROW[:, :, :].rearrange("p r n -> p (r n)"), rows.to_broadcast([P, len(ROWS) * E]))\
                .then_inc(w_in["const"], 16)
            act.dma_start(hTs[1][:], hT[1].rearrange("(c p) n -> p c n", p=P)).then_inc(hT_in[1], 16)
            for step in STEPS:
                kind = step[0]
                X = tail_of(step)
                if kind == "exp":
                    _, tp, stage = step
                    if tp >= 1:
                        act.wait_ge(pv_done, 3 * (tp - 1) + stage + 1)
                    for hh in range(2):
                        n = 2 * (3 * tp + stage) + hh
                        act.wait_ge(st_ready, n + 1)
                        act_fn(probs[n % UNITS_P][:], pST[n % ST_BANKS][:], ACT.Exp).then_inc(exp_done, 1)
                    continue
                if kind == "pv" and step[2] == 2:
                    tp = step[1]
                    act.wait_ge(pv_done, 3 * tp + 3)
                    if tp >= 4 and tp % 4 == 0:
                        ready(act, "oq", tp // 4 - 1)
                    act_fn(oTs[:, tp % 4, :], pO[:, 0:TQ], ACT.Copy).then_inc(oT_taken, 1)
                    continue
                if kind == "split":
                    _, c, b = step
                    n = C * b + c
                    taken(act, f"kq{c}1", b)
                    if b >= 1:
                        act.wait_ge(kq_out, SPILLS * 16 * b)
                    act_fn(parts[:, 0, c, :], kq[c], ACT.Copy).then_inc(kq_hi, 1)
                    act.wait_ge(kq_rem, n + 1)
                    act_fn(parts[:, 1, c, :], kq[c], ACT.Copy).then_inc(kq_mid, 1)
                    continue
                if kind not in ("unit", "post"):
                    continue
                _, name, b = step
                if name == "vb":
                    act.wait_ge(w_in["cols"], 16)
                elif name == "sq":
                    taken(act, "proj", b)
                    if 1 <= b < B - 1:
                        act.wait_ge(out_done, 16 * b)
                    for a in range(QT):
                        last = act_fn(X.Z[:, a, :], X.xob[:, a, :], ACT.Square, accum_out=X.ss[:, a:a + 1])
                    last.then_inc(did["sq"], 1)
                elif name in ("gelu0", "gelu1"):
                    i = int(name[4])
                    taken(act, "up1" if i == 0 else "up3", b)
                    part = X.U[:, i * FC // 2:(i + 1) * FC // 2, :]
                    act_fn(part, part, ACT.Gelu_apprx_tanh).then_inc(did[name], 1)
                elif name == "gsq":
                    act.wait_ge(did["gc"], b + 1)
                    act_fn(X.T[:, :, :], X.SX[:, :, :], ACT.Square).then_inc(did["gq"], 1)
                elif name == "decay":
                    taken(act, "td2", b)
                    act_fn(X.WD, X.WD, ACT.Exp, scale=-1.0).then_inc(did["wd"], 1)
                elif name == "g":
                    bk = ready(act, name, b)
                    act_fn(X.TH, tiles(bk[:]), ACT.Tanh, scale=0.5).then_inc(did["th"], 1)
                elif READS_LAST.get(name) == "A":
                    bk = ready(act, name, b)
                    view = tiles(bk[:])
                    if name[:2] == "vp":
                        i = int(name[2])
                        if b == 0 and i == 0:
                            act.wait_ge(v_ones, 1)
                        if b >= 2 and i == 0:
                            act.wait_ge(pv_done, 3 * PAIRS * (b - 1))
                        at = 2 * i * NH * VW
                        vn = Vn[b % 2][:, at:at + 2 * NH * VW].rearrange("p (a h d) -> p a h d", a=2, h=NH)
                        last = act_fn(vn[:, :, :, 0:DH],
                                 bk[:, :].rearrange("p (a h d) -> p a h d", a=2, h=NH), ACT.Copy)
                    elif name == "m":
                        if b >= 1:
                            act.wait_ge(m_in[(b - 1) % 2], 32 * ((b - 1) // 2 + 1))
                        last = act_fn(mT[:], bk[:, :].bitcast(BF16)[0:2 * HH, 0:TQ], ACT.Copy)
                    elif name == "ogT":
                        last = act_fn(X.T, view, ACT.Copy, scale=0.5)
                    elif name == "zT":
                        for c in range(C):
                            last = act_fn(X.T[:, c, :], view[:, c, :], ACT.Copy, scale=col("post_w", c))
                    elif name in ("xaT", "xcT"):
                        ln = "ln1" if name == "xaT" else "ln2"
                        for c in range(C):
                            last = act_fn(X.XA[:, c, 1:1 + TQ], view[:, c, :], ACT.Identity,
                                     bias=col(ln + "_b", c), scale=col(ln + "_w", c))
                    elif name == "maa1":
                        last = act_fn(X.xob[:, 0, :], bk[:, 0:TQ], ACT.Tanh)
                    elif name == "maag":
                        last = act_fn(X.xob[0:DM, 1, :], bk[0:DM, 0:TQ], ACT.Tanh)
                    elif name == "td1":
                        last = act_fn(X.TH[0:DD, 0, :], bk[0:DD, 0:TQ], ACT.Tanh)
                    elif name == "td2":
                        for c in range(C):
                            last = act_fn(X.WD[:, c, :], view[:, c, :], ACT.Exp, bias=col("decay", c))
                    elif name == "rr":
                        last = act_fn(X.TH, view, ACT.Tanh, scale=0.5)
                    elif name == "kk":
                        last = act_fn(X.WD, view, ACT.Relu)
                    else:
                        if name == "dT":
                            act.wait_ge(did["mix_g"], b + 1)
                        dst = {"oT": X.T, "v": X.VT, "k": X.KT, "r": X.RT, "dT": X.VN, "wkv": X.T}[name]
                        last = act_fn(dst[:, :, :], view, ACT.Copy)
                    last.then_inc(taken_by["A"], 1)

        @blk.gpsimd
        def _(pool):
            g = nc.gpsimd
            ones2 = float(np.array([0x3F803F80], np.uint32).view(np.float32)[0])
            for s in range(3):
                g.memset(Kst[s][R_MASK:R_LO + 1].rearrange("p h n -> p (h n)").bitcast(F32), ones2)
                g.memset(Qst[s][R_MASK:R_LO + 1].rearrange("p h n -> p (h n)").bitcast(F32), ones2)\
                 .then_inc(rows_set, 1)
                pool.wait_ge(rows_set, s + 1)
            for i in range(2):
                g.memset(Vn[i][:, NT * NH * VW:], 0.0)
                last = g.memset(Vn[i][:, DH:NT * NH * VW:VW], 1.0)
            last.then_inc(v_ones, 1)
            g.memset(half[:], -0.5).then_inc(half_ok, 1)
            pool.wait_ge(half_ok, 1)

            def root(src, scale, eps, first, second, b):
                g.tensor_scalar(X.rstd[:], src, scale, eps, ALU.mult, ALU.add).then_inc(did[first], 1)
                pool.wait_ge(did[first], b + 1)
                g.tensor_tensor(X.rstd[:], X.rstd[:], half[:], ALU.pow).then_inc(did[second], 1)

            for step in STEPS:
                kind = step[0]
                X = tail_of(step)
                if kind == "split":
                    _, c, b = step
                    pool.wait_ge(kq_mid, C * b + c + 1)
                    g.tensor_tensor(parts[:, 2, c, :], kq[c], parts[:, 1, c, :], ALU.subtract).then_inc(kq_lo, 1)
                    continue
                if kind not in ("unit", "post"):
                    continue
                _, name, b = step
                if name == "x":
                    pool.wait_ge(w_in["cols"], 16)
                    if b == 0:
                        taken(pool, "vb", 0)
                    pool.wait_ge(x_in, 16 * (b + 1))
                    g.tensor_tensor(X.xob, X.xb2, row("out_b"), ALU.add).then_inc(did["xob"], 1)
                    pool.wait_ge(did["xob"], b + 1)
                    g.tensor_tensor(X.xb2, X.xb2, row("b2"), ALU.add).then_inc(did["xb"], 1)
                elif name == "rms":
                    pool.wait_ge(did["sq"], b + 1)
                    root(X.ss[:], 1.0 / E, 1e-6, "rr1", "rs1", b)
                elif name == "root1":
                    pool.wait_ge(did["mv1"], b + 1)
                    root(X.mv[:, :, 1], 1.0, 1e-5, "rr2", "rs2", b)
                elif name == "root2":
                    pool.wait_ge(did["mv2"], b + 1)
                    root(X.mv[:, :, 1], 1.0, 1e-5, "rr3", "rs3", b)
                elif name in ("xaT", "xcT"):
                    first = name == "xaT"
                    at = COLS["shift0"][0] + b * C * 2
                    prev = COL[:, at:at + 2 * C].rearrange("p (c k) -> p c k", c=C)[:, :, 1 if first else 0]
                    pool.wait_ge(did["z2" if first else "z3"], b + 1)
                    g.tensor_copy(X.XA[:, :, 0], prev).then_inc(did["c0" if first else "c1"], 1)
                elif name == "add_g":
                    taken(pool, "mix_" + name[4], b)
                    mb = X.mixed[name[4]]
                    g.tensor_tensor(mb, mb, X.XA[:, :, 1:1 + TQ], ALU.add).then_inc(did["mix_" + name[4]], 1)
                elif name == "kv1":
                    c = 1
                    pool.wait_ge(v_in[c], 16 * (b + 1))
                    taken(pool, "k", b)
                    g.tensor_tensor(X.KV[c], X.KV[c], X.KT[:, c, :][:, None, :].to_broadcast([P, S, TQ]), ALU.mult)\
                     .then_inc(did[name], 1)
                elif name == "gate":
                    taken(pool, "g", b)
                    g.tensor_tensor(X.TH, X.G2, row("gn_w"), ALU.mult).then_inc(did["wg"], 1)
                    pool.wait_ge(did["wg"], b + 1)
                    g.tensor_tensor(X.G2, X.G2, row("gn_b"), ALU.mult).then_inc(did["bg"], 1)
                elif name in ("rs00", "rs10"):
                    c = int(name[2])
                    pool.wait_ge(did[f"sc{c}0"], b + 1)
                    taken(pool, "r", b)
                    if c == 1:
                        pool.wait_ge(did["p00"], 2 * b + 2)
                        pool.wait_ge(did["p01"], b + 1)
                    at = COLS["state0"][0] + (b * C + c) * S
                    g.tensor_scalar(X.PR[c][:, 0:S // 2, 0], COL[:, at:at + S // 2], X.RT[:, c, 0:1], None, ALU.mult)\
                     .then_inc(did[f"p{c}0"], 1)
                    g.tensor_tensor(X.PR[c][:, 0:S // 2, 1:TQ], X.KV[c][:, 0:S // 2, 0:TQ - 1],
                                    X.RT[:, c, 1:TQ][:, None, :].to_broadcast([P, S // 2, TQ - 1]), ALU.mult)\
                     .then_inc(did[f"p{c}0"], 1)
                elif name == "gated":
                    pool.wait_ge(did["gq"], b + 1)
                    pool.wait_ge(did["wg"], b + 1)
                    g.tensor_tensor(X.SX, X.SX, X.TH, ALU.mult).then_inc(did["gt"], 1)

        @blk.vector
        def _(dve):
            v = nc.vector
            dve.wait_ge(w_in["mask"], 16)
            v.tensor_scalar(maskrow[:, :, 0:TC], masks, 0, MASKED, ALU.is_equal, ALU.mult)
            v.memset(maskrow[:, :, TC:NK], 0.0).then_inc(mask_ok, 1)
            dve.wait_ge(w_in["cols"], 16)

            def moments(x_, b, st, m):
                for a in range(QT):
                    last = v.bn_stats(X.stat[:, a, :], x_[:, a, :])
                last.then_inc(did[st], 1)
                dve.wait_ge(did[st], b + 1)
                for a in range(QT):
                    last = v.bn_aggr(X.mv[:, a, :], X.stat[:, a, :])
                last.then_inc(did[m], 1)

            def scan(c, first, b, done):
                at = COLS["state0"][0] + (b * C + c) * S
                for j in range(first, first + S // 2):
                    last = v.tensor_tensor_scan(X.KV[c][:, j, :], X.WD[:, c, :], X.KV[c][:, j, :],
                                                COL[:, at + j:at + j + 1], ALU.mult, ALU.add)
                last.then_inc(did[done], 1)

            def reciprocal_root(b):
                n = 10 * b
                v.tensor_scalar(X.gtmp[:].bitcast(I32), X.gvar[:].bitcast(I32), 1, None, ALU.logical_shift_right)\
                 .then_inc(newton, 1)
                dve.wait_ge(newton, n + 1)
                v.tensor_scalar(X.grstd[:].bitcast(I32), X.gtmp[:].bitcast(I32), -1.0, float(0x5F3759DF),
                                ALU.mult, ALU.add).then_inc(newton, 1)
                for i in range(3):
                    dve.wait_ge(newton, n + 3 * i + 2)
                    v.tensor_tensor(X.gtmp[:], X.grstd[:], X.grstd[:], ALU.mult).then_inc(newton, 1)
                    dve.wait_ge(newton, n + 3 * i + 3)
                    v.scalar_tensor_tensor(X.gtmp[:], X.gtmp[:], -0.5, X.gvar[:], ALU.mult, ALU.mult).then_inc(newton, 1)
                    dve.wait_ge(newton, n + 3 * i + 4)
                    last = v.scalar_tensor_tensor(X.grstd[:], X.gtmp[:], 1.5, X.grstd[:], ALU.add, ALU.mult)
                    if i < 2:
                        last.then_inc(newton, 1)
                return last

            for step in STEPS:
                kind = step[0]
                X = tail_of(step)
                if kind == "max":
                    n = step[1]
                    t, i = divmod(n, FILLS)
                    hf, h = divmod(t, HH)
                    dve.wait_ge(max_ready, n + 1)
                    if i < QT:
                        src, dst = pMX[n % 2][:, 0:512], mx[hf % 2][:, 0, i, h:h + 1]
                    else:
                        src, dst = tiles(pMX[n % 2][:]), mx[hf % 2][:, 1, :, h]
                    v.tensor_reduce(dst, src, AX.X, ALU.max).then_inc(max_done, 1)
                elif kind == "split":
                    _, c, b = step
                    n = C * b + c
                    dve.wait_ge(kq_hi, n + 1)
                    v.tensor_tensor(kq[c], kq[c], parts[:, 0, c, :], ALU.subtract).then_inc(kq_rem, 1)
                elif kind == "post":
                    _, name, b = step
                    if name == "z":
                        dve.wait_ge(did["rs1"], b + 1)
                        for a in range(QT):
                            last = v.tensor_scalar(X.Z[:, a, :], X.xob[:, a, :], X.rstd[:, a:a + 1], None, ALU.mult)
                        last.then_inc(did["z"], 1)
                    elif name in ("stat1", "stat2"):
                        first = name == "stat1"
                        taken(dve, "down" if first else "wo", b)
                        moments(X.xb2 if first else X.xob, b, "st1" if first else "st2", "mv1" if first else "mv2")
                    elif name in ("z2", "z3"):
                        src = X.xb2 if name == "z2" else X.xob
                        dve.wait_ge(did["rs2" if name == "z2" else "rs3"], b + 1)
                        for a in range(QT):
                            last = v.tensor_scalar(X.Z[:, a, :], src[:, a, :], X.mv[:, a, 0:1], X.rstd[:, a:a + 1],
                                                   ALU.subtract, ALU.mult)
                        last.then_inc(did[name], 1)
                    elif name in ("sx", "sx2"):
                        first = name == "sx"
                        taken(dve, "xaT" if first else "xcT", b)
                        dve.wait_ge(did["c0" if first else "c1"], b + 1)
                        v.tensor_tensor(X.SX, X.XA[:, :, 0:TQ], X.XA[:, :, 1:1 + TQ], ALU.subtract).then_inc(did[name], 1)
                    elif name in ("add_v", "add_k", "add_w", "add_r"):
                        taken(dve, "mix_" + name[4], b)
                        mb = X.mixed[name[4]]
                        v.tensor_tensor(mb, mb, X.XA[:, :, 1:1 + TQ], ALU.add).then_inc(did["mix_" + name[4]], 1)
                    elif name == "kv0":
                        dve.wait_ge(v_in[0], 16 * (b + 1))
                        taken(dve, "k", b)
                        v.tensor_tensor(X.KV[0], X.KV[0], X.KT[:, 0, :][:, None, :].to_broadcast([P, S, TQ]), ALU.mult)\
                         .then_inc(did[name], 1)
                    elif name == "ruk":
                        taken(dve, "r", b)
                        taken(dve, "k", b)
                        for c in range(C):
                            last = v.scalar_tensor_tensor(X.RUK[:, c, :], X.RT[:, c, :], col("u", c), X.KT[:, c, :],
                                                          ALU.mult, ALU.mult)
                        last.then_inc(did["ruk"], 1)
                    elif name == "kk2":
                        taken(dve, "kk", b)
                        v.tensor_tensor(X.VT, X.WD, X.WD, ALU.mult).then_inc(did["kk"], 1)
                    elif name == "xin":
                        dve.wait_ge(did["sx"], b + 1)
                        for c in range(C):
                            last = v.scalar_tensor_tensor(X.T[:, c, :], X.SX[:, c, :], col("maa_x", c), X.XA[:, c, 1:1 + TQ],
                                                          ALU.mult, ALU.add)
                        last.then_inc(did["xin"], 1)
                    elif name in ("xk", "xr"):
                        dst = X.KT if name == "xk" else X.RT
                        dve.wait_ge(did["sx2"], b + 1)
                        for c in range(C):
                            last = v.scalar_tensor_tensor(dst[:, c, :], X.SX[:, c, :], col("ffn_" + name[1], c),
                                                          X.XA[:, c, 1:1 + TQ], ALU.mult, ALU.add)
                        last.then_inc(did[name], 1)
                    elif name[:4] == "scan":
                        c, part = int(name[4]), int(name[5])
                        if part == 0:
                            dve.wait_ge(did["wd"], b + 1)
                            dve.wait_ge(did[f"kv{c}"], b + 1)
                        scan(c, part * S // 2, b, "sc" + name[4:])
                    elif name in ("rs01", "rs11"):
                        c = int(name[2])
                        dve.wait_ge(did[f"sc{c}1"], b + 1)
                        taken(dve, "r", b)
                        if c == 1:
                            dve.wait_ge(did["p00"], 2 * b + 2)
                            dve.wait_ge(did["p01"], b + 1)
                        at = COLS["state0"][0] + (b * C + c) * S + S // 2
                        v.tensor_scalar(X.PR[c][:, S // 2:, 0], COL[:, at:at + S // 2], X.RT[:, c, 0:1], None, ALU.mult)
                        v.tensor_tensor(X.PR[c][:, S // 2:, 1:TQ], X.KV[c][:, S // 2:, 0:TQ - 1],
                                        X.RT[:, c, 1:TQ][:, None, :].to_broadcast([P, S // 2, TQ - 1]), ALU.mult)\
                         .then_inc(did[f"p{c}1"], 1)
                    elif name == "center":
                        o3 = X.SX[:, :, :].rearrange("p a (h j) -> p (a h) j", j=S)
                        taken(dve, "ojT", b)
                        v.tensor_reduce(X.gsum[:], o3, AX.X, ALU.add).then_inc(did["gs"], 1)
                        dve.wait_ge(did["gs"], b + 1)
                        v.scalar_tensor_tensor(o3, X.gsum[:, :, None].to_broadcast([P, QT * H, S]), -1.0 / S, o3,
                                               ALU.mult, ALU.add).then_inc(did["gc"], 1)
                    elif name == "gvar":
                        dve.wait_ge(did["gq"], b + 1)
                        v.tensor_reduce(X.gvar[:], X.T[:, :, :].rearrange("p a (h j) -> p (a h) j", j=S), AX.X, ALU.add)\
                         .then_inc(did["gv"], 1)
                        dve.wait_ge(did["gv"], b + 1)
                        v.tensor_scalar(X.gvar[:], X.gvar[:], 1.0 / S, 1e-5, ALU.mult, ALU.add).then_inc(did["ge"], 1)
                    elif name == "groot":
                        dve.wait_ge(did["ge"], b + 1)
                        reciprocal_root(b).then_inc(did["gr"], 1)
                    elif name == "gout":
                        o3 = X.SX[:, :, :].rearrange("p a (h j) -> p (a h) j", j=S)
                        dve.wait_ge(did["gr"], b + 1)
                        dve.wait_ge(did["gt"], b + 1)
                        v.tensor_tensor(o3, o3, X.grstd[:, :, None].to_broadcast([P, QT * H, S]), ALU.mult)\
                         .then_inc(did["gw"], 1)
                        dve.wait_ge(did["gw"], b + 1)
                        dve.wait_ge(did["bg"], b + 1)
                        v.tensor_tensor(X.SX, X.SX, X.G2, ALU.add).then_inc(did["gg"], 1)
                    elif name == "out":
                        taken(dve, "fv", b)
                        v.scalar_tensor_tensor(X.Z, X.G2, 0.5, X.xob, ALU.mult, ALU.add).then_inc(did["fo"], 1)
                elif kind == "unit":
                    _, name, b = step
                    if name == "m":
                        hf = b
                        if hf == 0:
                            dve.wait_ge(w_in["const"], 80)
                            v.tensor_copy(identb[:], ident[:]).then_inc(identb_ok, 1)
                        dve.wait_ge(max_done, HH * FILLS * (hf + 1))
                        m = mx[hf % 2]
                        v.tensor_tensor(m[:, 0], m[:, 0], m[:, 1], ALU.max).then_inc(m_all, 1)
                        dve.wait_ge(m_all, hf + 1)
                        if hf >= 1:
                            ready(dve, "m", hf - 1)
                        v.tensor_scalar(mhl[:, :, 0, :], m[:, 0], -1.0, None, ALU.mult).then_inc(m_hi, 1)
                        dve.wait_ge(m_hi, hf + 1)
                        v.scalar_tensor_tensor(mhl[:, :, 1, :], m[:, 0], -1.0, mhl[:, :, 0, :],
                                               ALU.mult, ALU.subtract).then_inc(m_split, 1)
                    if READS_LAST[name] != "D":
                        continue
                    bk = ready(dve, name, b)
                    view = tiles(bk[:])
                    if name[:2] == "kq":
                        c, piece = int(name[2]), int(name[3])
                        if b >= 1 and piece == 0:
                            dve.wait_ge(kq_lo, C * (b - 1) + c + 1)
                        if piece == 0:
                            last = v.tensor_scalar(kq[c][:, 0:512], bk[:], col("k_b", c), None, ALU.add)
                        else:
                            v.tensor_scalar(kq[c][:, 512:NK], bk[:, 0:256], col("k_b", c), None, ALU.add)
                            last = v.tensor_scalar(kq[c][:, NK:NK + TQ], bk[:, 256:512], col("q_b", c), 1.0 / DH,
                                                   ALU.add, ALU.mult)
                        last.then_inc(taken_by["D"], 1)
                    elif name == "vb":
                        dve.wait_ge(w_in["const"], 80)
                        out_b = ROW[:, ROWS["out_b"], :]
                        v.tensor_tensor(out_b, bk[:, 0:E], out_b, ALU.add).then_inc(taken_by["D"], 1)
                    elif name == "oq":
                        hf = b
                        b, part = divmod(hf, 2)
                        o_ps = bk[:, :].rearrange("p (t h d) -> p t h d", t=QT, h=HH)
                        v.reciprocal(rsum[:], o_ps[:, :, :, DH]).then_inc(rs_done, 1)
                        dve.wait_ge(rs_done, hf + 1)
                        if b >= 2 and part == 0:
                            taken(dve, "oT", b - 2)
                        at = part * HH * DH
                        v.tensor_tensor(osb[b % 2][:, :, at:at + HH * DH].rearrange("p a (h d) -> p a h d", h=HH),
                                        o_ps[:, :, :, 0:DH], rsum[:, :, :, None].to_broadcast([P, QT, HH, DH]),
                                        ALU.mult).then_inc(taken_by["D"], 1)
                    elif name == "proj":
                        dve.wait_ge(did["xob"], b + 1)
                        v.tensor_tensor(X.xob, view, X.xob, ALU.add).then_inc(taken_by["D"], 1)
                    elif name[:2] == "up":
                        if b == 0 and name == "up0":
                            dve.wait_ge(kq_lo, C * B)
                        for i in range(2):
                            f = 2 * int(name[2]) + i
                            last = v.tensor_scalar(X.U[:, f, :], view[:, i, :], col("b1", f), None, ALU.add)
                        last.then_inc(taken_by["D"], 1)
                    elif name == "down":
                        dve.wait_ge(did["xb"], b + 1)
                        v.tensor_tensor(X.xb2, view, X.xb2, ALU.add).then_inc(taken_by["D"], 1)
                    elif name[:4] == "mix_":
                        f = MIX[name[4]]
                        if b == 0 and name == "mix_v":
                            dve.wait_ge(kq_out, SPILLS * 16 * B)
                        for c in range(C):
                            last = v.scalar_tensor_tensor(X.mixed[name[4]][:, c, :], view[:, c, :],
                                                          col("stack", f * C + c), X.SX[:, c, :], ALU.add, ALU.mult)
                        last.then_inc(taken_by["D"], 1)
                    elif name == "g":
                        dve.wait_ge(did["th"], b + 1)
                        v.scalar_tensor_tensor(X.G2, X.TH, 1.0, view, ALU.add, ALU.mult)\
                         .then_inc(taken_by["D"], 1)
                    elif name == "diag":
                        dve.wait_ge(v_out, 16 * (b + 1))
                        v.tensor_tensor(X.VT, view, X.VT, ALU.mult).then_inc(taken_by["D"], 1)
                    elif name == "ojT":
                        taken(dve, "dT", b)
                        v.tensor_tensor(X.SX[:, :, :].rearrange("p a (h j) -> p a h j", j=S),
                                        bk[:, :].rearrange("p (a j h) -> p a h j", a=QT, j=S),
                                        X.VN.rearrange("p a (h j) -> p a h j", j=S), ALU.add)\
                         .then_inc(taken_by["D"], 1)
                    elif name == "wo":
                        v.tensor_tensor(X.xob, view, X.xb2, ALU.add).then_inc(taken_by["D"], 1)
                    elif name == "fv":
                        taken(dve, "rr", b)
                        v.scalar_tensor_tensor(X.G2, X.TH, 1.0, view, ALU.add, ALU.mult).then_inc(taken_by["D"], 1)


def kernel(**inputs):
    import concourse.bacc as bacc
    from concourse.bass_utils import run_bass_kernel_spmd

    i = {n: np.asarray(a) for n, a in inputs.items()}
    L0 = {n[len("L0_xattn_"):]: a for n, a in i.items() if n.startswith("L0_xattn_")}
    L1 = {n[len("L1_xattn_"):]: a for n, a in i.items() if n.startswith("L1_xattn_")}
    x, ctxs = i["x"], i["ctx_2048"]

    def chunked(w):
        return w.reshape(w.shape[0] // P, P, -1).transpose(1, 0, 2).reshape(P, -1)

    def by_dim(w):
        return w.reshape(-1, NH // C, C, DH).transpose(0, 2, 3, 1).reshape(w.shape[0], E)

    kvw = L0["kv_w"].reshape(E, NH, DH, 2)
    kvb = L0["kv_b"].reshape(NH, DH, 2)
    k_w, v_w = kvw[..., 0].reshape(E, E), kvw[..., 1].reshape(E, E)
    per_partition = {
        "q_b": by_dim(L0["q_b"].reshape(1, E)).reshape(E, 1), "k_b": by_dim(kvb[..., 0].reshape(1, E)).reshape(E, 1),
        "post_w": L0["postnorm_w"].reshape(E, 1), "b1": L0["mlp_b1"].reshape(FF, 1),
        "ln1_w": L1["ln1_w"].reshape(E, 1), "ln1_b": L1["ln1_b"].reshape(E, 1),
        "ln2_w": L1["ln2_w"].reshape(E, 1), "ln2_b": L1["ln2_b"].reshape(E, 1),
        "maa_x": L1["maa_x"].reshape(E, 1), "stack": L1["maa_stack"].reshape(NF * E, 1),
        "decay": L1["time_decay"].reshape(E, 1), "u": L1["u"].reshape(E, 1),
        "ffn_k": L1["ffn_maa_k"].reshape(E, 1), "ffn_r": L1["ffn_maa_r"].reshape(E, 1),
        "shift0": ctxs[:, 0:2].transpose(0, 2, 1).reshape(B * E, 2),
        "v_b": kvb[..., 1].reshape(E, 1),
        "state0": ctxs[:, 2:2 + S].reshape(B * E, S),
    }
    arrays = {
        "hT": np.concatenate([ctxs.transpose(0, 2, 1), x.transpose(0, 2, 1)], axis=2),
        "x": x,
        "mask": i["mask_BxS2_ik0"].reshape(1, B, TC),
        "cols": np.concatenate([chunked(per_partition[n]) for n in COLS], axis=1),
        "rows": np.concatenate([L0["out_b"], L0["mlp_b2"], L1["gn_w"], L1["gn_b"]])[None],
        "ident_in": np.eye(P, dtype=np.float32),
        "bsum_in": np.kron(np.eye(H), np.ones((S, 1))).astype(np.float32).reshape(C, P, H).transpose(1, 0, 2),
        "bfull_in": np.kron(np.eye(P // S), np.ones((S, S))).astype(np.float32),
        "pick_in": np.kron(np.eye(2), np.kron(np.ones((2, 1)), np.diag([1] * VW + [0] * (32 - VW)))).astype(np.float32),
        "w_kq": np.stack([chunked(by_dim(k_w)), chunked(by_dim(L0["q_w"]))], axis=1).reshape(P, 2, C, E),
        "w_vo": np.stack([chunked(v_w), chunked(L0["out_w"])], axis=1).reshape(P, 2, C, E),
        "w_up": chunked(L0["mlp_w1"]).reshape(P, C, FF),
        "w_down": chunked(L0["mlp_w2"]).reshape(P, FC, E),
        "w_maa1": chunked(L1["maa_w1"]).reshape(P, C, NF * DM),
        "w_maa2": L1["maa_w2"].reshape(NF * DM, E),
        "w_td1": chunked(L1["td_w1"]).reshape(P, C, DD),
        "w_td2": L1["td_w2"],
        "w_sq": np.stack([chunked(L1[n].T) for n in SQUARE], axis=1).reshape(P, len(SQUARE), C, E),
    }
    nc = bacc.Bacc("TRN2", target_bir_lowering=False, num_devices=1)
    arrays = {n: np.ascontiguousarray(a) for n, a in arrays.items()}
    args = {n: nc.dram_tensor(n, a.shape, mybir.dt.from_np(a.dtype), kind="ExternalInput").ap()
            for n, a in arrays.items()}
    out = nc.dram_tensor("out", (B, TQ, E), F32, kind="ExternalOutput").ap()
    build(nc, out=out, **args)
    r = run_bass_kernel_spmd(nc, [arrays], core_ids=[0])
    return r.results[0]["out"]
```
